# Optimizing a Trainium2 kernel written in Bass

```python
import numpy as np
import jax
import jax.numpy as jnp

def _softmax(x, axis=-1):
    return jax.nn.softmax(x, axis=axis)

def _gelu(x):
    return jax.nn.gelu(x, approximate=True)

def _silu(x):
    return jax.nn.silu(x)

def _sigmoid(x):
    return jax.nn.sigmoid(x)

def _layernorm(x, axis=-1, eps=1e-05):
    m = jnp.mean(x, axis=axis, keepdims=True)
    v = jnp.var(x, axis=axis, keepdims=True)
    return (x - m) / jnp.sqrt(v + eps)

def _scatter_add(tgt, idx, src, axis=0):
    return tgt.at[idx].add(src)

def _segment_sum(src, seg, n):
    return jax.ops.segment_sum(src, seg, n)
kernel_name = 'mk_adj_ffn_d2_adj_r2_2ae07b'

def setup_inputs(seed: int=0):
    np.random.seed(seed)
    _w = jnp.asarray

    def _rec_inputs():
        import jax
        import jax.numpy as jnp
        _gk = jax.random.key(seed)
        x = -8.776e-05 + 1 * jax.random.normal(jax.random.fold_in(_gk, 1), (10000, 128), jnp.float32)
        _w = (1.0 + jnp.arange(10000, dtype=jnp.float32)) ** (-0.5)
        _w = _w / _w.mean()
        _pij = jnp.clip(0.0016 * _w[:, None] * _w[None, :], 0.0, 1.0)
        _a = jax.random.uniform(jax.random.fold_in(_gk, 2), (10000, 10000)) < _pij
        _a = jnp.logical_or(_a, jnp.eye(10000, dtype=bool))
        _af = _a.astype(jnp.float32)
        _af = _af * jax.random.uniform(jax.random.fold_in(_gk, 3), (10000, 10000), jnp.float32, 0.05, 1)
        adj = _af
        return (x, adj)
    x, adj = _rec_inputs()

    def _L0_gnn_setup():
        import jax, jax.numpy as jnp
        import numpy as np
        N_USER = 10000
        N_ITEM = 10000
        HID = 128
        key = jax.random.key(seed)
        k1, k2, k3, k4, k5, k6, k7 = jax.random.split(key, 7)
        scale = 1.0 / np.sqrt(HID)
        return {'user_feat': jax.random.normal(k1, (N_USER, HID), dtype=jnp.float32), 'item_feat': jax.random.normal(k2, (N_ITEM, HID), dtype=jnp.float32), 'adj': jax.random.uniform(k3, (N_USER, N_ITEM), dtype=jnp.float32), 'W_item': jax.random.uniform(k4, (HID, HID), dtype=jnp.float32, minval=-scale, maxval=scale), 'b_item': jax.random.uniform(k5, (HID,), dtype=jnp.float32, minval=-scale, maxval=scale), 'W_user': jax.random.uniform(k6, (HID, HID), dtype=jnp.float32, minval=-scale, maxval=scale), 'b_user': jax.random.uniform(k7, (HID,), dtype=jnp.float32, minval=-scale, maxval=scale)}
    _L0_gnn_all = _L0_gnn_setup()
    _L0_gnn_in = {k: v for k, v in _L0_gnn_all.items() if k in ('item_feat', 'W_item', 'b_item', 'W_user', 'b_user')}
    del _L0_gnn_all

    def _L0_ffn_setup():
        import jax, jax.numpy as jnp
        import numpy as np
        B, T, D, H, L = (16, 2048, 128, 128, 2)

        def _lstm(x, W_ih, W_hh, b_ih, b_hh):
            x_proj = jnp.einsum('btd,gd->btg', x, W_ih) + b_ih + b_hh
            h0 = jnp.zeros((x.shape[0], W_hh.shape[1]), x.dtype)
            c0 = jnp.zeros_like(h0)

            def step(carry, xp):
                h, c = carry
                gates = xp + h @ W_hh.T
                i, f, g, o = jnp.split(gates, 4, axis=-1)
                c = jax.nn.sigmoid(f) * c + jax.nn.sigmoid(i) * jnp.tanh(g)
                h = jax.nn.sigmoid(o) * jnp.tanh(c)
                return ((h, c), h)
            _, hs = jax.lax.scan(step, (h0, c0), jnp.swapaxes(x_proj, 0, 1))
            return jnp.swapaxes(hs, 0, 1)
        key = jax.random.key(seed)
        ks = jax.random.split(key, 9)
        s = 1.0 / np.sqrt(H)
        u = lambda k, shape: jax.random.uniform(k, shape, jnp.float32, -s, s)
        return {'x': jax.random.normal(ks[0], (B, T, D), jnp.float32), 'W_ih': u(ks[1], (4 * H, D)), 'W_hh': u(ks[2], (4 * H, H)), 'b_ih': u(ks[3], (4 * H,)), 'b_hh': u(ks[4], (4 * H,)), 'W_lin': u(ks[5], (L, H)), 'b_lin': u(ks[6], (L,)), 'fw_att': jnp.full((1, H), 0.001, jnp.float32), 'bw_att': jnp.full((1, H), 0.001, jnp.float32)}
    _L0_ffn_all = _L0_ffn_setup()
    _L0_ffn_in = {k: v for k, v in _L0_ffn_all.items() if k in ('W_ih', 'W_hh', 'b_ih', 'b_hh', 'W_lin', 'b_lin', 'fw_att', 'bw_att')}
    del _L0_ffn_all

    def _L1_gnn_setup():
        import jax, jax.numpy as jnp
        import numpy as np
        N = 4096
        F_IN = 128
        F_OUT = 128
        key = jax.random.key(seed)
        k1, k2, k3 = jax.random.split(key, 3)
        H = jax.random.normal(k1, (N, F_IN), dtype=jnp.float32)
        A_tilde = jax.random.uniform(k2, (N, N), dtype=jnp.float32)
        limit = np.sqrt(6.0 / (F_IN + F_OUT)).astype(np.float32)
        W = jax.random.uniform(k3, (F_IN, F_OUT), dtype=jnp.float32, minval=-limit, maxval=limit)
        return {'H': H, 'A_tilde': A_tilde, 'W': W}
    _L1_gnn_all = _L1_gnn_setup()
    _L1_gnn_in = {k: v for k, v in _L1_gnn_all.items() if k in ('W',)}
    del _L1_gnn_all

    def _L1_ffn_setup():
        import jax, jax.numpy as jnp
        import numpy as np
        H, P, G, NS, K = (8, 64, 64, 64, 3)
        D_INNER = H * P
        CONV_DIM = D_INNER + 2 * NS
        D_IN_PROJ = 2 * D_INNER + 2 * NS + 2 * H

        def _hydra(u, in_w, conv_w, conv_b, dt_bias, A_log, Dp, fcD_w, norm_w, out_w):
            Bt, L, _ = u.shape
            zxbcdt = u @ in_w.T
            z = zxbcdt[..., :D_INNER]
            xBC = zxbcdt[..., D_INNER:D_INNER + CONV_DIM]
            dt = zxbcdt[..., -2 * H:]
            dt = jnp.concatenate([dt[..., :H], jnp.flip(dt[..., H:], axis=1)], axis=0)
            dt = jax.nn.softplus(dt + dt_bias)
            xp = jnp.pad(xBC, ((0, 0), (K - 1, 0), (0, 0)))
            xBC = sum((xp[:, k:k + L, :] * conv_w[:, k] for k in range(K))) + conv_b
            xBC = jax.nn.silu(xBC)
            x = xBC[..., :D_INNER]
            Bm = xBC[..., D_INNER:D_INNER + NS]
            Cm = xBC[..., D_INNER + NS:]
            x_og = x
            x2 = jnp.concatenate([x, jnp.flip(x, 1)], 0).reshape(2 * Bt, L, H, P)
            B2 = jnp.concatenate([Bm, jnp.flip(Bm, 1)], 0)
            C2 = jnp.concatenate([Cm, jnp.flip(Cm, 1)], 0)
            dA = jnp.exp(dt * -jnp.exp(A_log))
            dBx = jnp.einsum('blh,bln,blhp->blhpn', dt, B2, x2)

            def step(h, inp):
                dA_t, dBx_t, C_t = inp
                h = h * dA_t[:, :, None, None] + dBx_t
                return (h, jnp.einsum('bhpn,bn->bhp', h, C_t))
            h0 = jnp.zeros((2 * Bt, H, P, NS), u.dtype)
            _, ys = jax.lax.scan(step, h0, (dA.transpose(1, 0, 2), dBx.transpose(1, 0, 2, 3, 4), C2.transpose(1, 0, 2)))
            y = ys.transpose(1, 0, 2, 3).reshape(2 * Bt, L, D_INNER)
            y_fw, y_bw = (y[:Bt], jnp.flip(y[Bt:], 1))
            y = jnp.pad(y_fw[:, :-1], ((0, 0), (1, 0), (0, 0))) + jnp.pad(y_bw[:, 1:], ((0, 0), (0, 1), (0, 0)))
            y = y + x_og * jnp.repeat(x_og @ fcD_w.T + Dp, P, axis=-1)
            yg = y * jax.nn.silu(z)
            yg = yg * jax.lax.rsqrt(jnp.mean(jnp.square(yg), -1, keepdims=True) + 1e-05) * norm_w
            return yg @ out_w.T
        key = jax.random.key(seed)
        ks = jax.random.split(key, 10)
        dim, Bsz, N = (128, 4, 4096)
        s = 0.02
        return {'x': jax.random.normal(ks[0], (Bsz, N, dim), jnp.float32), 'W_fx': jax.random.normal(ks[1], (D_INNER, dim), jnp.float32) * s, 'b_fx': jnp.zeros((D_INNER,), jnp.float32), 'W_x': jax.random.normal(ks[2], (D_INNER, dim), jnp.float32) * s, 'b_x': jnp.zeros((D_INNER,), jnp.float32), 'W_slice': jax.random.normal(ks[3], (G, P), jnp.float32) * s, 'b_slice': jnp.zeros((G,), jnp.float32), 'temperature': jnp.full((1, H, 1, 1), 0.5, jnp.float32), 'hy_in_w': jax.random.normal(ks[4], (D_IN_PROJ, D_INNER), jnp.float32) * s, 'hy_conv_w': jax.random.normal(ks[5], (CONV_DIM, K), jnp.float32) * s, 'hy_conv_b': jnp.zeros((CONV_DIM,), jnp.float32), 'hy_dt_bias': jnp.log(jnp.expm1(jnp.full((H,), 0.01, jnp.float32))), 'hy_A_log': jnp.log(jnp.linspace(1.0, 16.0, H)).astype(jnp.float32), 'hy_D': jnp.ones((H,), jnp.float32), 'hy_fcD_w': jax.random.normal(ks[6], (H, D_INNER), jnp.float32) * s, 'hy_norm_w': jnp.ones((D_INNER,), jnp.float32), 'hy_out_w': jax.random.normal(ks[7], (D_INNER, D_INNER), jnp.float32) * s, 'out_w': jax.random.normal(ks[8], (dim, D_INNER), jnp.float32) * s, 'out_b': jnp.zeros((dim,), jnp.float32)}
    _L1_ffn_all = _L1_ffn_setup()
    _L1_ffn_in = {k: v for k, v in _L1_ffn_all.items() if k in ('W_fx', 'b_fx', 'W_x', 'b_x', 'W_slice', 'b_slice', 'temperature', 'hy_in_w', 'hy_conv_w', 'hy_conv_b', 'hy_dt_bias', 'hy_A_log', 'hy_D', 'hy_fcD_w', 'hy_norm_w', 'hy_out_w', 'out_w', 'out_b')}
    del _L1_ffn_all
    return {'x': x, 'adj': adj, 'L0_gnn_item_feat': _L0_gnn_in['item_feat'], 'L0_gnn_W_item': _L0_gnn_in['W_item'], 'L0_gnn_b_item': _L0_gnn_in['b_item'], 'L0_gnn_W_user': _L0_gnn_in['W_user'], 'L0_gnn_b_user': _L0_gnn_in['b_user'], 'L0_ffn_W_ih': _L0_ffn_in['W_ih'], 'L0_ffn_W_hh': _L0_ffn_in['W_hh'], 'L0_ffn_b_ih': _L0_ffn_in['b_ih'], 'L0_ffn_b_hh': _L0_ffn_in['b_hh'], 'L0_ffn_W_lin': _L0_ffn_in['W_lin'], 'L0_ffn_b_lin': _L0_ffn_in['b_lin'], 'L0_ffn_fw_att': _L0_ffn_in['fw_att'], 'L0_ffn_bw_att': _L0_ffn_in['bw_att'], 'L1_gnn_W': _L1_gnn_in['W'], 'L1_ffn_W_fx': _L1_ffn_in['W_fx'], 'L1_ffn_b_fx': _L1_ffn_in['b_fx'], 'L1_ffn_W_x': _L1_ffn_in['W_x'], 'L1_ffn_b_x': _L1_ffn_in['b_x'], 'L1_ffn_W_slice': _L1_ffn_in['W_slice'], 'L1_ffn_b_slice': _L1_ffn_in['b_slice'], 'L1_ffn_temperature': _L1_ffn_in['temperature'], 'L1_ffn_hy_in_w': _L1_ffn_in['hy_in_w'], 'L1_ffn_hy_conv_w': _L1_ffn_in['hy_conv_w'], 'L1_ffn_hy_conv_b': _L1_ffn_in['hy_conv_b'], 'L1_ffn_hy_dt_bias': _L1_ffn_in['hy_dt_bias'], 'L1_ffn_hy_A_log': _L1_ffn_in['hy_A_log'], 'L1_ffn_hy_D': _L1_ffn_in['hy_D'], 'L1_ffn_hy_fcD_w': _L1_ffn_in['hy_fcD_w'], 'L1_ffn_hy_norm_w': _L1_ffn_in['hy_norm_w'], 'L1_ffn_hy_out_w': _L1_ffn_in['hy_out_w'], 'L1_ffn_out_w': _L1_ffn_in['out_w'], 'L1_ffn_out_b': _L1_ffn_in['out_b']}

def reference(x, adj, L0_gnn_item_feat, L0_gnn_W_item, L0_gnn_b_item, L0_gnn_W_user, L0_gnn_b_user, L0_ffn_W_ih, L0_ffn_W_hh, L0_ffn_b_ih, L0_ffn_b_hh, L0_ffn_W_lin, L0_ffn_b_lin, L0_ffn_fw_att, L0_ffn_bw_att, L1_gnn_W, L1_ffn_W_fx, L1_ffn_b_fx, L1_ffn_W_x, L1_ffn_b_x, L1_ffn_W_slice, L1_ffn_b_slice, L1_ffn_temperature, L1_ffn_hy_in_w, L1_ffn_hy_conv_w, L1_ffn_hy_conv_b, L1_ffn_hy_dt_bias, L1_ffn_hy_A_log, L1_ffn_hy_D, L1_ffn_hy_fcD_w, L1_ffn_hy_norm_w, L1_ffn_hy_out_w, L1_ffn_out_w, L1_ffn_out_b):
    import jax
    import jax.numpy as jnp

    def _L0_gnn_ref(user_feat, item_feat, adj, W_item, b_item, W_user, b_user):
        import jax, jax.numpy as jnp
        import numpy as np
        N_USER = 10000
        N_ITEM = 10000
        HID = 128
        h = item_feat @ W_item.T + b_item
        b = user_feat @ W_user.T + b_user
        return jax.nn.relu(adj @ h + b)

    def _L0_ffn_ref(x, W_ih, W_hh, b_ih, b_hh, W_lin, b_lin, fw_att, bw_att):
        import jax, jax.numpy as jnp
        import numpy as np
        B, T, D, H, L = (16, 2048, 128, 128, 2)

        def _lstm(x, W_ih, W_hh, b_ih, b_hh):
            x_proj = jnp.einsum('btd,gd->btg', x, W_ih) + b_ih + b_hh
            h0 = jnp.zeros((x.shape[0], W_hh.shape[1]), x.dtype)
            c0 = jnp.zeros_like(h0)

            def step(carry, xp):
                h, c = carry
                gates = xp + h @ W_hh.T
                i, f, g, o = jnp.split(gates, 4, axis=-1)
                c = jax.nn.sigmoid(f) * c + jax.nn.sigmoid(i) * jnp.tanh(g)
                h = jax.nn.sigmoid(o) * jnp.tanh(c)
                return ((h, c), h)
            _, hs = jax.lax.scan(step, (h0, c0), jnp.swapaxes(x_proj, 0, 1))
            return jnp.swapaxes(hs, 0, 1)
        lstm_out = _lstm(x, W_ih, W_hh, b_ih, b_hh)
        logits = jnp.einsum('bth,lh->btl', lstm_out, W_lin) + b_lin
        g = jax.lax.stop_gradient(jnp.argmax(logits, axis=-1).astype(lstm_out.dtype))[..., None]
        w = g * lstm_out
        inc = jnp.cumsum(w, axis=1)
        prefix = inc - w
        suffix = inc[:, -1:, :] - inc
        return 2.0 * lstm_out + prefix * fw_att + suffix * bw_att

    def _L1_gnn_ref(H, A_tilde, W):
        import jax, jax.numpy as jnp
        import numpy as np
        N = 4096
        F_IN = 128
        F_OUT = 128
        d_inv_sqrt = jnp.sum(A_tilde, axis=1) ** (-0.5)
        A_norm = d_inv_sqrt[:, None] * A_tilde * d_inv_sqrt[None, :]
        H_next = A_norm @ H @ W
        return jax.nn.relu(H_next)

    def _L1_ffn_ref(x, W_fx, b_fx, W_x, b_x, W_slice, b_slice, temperature, hy_in_w, hy_conv_w, hy_conv_b, hy_dt_bias, hy_A_log, hy_D, hy_fcD_w, hy_norm_w, hy_out_w, out_w, out_b):
        import jax, jax.numpy as jnp
        import numpy as np
        H, P, G, NS, K = (8, 64, 64, 64, 3)
        D_INNER = H * P
        CONV_DIM = D_INNER + 2 * NS
        D_IN_PROJ = 2 * D_INNER + 2 * NS + 2 * H

        def _hydra(u, in_w, conv_w, conv_b, dt_bias, A_log, Dp, fcD_w, norm_w, out_w):
            Bt, L, _ = u.shape
            zxbcdt = u @ in_w.T
            z = zxbcdt[..., :D_INNER]
            xBC = zxbcdt[..., D_INNER:D_INNER + CONV_DIM]
            dt = zxbcdt[..., -2 * H:]
            dt = jnp.concatenate([dt[..., :H], jnp.flip(dt[..., H:], axis=1)], axis=0)
            dt = jax.nn.softplus(dt + dt_bias)
            xp = jnp.pad(xBC, ((0, 0), (K - 1, 0), (0, 0)))
            xBC = sum((xp[:, k:k + L, :] * conv_w[:, k] for k in range(K))) + conv_b
            xBC = jax.nn.silu(xBC)
            x = xBC[..., :D_INNER]
            Bm = xBC[..., D_INNER:D_INNER + NS]
            Cm = xBC[..., D_INNER + NS:]
            x_og = x
            x2 = jnp.concatenate([x, jnp.flip(x, 1)], 0).reshape(2 * Bt, L, H, P)
            B2 = jnp.concatenate([Bm, jnp.flip(Bm, 1)], 0)
            C2 = jnp.concatenate([Cm, jnp.flip(Cm, 1)], 0)
            dA = jnp.exp(dt * -jnp.exp(A_log))
            dBx = jnp.einsum('blh,bln,blhp->blhpn', dt, B2, x2)

            def step(h, inp):
                dA_t, dBx_t, C_t = inp
                h = h * dA_t[:, :, None, None] + dBx_t
                return (h, jnp.einsum('bhpn,bn->bhp', h, C_t))
            h0 = jnp.zeros((2 * Bt, H, P, NS), u.dtype)
            _, ys = jax.lax.scan(step, h0, (dA.transpose(1, 0, 2), dBx.transpose(1, 0, 2, 3, 4), C2.transpose(1, 0, 2)))
            y = ys.transpose(1, 0, 2, 3).reshape(2 * Bt, L, D_INNER)
            y_fw, y_bw = (y[:Bt], jnp.flip(y[Bt:], 1))
            y = jnp.pad(y_fw[:, :-1], ((0, 0), (1, 0), (0, 0))) + jnp.pad(y_bw[:, 1:], ((0, 0), (0, 1), (0, 0)))
            y = y + x_og * jnp.repeat(x_og @ fcD_w.T + Dp, P, axis=-1)
            yg = y * jax.nn.silu(z)
            yg = yg * jax.lax.rsqrt(jnp.mean(jnp.square(yg), -1, keepdims=True) + 1e-05) * norm_w
            return yg @ out_w.T
        B, N, _ = x.shape
        fx = (x @ W_fx.T + b_fx).reshape(B, N, H, P).transpose(0, 2, 1, 3)
        xm = (x @ W_x.T + b_x).reshape(B, N, H, P).transpose(0, 2, 1, 3)
        temp = jnp.maximum(temperature, 1e-06)
        sw = jax.nn.softmax((xm @ W_slice.T + b_slice) / temp, axis=-1)
        snorm = sw.sum(2)
        st = jnp.einsum('bhnc,bhng->bhgc', fx, sw) / (snorm + 1e-05)[..., None]
        st = st.transpose(0, 2, 1, 3).reshape(B, G, D_INNER)
        ot = _hydra(st, hy_in_w, hy_conv_w, hy_conv_b, hy_dt_bias, hy_A_log, hy_D, hy_fcD_w, hy_norm_w, hy_out_w)
        ot = ot.reshape(B, G, H, P).transpose(0, 2, 1, 3)
        out = jnp.einsum('bhgc,bhng->bhnc', ot, sw).transpose(0, 2, 1, 3).reshape(B, N, D_INNER)
        return out @ out_w.T + out_b
    x = x + _L0_gnn_ref(_layernorm(x, axis=-1), L0_gnn_item_feat, adj, L0_gnn_W_item, L0_gnn_b_item, L0_gnn_W_user, L0_gnn_b_user)
    x = x + _L0_ffn_ref(_layernorm(x, axis=-1)[None], L0_ffn_W_ih, L0_ffn_W_hh, L0_ffn_b_ih, L0_ffn_b_hh, L0_ffn_W_lin, L0_ffn_b_lin, L0_ffn_fw_att, L0_ffn_bw_att)[0]
    x = x + _L1_gnn_ref(_layernorm(x, axis=-1), adj, L1_gnn_W)
    x = x + _L1_ffn_ref(_layernorm(x, axis=-1)[None], L1_ffn_W_fx, L1_ffn_b_fx, L1_ffn_W_x, L1_ffn_b_x, L1_ffn_W_slice, L1_ffn_b_slice, L1_ffn_temperature, L1_ffn_hy_in_w, L1_ffn_hy_conv_w, L1_ffn_hy_conv_b, L1_ffn_hy_dt_bias, L1_ffn_hy_A_log, L1_ffn_hy_D, L1_ffn_hy_fcD_w, L1_ffn_hy_norm_w, L1_ffn_hy_out_w, L1_ffn_out_w, L1_ffn_out_b)[0]
    return x

_drawn_inputs = setup_inputs


def setup_inputs(seed=0):
    import zlib

    import numpy as np

    out = dict(_drawn_inputs(seed))
    spreads = {'L0_ffn_fw_att': (0.0010000000474974513, 0.6),
     'L0_ffn_bw_att': (0.0010000000474974513, 0.6),
     'L1_ffn_b_fx': (0.0, 0.1),
     'L1_ffn_b_x': (0.0, 2.0),
     'L1_ffn_b_slice': (0.0, 2.0),
     'L1_ffn_temperature': (0.5, 0.6),
     'L1_ffn_hy_conv_b': (0.0, 0.1),
     'L1_ffn_hy_dt_bias': (-4.600166320800781, 0.6),
     'L1_ffn_hy_D': (1.0, 0.6),
     'L1_ffn_hy_norm_w': (1.0, 0.6),
     'L1_ffn_out_b': (0.0, 0.1)}
    factors = {'L1_ffn_W_x': 8.0,
     'L1_ffn_W_slice': 8.0,
     'L1_ffn_hy_conv_w': 25.478,
     'L1_ffn_hy_A_log': 64.0,
     'L1_ffn_hy_fcD_w': 46.173}
    for name, (base, spread) in spreads.items():
        noise = np.random.default_rng([zlib.crc32(name.encode()), seed]).standard_normal(out[name].shape)
        drawn = base * np.exp(spread * noise) if base else spread * noise
        out[name] = jnp.asarray(drawn.astype(out[name].dtype))
    for name, factor in factors.items():
        out[name] = (out[name] * factor).astype(out[name].dtype)
    return out
```

```python
from contextlib import ExitStack

import numpy as np

import concourse.bass as bass
from concourse import mybir

F32 = mybir.dt.float32
I32 = mybir.dt.int32
ALU = mybir.AluOpType
ACT = mybir.ActivationFunctionType
AXX = mybir.AxisListType.X

N, D = 10000, 128
T = 125
TILES = N // T
GROUP = 4
GROUPS = TILES // GROUP
GT = GROUP * T
GD = GROUP * D
EPS = 1e-5
DE = D + 1

SLOTS = 4
PB = 5
PCOLS = PB * T
BODY = SLOTS * PB
TURNS = TILES // BODY
STAGES = 4
AHEAD = 2


def chain(engine, sem, start=0):
    count = [start]

    def link(instruction):
        count[0] = count[0] + 1
        instruction.then_inc(sem, 1)
        engine.wait_ge(sem, count[0])
    return link


def inverse_root(nc, link, out, root, value, spare):
    link(nc.vector.reciprocal(out, root))
    link(nc.vector.tensor_tensor(spare, value, out, ALU.mult))
    link(nc.vector.tensor_tensor(spare, spare, out, ALU.mult))
    link(nc.vector.tensor_scalar(spare, spare, -0.5, 1.5, ALU.mult, ALU.add))
    link(nc.vector.tensor_tensor(out, out, spare, ALU.mult))


def setup(nc, m, W_item, b_item, W_user, b_user, W_ih, W_hh, b_ih, b_hh, gnn_w, x, item):
    with ExitStack() as c:
        sem = lambda n: c.enter_context(nc.semaphore(n))
        sb = lambda n, s: c.enter_context(nc.sbuf_tensor(n, s, F32))
        x_loaded, w_loaded, rows_loaded = sem("x_loaded"), sem("w_loaded"), sem("rows_loaded")
        item_loaded = [sem(f"item_loaded{k}") for k in range(2)]
        id_zero, id_done, ones_set = sem("id_zero"), sem("id_done"), sem("ones_set")
        w_turned, w_kept = sem("w_turned"), sem("w_kept")
        item_turned, item_staged, item_done, item_kept = (
            sem("item_turned"), sem("item_staged"), sem("item_done"), sem("item_kept"))
        wraw = sb("wraw", [128, 10, 128])
        item_in = [sb(f"item_in{k}", [T, GROUP, D]) for k in range(2)]
        item_t = [sb(f"item_t{k}", [D, GT]) for k in range(2)]
        brow = sb("brow", [1, GROUP, D])
        b2 = sb("b2", [128, 4])
        bank = m["bank"]
        x_view = x.rearrange("(t p) d -> p t d", p=T)
        item_view = item.rearrange("(t p) d -> p t d", p=T)
        row = lambda v: v.rearrange("(a d) -> a d", a=1)
        block = c.enter_context(nc.Block())

        @block.sync
        def _(sp):
            sp.dma_start(wraw[:, 0, :], W_item).then_inc(w_loaded, 16)
            sp.dma_start(wraw[:, 1, :], W_user).then_inc(w_loaded, 16)
            sp.dma_start(wraw[:, 2:6, :], W_ih.rearrange("(k p) d -> p k d", p=128)).then_inc(w_loaded, 16)
            sp.dma_start(wraw[:, 6:10, :], W_hh.rearrange("(k p) d -> p k d", p=128)).then_inc(w_loaded, 16)
            for q in range(GROUP):
                sp.dma_start(brow[0:1, q, :], row(b_item)).then_inc(rows_loaded, 16)
            sp.dma_start(m["gnn_w"][:], gnn_w).then_inc(rows_loaded, 16)
            sp.dma_start(m["gate_b"][:], b_ih.rearrange("(k p) -> p k", p=128), allow_slow_non_contiguous=True).then_inc(rows_loaded, 16)
            sp.dma_start(b2[:], b_hh.rearrange("(k p) -> p k", p=128), allow_slow_non_contiguous=True).then_inc(rows_loaded, 16)
            sp.wait_ge(ones_set, 2)
            for q in range(2):
                sp.dma_start(m["open_row"][0:1, q, 0:D], row(b_user)).then_inc(rows_loaded, 16)
            for k in range(2):
                sp.dma_start(item_in[k][:], item_view[:, k * GROUP:(k + 1) * GROUP, :]).then_inc(item_loaded[k], 16)
            for k in range(4):
                sp.dma_start(m["stream"][:, k * 20:(k + 1) * 20, :],
                             x_view[:, k * 20:(k + 1) * 20, :]).then_inc(x_loaded, 16)
            with sp.Fori(0, GROUPS // 2 - 1) as i:
                for k in range(2):
                    sp.wait_ge(item_turned, i * 2 + (k + 1))
                    sp.dma_start(item_in[k][:], item_view[:, bass.ds((i * 2 + 2 + k) * GROUP, GROUP), :]
                                 ).then_inc(item_loaded[k], 16)
            sp.wait_ge(x_loaded, 64)
            sp.wait_ge(rows_loaded, 16 * 9)

        @block.gpsimd
        def _(pool):
            nc.gpsimd.memset(m["ident"][:], 0.0).then_inc(id_zero, 1)
            pool.wait_ge(id_zero, 1)
            nc.gpsimd.affine_select(out=m["ident"][:], in_=m["ident"][:], compare_op=ALU.not_equal, fill=1.0,
                                    base=0, pattern=[[-1, 128]], channel_multiplier=1).then_inc(id_done, 1)

        @block.tensor
        def _(pe):
            pe.wait_ge(id_done, 1)
            pe.wait_ge(w_loaded, 64)
            for k in range(10):
                nc.tensor.transpose(bank[k // 4][:, (k % 4) * 128:(k % 4 + 1) * 128], wraw[:, k, :],
                                    m["ident"][:]).then_inc(w_turned, 1)
            pe.wait_ge(w_kept, 3)
            pe.wait_ge(rows_loaded, 16 * 9)
            pe.wait_ge(ones_set, 2)
            with pe.Fori(0, GROUPS // 2) as i:
                for k in range(2):
                    pe.wait_ge(item_loaded[k], (i + 1) * 16)
                    for q in range(GROUP):
                        t = nc.tensor.transpose(bank[k][:, q * T:(q + 1) * T], item_in[k][:, q, :],
                                                m["ident"][0:T, 0:T])
                    t.then_inc(item_turned, 1)
                    pe.wait_ge(item_staged, i * 2 + (k + 1))
                    pe.wait_ge(item_kept, i * 2 + (k + 1))
                    nc.tensor.matmul(bank[2 + k][0:T, 0:GD], m["ones_row"][0:1, 0:T],
                                     brow[0:1].rearrange("a q d -> a (q d)"),
                                     start=True, stop=False, skip_group_check=True)
                    for q in range(GROUP):
                        t = nc.tensor.matmul(bank[2 + k][0:T, q * D:(q + 1) * D], item_t[k][:, q * T:(q + 1) * T],
                                             m["w_item"][:], start=False, stop=(q == GROUP - 1),
                                             skip_group_check=True)
                    t.then_inc(item_done, 1)

        @block.scalar
        def _(act):
            with act.Fori(0, GROUPS // 2) as i:
                for k in range(2):
                    act.wait_ge(item_turned, i * 2 + (k + 1))
                    nc.scalar.activation(item_t[k][:], bank[k][:, 0:GT], ACT.Copy).then_inc(item_staged, 1)

        @block.vector
        def _(dve):
            nc.vector.memset(m["ones_row"][:], 1.0).then_inc(ones_set, 1)
            nc.vector.memset(m["open_row"][:], 0.0).then_inc(ones_set, 1)
            nc.vector.memset(m["zero_row"][:], 0.0)
            nc.vector.memset(m["wide1"][0:T, 0:TILES * DE].rearrange("p (t d) -> p t d", d=DE)[:, :, D:DE], 1.0)
            dve.wait_ge(w_turned, 10)
            nc.vector.tensor_copy(m["w_item"][:], bank[0][:, 0:128]).then_inc(w_kept, 1)
            nc.vector.tensor_copy(m["w_user"][:], bank[0][:, 128:256])
            nc.vector.tensor_copy(m["w_ih"][:, 0:256], bank[0][:, 256:512])
            nc.vector.tensor_copy(m["w_ih"][:, 256:512], bank[1][:, 0:256])
            nc.vector.tensor_copy(m["w_hh"][:, 0:256], bank[1][:, 256:512]).then_inc(w_kept, 1)
            nc.vector.memset(m["note"][0:1, 0:1], 0.0).then_inc(item_kept, 1)
            nc.vector.tensor_copy(m["w_hh"][:, 256:512], bank[2][:, 0:256]).then_inc(w_kept, 1)
            nc.vector.memset(m["note"][0:1, 1:2], 0.0).then_inc(item_kept, 1)
            dve.wait_ge(rows_loaded, 16 * 9)
            nc.vector.tensor_tensor(m["gate_b"][:], m["gate_b"][:], b2[:], ALU.add)
            items = m["wide1"][0:T, 0:TILES * DE].rearrange("p (t d) -> p t d", d=DE)
            with dve.Fori(0, GROUPS // 2) as i:
                for k in range(2):
                    dve.wait_ge(item_done, i * 2 + (k + 1))
                    nc.vector.tensor_copy(items[:, bass.ds((i * 2 + k) * GROUP, GROUP), 0:D],
                                          bank[2 + k][0:T, 0:GD].rearrange("p (q d) -> p q d", d=D)
                                          ).then_inc(item_kept, 1)


def norm_stats(nc, m, tag):
    with ExitStack() as c:
        sem = lambda n: c.enter_context(nc.semaphore(n + tag))
        sb = lambda n, s: c.enter_context(nc.sbuf_tensor(n + tag, s, F32))
        stats_done, var_done, root_done, step = sem("stats_done"), sem("var_done"), sem("root_done"), sem("nstep")
        parts = sb("parts", [T, TILES, 6])
        var, root, corr = sb("var", [T, TILES]), sb("root", [T, TILES]), sb("corr", [T, TILES])
        block = c.enter_context(nc.Block())

        @block.vector
        def _(dve):
            with dve.Fori(0, GROUPS) as g:
                for q in range(GROUP):
                    nc.vector.bn_stats(parts[:, bass.ds(g * GROUP + q, 1), :], m["stream"][:, bass.ds(g * GROUP + q, 1), :]
                                       ).then_inc(stats_done, 1)
            dve.wait_ge(stats_done, TILES)
            link = chain(dve, step)
            link(nc.vector.tensor_tensor(corr[:], parts[:, :, 1], parts[:, :, 4], ALU.subtract))
            link(nc.vector.tensor_tensor(root[:], corr[:], corr[:], ALU.mult))
            link(nc.vector.tensor_tensor(m["mean"][:], parts[:, :, 1], parts[:, :, 4], ALU.add))
            link(nc.vector.tensor_scalar(m["mean"][:], m["mean"][:], 0.5, None, ALU.mult))
            link(nc.vector.tensor_tensor(var[:], parts[:, :, 2], parts[:, :, 5], ALU.add))
            link(nc.vector.tensor_scalar(var[:], var[:], 1.0 / D, EPS, ALU.mult, ALU.add))
            nc.vector.scalar_tensor_tensor(var[:], root[:], 0.25, var[:], ALU.mult, ALU.add).then_inc(var_done, 1)
            dve.wait_ge(root_done, 1)
            inverse_root(nc, link, m["rstd"][:], root[:], var[:], corr[:])

        @block.scalar
        def _(act):
            act.wait_ge(var_done, 1)
            nc.scalar.activation(root[:], var[:], ACT.Sqrt).then_inc(root_done, 1)


def norm_transposed(nc, m, tag):
    with ExitStack() as c:
        sem = lambda n: c.enter_context(nc.semaphore(n + tag))
        rows_ready, turned, kept = sem("rows_ready"), sem("turned"), sem("kept")
        rows = [c.enter_context(nc.sbuf_tensor(f"rows{k}{tag}", [T, GROUP, D], F32)) for k in range(2)]
        bank = m["bank"]
        block = c.enter_context(nc.Block())

        def normalise(dve, g, k):
            for q in range(GROUP):
                i = nc.vector.tensor_scalar(rows[k][:, q, :], m["stream"][:, bass.ds(g * GROUP + q, 1), :],
                                            m["mean"][:, bass.ds(g * GROUP + q, 1)],
                                            m["rstd"][:, bass.ds(g * GROUP + q, 1)], ALU.subtract, ALU.mult)
            i.then_inc(rows_ready, 1)

        @block.vector
        def _(dve):
            for k in range(2):
                normalise(dve, k, k)
            with dve.Fori(1, GROUPS // 2) as i:
                for k in range(2):
                    dve.wait_ge(turned, i * 2 + (k - 1))
                    normalise(dve, i * 2 + k, k)

        @block.tensor
        def _(pe):
            def turn(n, k):
                pe.wait_ge(rows_ready, n + 1)
                for q in range(GROUP):
                    t = nc.tensor.transpose(bank[k][:, q * T:(q + 1) * T], rows[k][:, q, :], m["ident"][0:T, 0:T])
                t.then_inc(turned, 1)
            for k in range(2):
                turn(k, k)
            with pe.Fori(1, GROUPS // 2) as i:
                for k in range(2):
                    pe.wait_ge(kept, i * 2 + (k - 1))
                    turn(i * 2 + k, k)

        @block.scalar
        def _(act):
            with act.Fori(0, GROUPS // 2) as i:
                for k in range(2):
                    act.wait_ge(turned, i * 2 + (k + 1))
                    nc.scalar.activation(m["wide2"][:, bass.ds((i * 2 + k) * GT, GT)], bank[k][:, 0:GT],
                                         ACT.Copy).then_inc(kept, 1)


def adjacency_pass(nc, m, adj, first):
    tag = "_a" if first else "_b"
    cols = DE if first else D
    with ExitStack() as c:
        sem = lambda n: c.enter_context(nc.semaphore(n + tag))
        sb = lambda n, s: c.enter_context(nc.sbuf_tensor(n + tag, s, F32))
        panel_loaded = [sem(f"panel_loaded{k}") for k in range(SLOTS)]
        panel_read, turned, sums_done, sums_read, user_staged, user_read = (
            sem("panel_read"), sem("turned"), sem("sums_done"), sem("sums_read"), sem("user_staged"), sem("user_read"))
        staged = [sem("staged_dve"), sem("staged_act")]
        relu_done, added = sem("relu_done"), sem("added")
        panel = [sb(f"panel{k}", [T, GROUP, PCOLS]) for k in range(SLOTS)]
        stage = [sb(f"stage{k}", [T, GT]) for k in range(STAGES)]
        user = sb("user", [D, GT])
        fresh = sb("fresh", [T, GROUP, D])
        bank = m["bank"]
        sums = [bank[4], bank[5]]
        rows = adj.rearrange("(t p) c -> p t c", p=T)
        feats = m["wide1"][0:T, 0:TILES * DE].rearrange("p (t d) -> p t d", d=DE)
        block = c.enter_context(nc.Block())

        @block.sync
        def _(sp):
            def load(g, turn, s):
                sp.dma_start(panel[s][:], rows[:, bass.ds(g * GROUP, GROUP), bass.ds(turn * (SLOTS * PCOLS) + s * PCOLS, PCOLS)]
                             ).then_inc(panel_loaded[s], 16)
            def slot_free(n, s):
                sp.wait_ge(panel_read, n + (s + 1))

            def rest_of(g):
                with sp.Fori(1, TURNS) as turn:
                    for s in range(SLOTS):
                        slot_free(g * (TURNS * SLOTS) + (turn - 1) * SLOTS, s)
                        load(g, turn, s)

            for s in range(SLOTS):
                load(0, 0, s)
            with sp.Fori(0, GROUPS - 1) as g:
                rest_of(g)
                for s in range(SLOTS):
                    slot_free(g * (TURNS * SLOTS) + (TURNS - 1) * SLOTS, s)
                    load(g + 1, 0, s)
            rest_of(GROUPS - 1)
            slot_free((GROUPS * TURNS - 1) * SLOTS, 0)
            load(0, 0, 0)
            for s in range(SLOTS):
                sp.wait_ge(panel_loaded[s], 16 * (GROUPS * TURNS + (s == 0)))

        @block.tensor
        def _(pe):
            def transposes(b):
                s = b % BODY // PB
                for q in range(GROUP):
                    t = nc.tensor.transpose(bank[b % STAGES][0:T, q * T:(q + 1) * T],
                                            panel[s][:, q, b % PB * T:(b % PB + 1) * T], m["ident"][0:T, 0:T])
                t.then_inc(turned, 1)
                return t

            def panel_ready(s, turns):
                pe.wait_ge(panel_loaded[s], turns * 16)

            panel_ready(0, 1)
            for b in range(AHEAD):
                transposes(b)
            with pe.Fori(0, GROUPS) as g:
                if first:
                    pe.wait_ge(user_staged, g + 1)
                pe.wait_ge(sums_read, g + 1)
                for h in range(2):
                    nc.tensor.matmul(sums[h][0:T, 0:2 * DE], m["ones_row"][0:1, 0:T],
                                     m["open_row" if first else "zero_row"][0:1].rearrange("a q d -> a (q d)"),
                                     start=True, stop=False, skip_group_check=True)
                if first:
                    for q in range(GROUP):
                        t = nc.tensor.matmul(sums[q // 2][0:T, q % 2 * DE:q % 2 * DE + D], user[:, q * T:(q + 1) * T],
                                             m["w_user"][:], start=False, stop=False, skip_group_check=True)
                    t.then_inc(user_read, 1)
                with pe.Fori(0, TURNS) as turn:
                    for b in range(BODY):
                        if (b + AHEAD) % PB == 0:
                            s = (b + AHEAD) // PB
                            panel_ready(s % SLOTS, g * TURNS + turn + (2 if s == SLOTS else 1))
                        t = transposes(b + AHEAD)
                        pe.wait_ge(staged[b % 2], g * (TILES // 2) + turn * (BODY // 2) + (b // 2 + 1))
                        for q in range(GROUP):
                            t = nc.tensor.matmul(sums[q // 2][0:T, q % 2 * DE:q % 2 * DE + cols],
                                                 stage[b % STAGES][:, q * T:(q + 1) * T],
                                                 feats[:, bass.ds(turn * BODY + b, 1), 0:cols],
                                                 start=False, stop=False, skip_group_check=True)
                        if (b + AHEAD) % PB == PB - 1:
                            t.then_inc(panel_read, 1)
                for h in range(2):
                    t = nc.tensor.matmul(sums[h][0:T, 0:2 * DE], m["ones_row"][0:1, 0:T],
                                         m["zero_row"][0:1].rearrange("a q d -> a (q d)"),
                                         start=False, stop=True, skip_group_check=True)
                t.then_inc(sums_done, 1)

        def evacuate(engine, which):
            def copy(n, b):
                engine.wait_ge(turned, n + 1)
                src, dst = bank[b % STAGES][0:T, 0:GT], stage[b % STAGES][:]
                if which == 0:
                    nc.vector.tensor_copy(dst, src).then_inc(staged[0], 1)
                else:
                    nc.scalar.activation(dst, src, ACT.Copy).then_inc(staged[1], 1)
            return copy

        @block.vector
        def _(dve):
            copy = evacuate(dve, 0)
            nc.vector.memset(fresh[:], 0.0).then_inc(sums_read, 1)
            with dve.Fori(0, GROUPS) as g:
                with dve.Fori(0, TURNS) as turn:
                    for b in range(0, BODY, 2):
                        copy(g * TILES + turn * BODY + b, b)
                dve.wait_ge(sums_done, g + 1)
                dve.wait_ge(added, g + 1)
                for h in range(2):
                    two = sums[h][0:T, 0:2 * DE].rearrange("p (q d) -> p q d", d=DE)
                    if first:
                        nc.vector.tensor_scalar(fresh[:, 2 * h:2 * h + 2, :], two[:, :, 0:D], 0.0, None, ALU.max)
                        i = nc.vector.tensor_copy(m["degree"][:, bass.ds(g * GROUP + 2 * h, 2)], two[:, :, D])
                    else:
                        for q in range(2):
                            i = nc.vector.tensor_scalar(fresh[:, 2 * h + q, :], two[:, q, 0:D],
                                                        m["dinv"][:, bass.ds(g * GROUP + 2 * h + q, 1)],
                                                        0.0, ALU.mult, ALU.max)
                i.then_inc(sums_read, 1)

        @block.scalar
        def _(act):
            copy = evacuate(act, 1)
            with act.Fori(0, GROUPS) as g:
                with act.Fori(0, TURNS) as turn:
                    for b in range(1, BODY, 2):
                        copy(g * TILES + turn * BODY + b, b)

        @block.gpsimd
        def _(pool):
            def add(g):
                pool.wait_ge(sums_read, g + 2)
                here = m["stream"][:, bass.ds(g * GROUP, GROUP), :]
                nc.gpsimd.tensor_tensor(here, here, fresh[:], ALU.add).then_inc(added, 1)

            if first:
                nc.gpsimd.tensor_copy(user[:], m["wide2"][:, 0:GT]).then_inc(user_staged, 1)
            nc.gpsimd.memset(m["note"][:], 0.0).then_inc(added, 1)
            with pool.Fori(1, GROUPS) as g:
                if first:
                    pool.wait_ge(user_read, g)
                    nc.gpsimd.tensor_copy(user[:], m["wide2"][:, bass.ds(g * GT, GT)]).then_inc(user_staged, 1)
                add(g - 1)
            add(GROUPS - 1)


def common(nc, c):
    sb = lambda n, s: c.enter_context(nc.sbuf_tensor(n, s, F32))
    return {
        "bank": [c.enter_context(nc.psum_tensor(f"bank{k}", [128, 512], F32)) for k in range(8)],
        "ident": sb("ident", [128, 128]),
        "stream": sb("stream", [T, TILES, D]),
        "wide1": sb("wide1", [128, TILES * DE]),
        "wide2": sb("wide2", [128, N]),
        "mean": sb("mean", [T, TILES]), "rstd": sb("rstd", [T, TILES]),
        "degree": sb("degree", [T, TILES]), "dinv": sb("dinv", [T, TILES]),
        "w_item": sb("w_item", [D, D]), "w_user": sb("w_user", [D, D]), "gnn_w": sb("gnn_w", [D, D]),
        "w_ih": sb("w_ih", [D, 512]), "w_hh": sb("w_hh", [D, 512]), "gate_b": sb("gate_b", [D, 4]),
        "ones_row": sb("ones_row", [1, 128]), "zero_row": sb("zero_row", [1, 2, DE]),
        "open_row": sb("open_row", [1, 2, DE]), "note": sb("note", [1, 2]),
    }


CHUNKS = 200
STEPS = N // CHUNKS
LANES = [(0, CHUNKS // 2), (CHUNKS // 2, CHUNKS)]
TOLERANCE = 1e-6
SURE = 2


def lstm(nc, m):
    with ExitStack() as c:
        sem = lambda n: c.enter_context(nc.semaphore(n + "_l"))
        sb = lambda n, s, d=F32: c.enter_context(nc.sbuf_tensor(n + "_l", s, d))
        prepared, sweep_open, compared = sem("prepared"), sem("sweep_open"), sem("compared")
        gates_summed = [sem(f"gates_summed{k}") for k in range(2)]
        gates_read = [sem(f"gates_read{k}") for k in range(2)]
        gates_done = [sem(f"gates_done{k}") for k in range(2)]
        parts_done = [sem(f"parts_done{k}") for k in range(2)]
        cell_done = [sem(f"cell_done{k}") for k in range(2)]
        tanh_done = [sem(f"tanh_done{k}") for k in range(2)]
        u_done = [sem(f"u_done{k}") for k in range(2)]
        marked, counted, flag_set = sem("marked"), sem("counted"), sem("flag_set")
        W = [hi - lo for lo, hi in LANES]
        pre = [sb(f"pre{k}", [D, 4, W[k]]) for k in range(2)]
        gate = [sb(f"gate{k}", [D, 4, W[k]]) for k in range(2)]
        keep = [sb(f"keep{k}", [D, W[k]]) for k in range(2)]
        put = [sb(f"put{k}", [D, W[k]]) for k in range(2)]
        tc = [sb(f"tc{k}", [D, W[k]]) for k in range(2)]
        cell = sb("cell", [D, CHUNKS])
        cell_start, u_start = sb("cell_start", [D, CHUNKS]), sb("u_start", [D, CHUNKS])
        near = sb("near", [D, 2, CHUNKS - 1])
        ones_col, total, flag = sb("ones_col", [D, 1]), sb("total", [1, 1]), sb("flag", [1, 1], I32)
        sums = [[m["bank"][0], m["bank"][1]], [m["bank"][2], m["bank"][3]]]
        tally = m["bank"][4]
        inputs = m["wide2"][:].rearrange("p (c l) -> p c l", l=STEPS)
        u_before = m["wide1"][:, 0:N].rearrange("p (c l) -> p c l", l=STEPS)
        u_now = m["wide1"][:, 1:N + 1].rearrange("p (c l) -> p c l", l=STEPS)
        I, F, G, O = range(4)
        block = c.enter_context(nc.Block())

        @block.tensor
        def _(pe):
            def sweep(s):
                with pe.Fori(0, STEPS // 2) as pair:
                    for odd in range(2):
                        t = pair * 2 + odd
                        for k, (lo, hi) in enumerate(LANES):
                            bank = sums[k][odd][:, 0:4 * W[k]].rearrange("p (g c) -> p g c", g=4)
                            for g in range(4):
                                nc.tensor.matmul(bank[:, g, :], m["w_ih"][:, g * D:(g + 1) * D],
                                                 inputs[:, lo:hi, bass.ds(t, 1)],
                                                 start=(g == 0), stop=False, skip_group_check=True)
                            pe.wait_ge(u_done[k], s * (STEPS + 1) + t + 1)
                            for g in range(4):
                                i = nc.tensor.matmul(bank[:, g, :], m["w_hh"][:, g * D:(g + 1) * D],
                                                     u_before[:, lo:hi, bass.ds(t, 1)],
                                                     start=False, stop=(g == 3), skip_group_check=True)
                            i.then_inc(gates_summed[k], 1)
                pe.wait_ge(marked, s + 1)
                nc.tensor.matmul(tally[0:1, 0:2 * (CHUNKS - 1)], ones_col[:], near[:].rearrange("p a c -> p (a c)"),
                                 start=True, stop=True).then_inc(counted, 1)

            pe.wait_ge(prepared, 1)
            with pe.Fori(0, SURE) as s:
                sweep(s)
            pe.wait_ge(flag_set, 1)
            unsettled = pe.value_load(flag[0:1, 0:1])
            with pe.If(unsettled > 0):
                sweep(SURE)
            pe.wait_ge(flag_set, 2)
            still_unsettled = pe.value_load(flag[0:1, 0:1])
            with pe.If(still_unsettled > 0):
                with pe.Fori(SURE + 1, CHUNKS) as s:
                    sweep(s)

        @block.scalar
        def _(act):
            def gates(k, n):
                act.wait_ge(gates_read[k], n + 1)
                nc.scalar.activation(gate[k][:], pre[k][:], ACT.Tanh).then_inc(gates_done[k], 1)

            def squash(k, n):
                lo, hi = LANES[k]
                act.wait_ge(cell_done[k], n + 1)
                nc.scalar.activation(tc[k][:], cell[:, lo:hi], ACT.Tanh, scale=0.5).then_inc(tanh_done[k], 1)

            def sweep(s):
                gates(0, s * STEPS)
                squash(0, s * STEPS)
                gates(1, s * STEPS)
                with act.Fori(1, STEPS) as t:
                    squash(1, s * STEPS + t - 1)
                    gates(0, s * STEPS + t)
                    squash(0, s * STEPS + t)
                    gates(1, s * STEPS + t)
                squash(1, s * STEPS + (STEPS - 1))

            with act.Fori(0, SURE) as s:
                sweep(s)
            act.wait_ge(flag_set, 1)
            unsettled = act.value_load(flag[0:1, 0:1])
            with act.If(unsettled > 0):
                sweep(SURE)
            act.wait_ge(flag_set, 2)
            still_unsettled = act.value_load(flag[0:1, 0:1])
            with act.If(still_unsettled > 0):
                with act.Fori(SURE + 1, CHUNKS) as s:
                    sweep(s)

        @block.vector
        def _(dve):
            for w, gain in ((m["w_ih"], 0.5), (m["w_hh"], 0.25)):
                nc.vector.tensor_scalar(w[:, 0:2 * D], w[:, 0:2 * D], gain, None, ALU.mult)
                nc.vector.tensor_scalar(w[:, 3 * D:4 * D], w[:, 3 * D:4 * D], gain, None, ALU.mult)
            nc.vector.tensor_scalar(m["w_hh"][:, 2 * D:3 * D], m["w_hh"][:, 2 * D:3 * D], 0.5, None, ALU.mult)
            nc.vector.tensor_scalar(m["gate_b"][:, 0:2], m["gate_b"][:, 0:2], 0.5, None, ALU.mult)
            nc.vector.tensor_scalar(m["gate_b"][:, 3:4], m["gate_b"][:, 3:4], 0.5, None, ALU.mult)
            nc.vector.memset(u_before[:, :, 0], 0.0)
            nc.vector.memset(cell_start[:], 0.0)
            nc.vector.memset(u_start[:], 0.0)
            nc.vector.memset(ones_col[:], 1.0).then_inc(prepared, 1)
            dve.wait_ge(prepared, 1)

            def take(k, n, odd):
                dve.wait_ge(gates_summed[k], n + 1)
                bank = sums[k][odd][:, 0:4 * W[k]].rearrange("p (g c) -> p g c", g=4)
                bias = m["gate_b"][:].rearrange("p (g a) -> p g a", a=1).to_broadcast([D, 4, W[k]])
                nc.vector.tensor_tensor(pre[k][:], bank, bias, ALU.add).then_inc(gates_read[k], 1)

            def update(k, n):
                lo, hi = LANES[k]
                dve.wait_ge(gates_done[k], n + 1)
                nc.vector.scalar_tensor_tensor(put[k][:], gate[k][:, I, :], 1.0, gate[k][:, G, :], ALU.add, ALU.mult)
                nc.vector.scalar_tensor_tensor(keep[k][:], gate[k][:, F, :], 1.0, cell[:, lo:hi], ALU.add, ALU.mult
                                               ).then_inc(parts_done[k], 1)
                dve.wait_ge(parts_done[k], n + 1)
                nc.vector.scalar_tensor_tensor(cell[:, lo:hi], keep[k][:], 0.5, put[k][:], ALU.mult, ALU.add
                                               ).then_inc(cell_done[k], 1)

            def emit(k, n, t):
                lo, hi = LANES[k]
                dve.wait_ge(tanh_done[k], n + 1)
                nc.vector.scalar_tensor_tensor(u_now[:, lo:hi, t] if isinstance(t, int) else u_now[:, lo:hi, bass.ds(t, 1)],
                                               gate[k][:, O, :], 1.0, tc[k][:], ALU.add, ALU.mult).then_inc(u_done[k], 1)

            def sweep(s):
                nc.vector.tensor_copy(cell[:], cell_start[:]).then_inc(sweep_open, 1)
                dve.wait_ge(sweep_open, s + 1)
                dve.sem_inc(u_done[0], 1)
                dve.sem_inc(u_done[1], 1)
                n = s * STEPS
                take(0, n, 0)
                update(0, n)
                take(1, n, 0)
                emit(0, n, 0)

                def step_of(t, odd):
                    n = s * STEPS + t
                    update(1, n - 1)
                    take(0, n, odd)
                    emit(1, n - 1, t - 1)
                    update(0, n)
                    take(1, n, odd)
                    emit(0, n, t)
                with dve.Fori(0, STEPS // 2 - 1) as pair:
                    step_of(pair * 2 + 1, 1)
                    step_of(pair * 2 + 2, 0)
                step_of(STEPS - 1, 1)
                n = s * STEPS + (STEPS - 1)
                update(1, n)
                emit(1, n, STEPS - 1)
                dve.wait_ge(u_done[1], n + s + 2)
                step = [0]

                def after(i):
                    step[0] = step[0] + 1
                    i.then_inc(compared, 1)
                    dve.wait_ge(compared, s * 8 + step[0])
                last = CHUNKS - 1
                after(nc.vector.tensor_tensor(near[:, 0, :], u_before[:, 1:CHUNKS, 0], u_start[:, 1:CHUNKS], ALU.subtract))
                after(nc.vector.tensor_tensor(near[:, 1, :], cell[:, 0:last], cell_start[:, 1:CHUNKS], ALU.subtract))
                after(nc.vector.tensor_tensor(near[:], near[:], near[:], ALU.mult))
                after(nc.vector.tensor_copy(u_start[:, 1:CHUNKS], u_before[:, 1:CHUNKS, 0]))
                after(nc.vector.tensor_copy(cell_start[:, 1:CHUNKS], cell[:, 0:last]))
                nc.vector.tensor_scalar(near[:], near[:], TOLERANCE * TOLERANCE, None, ALU.is_le).then_inc(marked, 1)
                dve.wait_ge(counted, s + 1)
                after(nc.vector.tensor_reduce(total[:], tally[0:1, 0:2 * last], AXX, ALU.add))
                after(nc.vector.tensor_scalar(total[:], total[:], -1.0, float(2 * last * D), ALU.mult, ALU.add))
                after(nc.vector.tensor_copy(flag[:], total[:]))

            with dve.Fori(0, SURE) as s:
                sweep(s)
            dve.sem_inc(flag_set, 1)
            unsettled = dve.value_load(flag[0:1, 0:1])
            with dve.If(unsettled > 0):
                sweep(SURE)
            dve.sem_inc(flag_set, 1)
            still_unsettled = dve.value_load(flag[0:1, 0:1])
            with dve.If(still_unsettled > 0):
                with dve.Fori(SURE + 1, CHUNKS) as s:
                    sweep(s)


def mix(nc, m, W_lin, b_lin, fw_att, bw_att):
    with ExitStack() as c:
        sem = lambda n: c.enter_context(nc.semaphore(n + "_m"))
        sb = lambda n, s: c.enter_context(nc.sbuf_tensor(n + "_m", s, F32))
        loaded, prepared, thr_made, step = sem("loaded"), sem("prepared"), sem("thr_made"), sem("step")
        logits, gated, scanned, summed = sem("logits"), sem("gated"), sem("scanned"), sem("summed")
        shifted, turned, added, total_known = sem("shifted"), sem("turned"), sem("added"), sem("total_known")
        w_lin, fw, bw, b_row = sb("w_lin", [D, 2]), sb("fw", [D, 1]), sb("bw", [D, 1]), sb("b_row", [1, 2])
        w_diff, thr = sb("w_diff", [D, 128]), sb("thr", [D, 1])
        k_inc, k_own, k_total = sb("k_inc", [D, 1]), sb("k_own", [D, 1]), sb("k_total", [D, 1])
        ones = sb("ones", [D, GT])
        own = [sb(f"own{k}", [D, GT]) for k in range(2)]
        inc = [sb(f"inc{k}", [D, GT]) for k in range(2)]
        part = [sb(f"part{k}", [D, GT]) for k in range(2)]
        moved = [sb(f"moved{k}", [D, GT]) for k in range(2)]
        bank = m["bank"]
        u = m["wide1"][:, 1:N + 1]
        block = c.enter_context(nc.Block())

        @block.sync
        def _(sp):
            sp.dma_start(w_lin[:], W_lin.rearrange("l d -> d l"), allow_slow_non_contiguous=True).then_inc(loaded, 16)
            sp.dma_start(fw[:], fw_att.rearrange("a d -> d a"), allow_slow_non_contiguous=True).then_inc(loaded, 16)
            sp.dma_start(bw[:], bw_att.rearrange("a d -> d a"), allow_slow_non_contiguous=True).then_inc(loaded, 16)
            sp.dma_start(b_row[:], b_lin.rearrange("(a l) -> a l", a=1)).then_inc(loaded, 16)

        @block.tensor
        def _(pe):
            pe.wait_ge(prepared, 2)
            nc.tensor.matmul(bank[2][:, 0:1], m["ones_row"][0:1, :], b_row[0:1, 0:1],
                             start=True, stop=True).then_inc(thr_made, 1)
            with pe.Fori(0, GROUPS // 2) as i:
                for k in range(2):
                    pe.wait_ge(gated, i * 2 + (k + 1))
                    nc.tensor.matmul(bank[k][:, 0:GT], w_diff[:], u[:, bass.ds((i * 2 + k) * GT, GT)],
                                     start=True, stop=True).then_inc(logits, 1)
            with pe.Fori(0, GROUPS // 2) as i:
                for k in range(2):
                    pe.wait_ge(shifted, i * 2 + (k + 1))
                    pe.wait_ge(added, i * 2 + (k + 1))
                    for q in range(GROUP):
                        t = nc.tensor.transpose(bank[3 + k][0:T, q * D:(q + 1) * D], moved[k][:, q * T:(q + 1) * T],
                                                m["ident"][:])
                    t.then_inc(turned, 1)

        @block.vector
        def _(dve):
            link = chain(dve, step)
            dve.wait_ge(loaded, 64)
            link(nc.vector.memset(ones[:], 1.0))
            link(nc.vector.tensor_tensor(w_lin[:, 0:1], w_lin[:, 1:2], w_lin[:, 0:1], ALU.subtract))
            nc.vector.tensor_scalar(w_diff[:], ones[:, 0:128], w_lin[:, 0:1], None, ALU.mult).then_inc(prepared, 1)
            link(nc.vector.tensor_tensor(b_row[0:1, 0:1], b_row[0:1, 0:1], b_row[0:1, 1:2], ALU.subtract))
            nc.vector.tensor_scalar(b_row[0:1, 0:1], b_row[0:1, 0:1], 2.0, None, ALU.mult).then_inc(prepared, 1)
            link(nc.vector.tensor_tensor(k_inc[:], fw[:], bw[:], ALU.subtract))
            nc.vector.tensor_scalar(k_inc[:], k_inc[:], 0.5, None, ALU.mult)
            nc.vector.tensor_scalar(k_own[:], fw[:], -0.5, None, ALU.mult)
            nc.vector.tensor_scalar(k_total[:], bw[:], 0.5, None, ALU.mult)
            nc.vector.memset(inc[1][:], 0.0)
            dve.wait_ge(thr_made, 1)
            link(nc.vector.tensor_copy(thr[:], bank[2][:, 0:1]))
            dve.sem_inc(gated, 2)
            dve.sem_inc(added, 2)
            with dve.Fori(0, GROUPS // 2) as i:
                for k in range(2):
                    n = i * 2 + k
                    here = u[:, bass.ds(n * GT, GT)]
                    dve.wait_ge(logits, n + 1)
                    nc.vector.scalar_tensor_tensor(own[k][:], bank[k][:, 0:GT], thr[:], here, ALU.is_gt, ALU.mult
                                                   ).then_inc(gated, 1)
                    dve.wait_ge(gated, n + 3)
                    nc.vector.tensor_tensor_scan(inc[k][:], ones[:], own[k][:], inc[1 - k][:, GT - 1:GT], ALU.mult, ALU.add
                                                 ).then_inc(scanned, 1)
                    dve.wait_ge(scanned, n + 1)
                    nc.vector.scalar_tensor_tensor(part[k][:], inc[k][:], k_inc[:], here, ALU.mult, ALU.add
                                                   ).then_inc(summed, 1)
                    dve.wait_ge(summed, 2 * n + 1)
                    nc.vector.scalar_tensor_tensor(here, own[k][:], k_own[:], part[k][:], ALU.mult, ALU.add
                                                   ).then_inc(summed, 1)
            nc.vector.tensor_tensor(k_total[:], k_total[:], inc[1][:, GT - 1:GT], ALU.mult).then_inc(total_known, 1)
            with dve.Fori(0, GROUPS // 2) as i:
                for k in range(2):
                    n = i * 2 + k
                    dve.wait_ge(turned, n + 1)
                    here = m["stream"][:, bass.ds(n * GROUP, GROUP), :]
                    nc.vector.tensor_tensor(here, bank[3 + k][0:T, 0:GD].rearrange("p (q d) -> p q d", d=D), here, ALU.add
                                            ).then_inc(added, 1)

        @block.scalar
        def _(act):
            act.wait_ge(total_known, 1)
            with act.Fori(0, GROUPS // 2) as i:
                for k in range(2):
                    n = i * 2 + k
                    act.wait_ge(added, n + 1)
                    nc.scalar.activation(moved[k][:], u[:, bass.ds(n * GT, GT)], ACT.Identity, bias=k_total[:]
                                         ).then_inc(shifted, 1)


def graph_features(nc, m):
    with ExitStack() as c:
        sem = lambda n: c.enter_context(nc.semaphore(n + "_f"))
        sb = lambda n, s: c.enter_context(nc.sbuf_tensor(n + "_f", s, F32))
        rooted, step, rows_ready, turned, kept, made, stored = (
            sem("rooted"), sem("step"), sem("rows_ready"), sem("turned"), sem("kept"), sem("made"), sem("stored"))
        rows = [sb(f"rows{k}", [T, GROUP, D]) for k in range(2)]
        norm_t = [sb(f"norm_t{k}", [D, GT]) for k in range(2)]
        root, spare = sb("root", [T, TILES]), sb("spare", [T, TILES])
        bank = m["bank"]
        feats = m["wide1"][0:T, 0:TILES * DE].rearrange("p (t d) -> p t d", d=DE)
        block = c.enter_context(nc.Block())

        @block.vector
        def _(dve):
            link = chain(dve, step)
            dve.wait_ge(rooted, 1)
            inverse_root(nc, link, m["dinv"][:], root[:], m["degree"][:], spare[:])

            def normalise(g, k):
                for q in range(GROUP):
                    i = nc.vector.tensor_scalar(rows[k][:, q, :], m["stream"][:, bass.ds(g * GROUP + q, 1), :],
                                                m["mean"][:, bass.ds(g * GROUP + q, 1)],
                                                m["rstd"][:, bass.ds(g * GROUP + q, 1)], ALU.subtract, ALU.mult)
                i.then_inc(rows_ready, 1)

            def store(g, k):
                dve.wait_ge(made, g + 1)
                scale = m["dinv"][:, bass.ds(g * GROUP, GROUP)].rearrange("p (q a) -> p q a", a=1).to_broadcast([T, GROUP, D])
                nc.vector.tensor_tensor(feats[:, bass.ds(g * GROUP, GROUP), 0:D],
                                        bank[2 + k][0:T, 0:GD].rearrange("p (q d) -> p q d", d=D), scale, ALU.mult
                                        ).then_inc(stored, 1)
            normalise(0, 0)
            normalise(1, 1)
            with dve.Fori(0, GROUPS // 2 - 1) as i:
                for k in range(2):
                    store(i * 2 + k, k)
                    normalise(i * 2 + (2 + k), k)
            store(GROUPS - 2, 0)
            store(GROUPS - 1, 1)

        @block.tensor
        def _(pe):
            def work(n, k, free):
                pe.wait_ge(rows_ready, n + 1)
                for q in range(GROUP):
                    t = nc.tensor.transpose(bank[k][:, q * T:(q + 1) * T], rows[k][:, q, :], m["ident"][0:T, 0:T])
                t.then_inc(turned, 1)
                pe.wait_ge(kept, n + 1)
                if free is not None:
                    pe.wait_ge(stored, free)
                for q in range(GROUP):
                    t = nc.tensor.matmul(bank[2 + k][0:T, q * D:(q + 1) * D], norm_t[k][:, q * T:(q + 1) * T], m["gnn_w"][:],
                                         start=(q == 0), stop=(q == GROUP - 1), skip_group_check=True)
                t.then_inc(made, 1)
            work(0, 0, None)
            work(1, 1, None)
            with pe.Fori(1, GROUPS // 2) as i:
                for k in range(2):
                    work(i * 2 + k, k, i * 2 + (k - 1))

        @block.scalar
        def _(act):
            nc.scalar.activation(root[:], m["degree"][:], ACT.Sqrt).then_inc(rooted, 1)
            with act.Fori(0, GROUPS // 2) as i:
                for k in range(2):
                    act.wait_ge(turned, i * 2 + (k + 1))
                    nc.scalar.activation(norm_t[k][:], bank[k][:, 0:GT], ACT.Copy).then_inc(kept, 1)


HEADS, HP, SL = 8, 64, 64
HID = HEADS * HP
HS = HEADS * SL
KC = HID // 128


def slice_weights(nc, m, W_fx, b_fx, W_x, b_x, W_slice, b_slice, temperature, fcD_w, hy_in_w, hy_out_w, out_w):
    with ExitStack() as c:
        sem = lambda n: c.enter_context(nc.semaphore(n + "_w"))
        sb = lambda n, s: c.enter_context(nc.sbuf_tensor(n + "_w", s, F32))
        loaded, turned, kept, step, temp_ready, temp_made, products = (
            sem("loaded"), sem("turned"), sem("kept"), sem("step"), sem("temp_ready"), sem("temp_made"), sem("products"))
        in_raw, in_last = sb("in_raw", [128, 9, HID]), sb("in_last", [16, HID])
        out_raw, o_raw, fx_raw = sb("out_raw", [128, KC, HID]), sb("o_raw", [128, HID]), sb("fx_raw", [128, KC, D])
        fcd_raw, x_raw, s_raw, s_t = sb("fcd_raw", [HEADS, HID]), sb("x_raw", [HP, HEADS, D]), sb("s_raw", [SL, HP]), sb("s_t", [HP, SL])
        bx, t_row, t_wide, bs_row = sb("bx", [HP, HEADS]), sb("t_row", [1, HEADS]), sb("t_wide", [1, HS]), sb("bs_row", [1, HS])
        t_all = sb("t_all", [128, HS])
        bank = m["bank"]
        row = lambda v: v.rearrange("(a d) -> a d", a=1)
        turns = [(m["s_t"][:], s_raw[:], SL, HP)]
        for k in range(KC):
            turns.append((m["w_fx"][:, k * 128:(k + 1) * 128], fx_raw[:, k, :], 128, D))
            turns.append((m["fcd"][:, k, :], fcd_raw[:, k * 128:(k + 1) * 128], HEADS, 128))
            for r in range(9):
                turns.append((m["w_in"][:, k, r * 128:(r + 1) * 128], in_raw[:, r, k * 128:(k + 1) * 128], 128, 128))
            turns.append((m["w_in"][:, k, 1152:1168], in_last[:, k * 128:(k + 1) * 128], 16, 128))
            for r in range(KC):
                turns.append((m["w_mix"][:, k, r * 128:(r + 1) * 128], out_raw[:, r, k * 128:(k + 1) * 128], 128, 128))
        for h in range(HEADS):
            turns.append((m["w_out"][:, h, :], o_raw[:, h * HP:(h + 1) * HP], 128, HP))
        loads = 9 + 2
        block = c.enter_context(nc.Block())

        @block.sync
        def _(sp):
            sp.dma_start(s_raw[:], W_slice).then_inc(loaded, 16)
            sp.dma_start(fx_raw[:], W_fx.rearrange("(k p) d -> p k d", p=128)).then_inc(loaded, 16)
            sp.dma_start(fcd_raw[:], fcD_w).then_inc(loaded, 16)
            sp.dma_start(in_raw[:], hy_in_w[0:1152].rearrange("(r p) d -> p r d", p=128)).then_inc(loaded, 16)
            sp.dma_start(in_last[:], hy_in_w[1152:1168]).then_inc(loaded, 16)
            sp.dma_start(out_raw[:], hy_out_w.rearrange("(r p) d -> p r d", p=128)).then_inc(loaded, 16)
            sp.dma_start(o_raw[:], out_w).then_inc(loaded, 16)
            sp.dma_start(x_raw[:], W_x.rearrange("(h p) d -> p h d", p=HP)).then_inc(loaded, 16)
            sp.dma_start(bx[:], b_x.rearrange("(h p) -> p h", p=HP), allow_slow_non_contiguous=True).then_inc(loaded, 16)
            sp.dma_start(t_row[:], temperature.rearrange("a h b c -> a (h b c)")).then_inc(loaded, 16)
            sp.dma_start(m["b_fx"][:], row(b_fx)).then_inc(loaded, 16)
            for h in range(HEADS):
                sp.dma_start(bs_row[0:1, h * SL:(h + 1) * SL], row(b_slice)).then_inc(loaded, 16)

        @block.tensor
        def _(pe):
            pe.wait_ge(loaded, 16 * (loads + HEADS))
            for n, (dst, src, r, cc) in enumerate(turns):
                if n >= 4:
                    pe.wait_ge(kept, n - 3)
                nc.tensor.transpose(bank[n % 4][0:cc, 0:r], src, m["ident"][0:r, 0:r]).then_inc(turned, 1)
            pe.wait_ge(kept, len(turns))
            pe.wait_ge(temp_ready, 1)
            nc.tensor.matmul(bank[4][:, :], m["ones_row"][:], t_wide[:], start=True, stop=True).then_inc(temp_made, 1)
            for h in range(HEADS):
                nc.tensor.matmul(bank[5][:, h * SL:(h + 1) * SL], x_raw[:, h, :], m["s_t"][:],
                                 start=(h == 0), stop=(h == HEADS - 1), skip_group_check=True)
            for h in range(HEADS):
                i = nc.tensor.matmul(bank[6][0:1, h * SL:(h + 1) * SL], bx[:, h:h + 1], m["s_t"][:],
                                     start=(h == 0), stop=(h == HEADS - 1), skip_group_check=True)
            i.then_inc(products, 1)

        @block.vector
        def _(dve):
            for n, (dst, src, r, cc) in enumerate(turns):
                dve.wait_ge(turned, n + 1)
                nc.vector.tensor_copy(dst, bank[n % 4][0:cc, 0:r]).then_inc(kept, 1)
            link = chain(dve, step)
            link(nc.vector.tensor_scalar(t_row[:], t_row[:], 1e-6, None, ALU.max))
            link(nc.vector.reciprocal(t_row[:], t_row[:]))
            nc.vector.tensor_copy(t_wide[:].rearrange("a (h g) -> a h g", g=SL),
                                  t_row[:].rearrange("a (h b) -> a h b", b=1).to_broadcast([1, HEADS, SL])).then_inc(temp_ready, 1)
            dve.wait_ge(temp_made, 1)
            link(nc.vector.tensor_copy(t_all[:], bank[4][:, :]))
            dve.wait_ge(products, 1)
            nc.vector.tensor_tensor(m["w_logit"][:], bank[5][:, :], t_all[:], ALU.mult)
            link(nc.vector.tensor_tensor(bs_row[:], bank[6][0:1, :], bs_row[:], ALU.add))
            nc.vector.tensor_tensor(m["b_logit"][:], bs_row[:], t_wide[:], ALU.mult)


def slice_tokens(nc, m, scratch):
    with ExitStack() as c:
        sem = lambda n: c.enter_context(nc.semaphore(n + "_s"))
        sb = lambda n, s: c.enter_context(nc.sbuf_tensor(n + "_s", s, F32))
        rows_ready, turned, kept, logits, maxed, lessened, exped, summed, inverted, weighed = (
            sem("rows_ready"), sem("turned"), sem("kept"), sem("logits"), sem("maxed"), sem("lessened"), sem("exped"),
            sem("summed"), sem("inverted"), sem("weighed"))
        w_turned, w_kept, used, ones_set = sem("w_turned"), sem("w_kept"), sem("used"), sem("ones_set")
        w_stored = [sem(f"w_stored{k}") for k in range(2)]
        rows = [sb(f"rows{k}", [T, GROUP, DE]) for k in range(2)]
        norm_t = [sb(f"norm_t{k}", [D, GT]) for k in range(2)]
        less = [sb(f"less{k}", [T, HEADS, SL]) for k in range(2)]
        weight = [sb(f"weight{k}", [T, HEADS, SL]) for k in range(2)]
        peak = [sb(f"peak{k}", [T, HEADS]) for k in range(2)]
        total = [sb(f"total{k}", [T, HEADS]) for k in range(2)]
        weight_t = [sb(f"weight_t{k}", [128, KC, T]) for k in range(2)]
        bank = m["bank"]
        block = c.enter_context(nc.Block())
        wide = lambda v: v[:].rearrange("p (h a) -> p h a", a=1).to_broadcast([T, HEADS, SL])

        def both_groups(i, first, last, tile, ahead):
            for k in range(2):
                g = i * 2 + k
                for q in range(GROUP):
                    tile(g * GROUP + q, k, q, first and k == 0 and q == 0)
                    if not (last and k == 1):
                        ahead(g + 1, 1 - k, q)

        def all_groups(engine, tile, ahead):
            both_groups(0, True, False, tile, ahead)
            with engine.Fori(1, GROUPS // 2 - 1) as i:
                both_groups(i, False, False, tile, ahead)
            both_groups(GROUPS // 2 - 1, False, True, tile, ahead)

        def wait_from(engine, s, value):
            if not isinstance(value, int) or value > 0:
                engine.wait_ge(s, value)

        @block.vector
        def _(dve):
            for k in range(2):
                nc.vector.memset(rows[k][:, :, D:DE], 1.0)

            def normalise(g, k):
                wait_from(dve, w_turned, (g - 1) * GROUP)
                for q in range(GROUP):
                    i = nc.vector.tensor_scalar(rows[k][:, q, 0:D], m["stream"][:, bass.ds(g * GROUP + q, 1), :],
                                                m["mean"][:, bass.ds(g * GROUP + q, 1)],
                                                m["rstd"][:, bass.ds(g * GROUP + q, 1)], ALU.subtract, ALU.mult)
                i.then_inc(rows_ready, 1)

            def finish(n, b):
                dve.wait_ge(exped, n + 1)
                nc.vector.tensor_reduce(total[b][:], less[b][:], AXX, ALU.add).then_inc(summed, 1)
                dve.wait_ge(summed, n + 1)
                nc.vector.reciprocal(total[b][:], total[b][:]).then_inc(inverted, 1)
                dve.wait_ge(inverted, n + 1)
                wait_from(dve, w_turned, n - 1)
                nc.vector.tensor_tensor(weight[b][:], less[b][:], wide(total[b]), ALU.mult).then_inc(weighed, 1)

            def tile(n, k, q, nothing_before):
                b = q % 2
                sums = bank[2 + b][0:T, :].rearrange("p (h g) -> p h g", g=SL)
                dve.wait_ge(logits, n + 1)
                nc.vector.tensor_reduce(peak[b][:], sums, AXX, ALU.max).then_inc(maxed, 1)
                dve.wait_ge(maxed, n + 1)
                nc.vector.tensor_tensor(less[b][:], sums, wide(peak[b]), ALU.subtract).then_inc(lessened, 1)
                if not nothing_before:
                    finish(n - 1, 1 - b)

            def ahead(g, k, q):
                if q == 1:
                    normalise(g, k)
            normalise(0, 0)
            all_groups(dve, tile, ahead)
            finish(TILES - 1, 1)

        @block.scalar
        def _(act):
            def keep_rows(g, k):
                act.wait_ge(turned, g + 1)
                nc.scalar.activation(norm_t[k][:], bank[k][:, 0:GT], ACT.Copy).then_inc(kept, 1)

            def keep_weights(n, b, stores):
                act.wait_ge(w_turned, n + 1)
                wait_from(act, w_stored[b], stores * 16)
                nc.scalar.activation(weight_t[b][:].rearrange("p k t -> p (k t)"), bank[4 + b][:, 0:KC * T],
                                     ACT.Copy).then_inc(w_kept, 1)

            def tile(n, k, q, nothing_before):
                b = q % 2
                act.wait_ge(lessened, n + 1)
                nc.scalar.activation(less[b][:], less[b][:], ACT.Exp).then_inc(exped, 1)
                if not nothing_before:
                    half = (n - q) // GROUP * 2 if isinstance(n, int) else half_of[0] + 2 * k
                    keep_weights(n - 1, 1 - b, half + (q - 1) // 2)

            def ahead(g, k, q):
                if q == 2:
                    keep_rows(g, k)
            half_of = [0]
            keep_rows(0, 0)
            both_groups(0, True, False, tile, ahead)
            with act.Fori(1, GROUPS // 2 - 1) as i:
                half_of[0] = i * 4
                both_groups(i, False, False, tile, ahead)
            both_groups(GROUPS // 2 - 1, False, True, tile, ahead)
            keep_weights(TILES - 1, 1, TILES // 2 - 1)

        @block.sync
        def _(sp):
            with sp.Fori(0, GROUPS) as g:
                for q in range(GROUP):
                    b = q % 2
                    sp.wait_ge(w_kept, g * GROUP + (q + 1))
                    sp.dma_start(scratch[bass.ds(g * GROUP + q, 1)].rearrange("a p c -> p (a c)"),
                                 weight_t[b][:].rearrange("p k t -> p (k t)")).then_inc(w_stored[b], 16)
            for b in range(2):
                sp.wait_ge(w_stored[b], 16 * (TILES // 2))

        @block.tensor
        def _(pe):
            zeros = m["zero_row"][0:1].rearrange("a q d -> a (q d)")
            for h in range(2):
                nc.tensor.matmul(bank[6 + h][:, 0:2 * DE], m["ones_row"][0:1, :], zeros, start=True, stop=False,
                                 skip_group_check=True)

            def turn_rows(g, k):
                pe.wait_ge(rows_ready, g + 1)
                for q in range(GROUP):
                    t = nc.tensor.transpose(bank[k][:, q * T:(q + 1) * T], rows[k][:, q, 0:D], m["ident"][0:T, 0:T])
                t.then_inc(turned, 1)

            def apply(n, k, q):
                b = q % 2
                pe.wait_ge(weighed, n + 1)
                flat = weight[b][:].rearrange("p h g -> p (h g)")
                for r in range(KC):
                    nc.tensor.matmul(bank[6 + r // 2][:, r % 2 * DE:(r % 2 + 1) * DE], flat[:, r * 128:(r + 1) * 128],
                                     rows[k][:, q, :], start=False, stop=False, skip_group_check=True)
                wait_from(pe, w_kept, n - 1)
                for r in range(KC):
                    t = nc.tensor.transpose(bank[4 + b][:, r * T:(r + 1) * T], flat[:, r * 128:(r + 1) * 128],
                                            m["ident"][0:T, 0:T])
                t.then_inc(w_turned, 1)

            def tile(n, k, q, nothing_before):
                b = q % 2
                if q == 0:
                    pe.wait_ge(kept, group_of[0] + (k + 1))
                nc.tensor.matmul(bank[2 + b][0:T, :], m["ones_row"][0:1, 0:T], m["b_logit"][:], start=True, stop=False)
                nc.tensor.matmul(bank[2 + b][0:T, :], norm_t[k][:, q * T:(q + 1) * T], m["w_logit"][:],
                                 start=False, stop=True).then_inc(logits, 1)
                if not nothing_before:
                    apply(n - 1, k if q else 1 - k, (q - 1) % GROUP)

            def ahead(g, k, q):
                if q == 2:
                    turn_rows(g, k)
            group_of = [0]
            turn_rows(0, 0)
            both_groups(0, True, False, tile, ahead)
            with pe.Fori(1, GROUPS // 2 - 1) as i:
                group_of[0] = i * 2
                both_groups(i, False, False, tile, ahead)
            group_of[0] = GROUPS - 2
            both_groups(GROUPS // 2 - 1, False, True, tile, ahead)
            apply(TILES - 1, 1, GROUP - 1)
            for h in range(2):
                nc.tensor.matmul(bank[6 + h][:, 0:2 * DE], m["ones_row"][0:1, :], zeros, start=False, stop=True,
                                 skip_group_check=True)


def mixer(nc, m, hy_conv_w, hy_conv_b, hy_dt_bias, hy_A_log, hy_D, hy_norm_w):
    with ExitStack() as c:
        sem = lambda n: c.enter_context(nc.semaphore(n + "_x"))
        sb = lambda n, s: c.enter_context(nc.sbuf_tensor(n + "_x", s, F32))
        loaded, pe_done, dve_done, act_done, step, dt_step = (
            sem("loaded"), sem("pe_done"), sem("dve_done"), sem("act_done"), sem("step"), sem("dt_step"))
        S = SL
        cw_x, cw_bc, cb_x, cb_bc = sb("cw_x", [128, KC, 3]), sb("cw_bc", [S, 2, 3]), sb("cb_x", [128, KC]), sb("cb_bc", [S, 2])
        dt_row, a_row, d_row, nw = sb("dt_row", [1, 16]), sb("a_row", [1, 16]), sb("d_row", [1, HEADS]), sb("nw", [128, KC])
        sums, sums_t, n_row, n_col = sb("sums", [128, KC, DE]), sb("sums_t", [D, HS]), sb("n_row", [1, HS]), sb("n_col", [S, HEADS])
        slices, slices_t = sb("slices", [S, HEADS, HP]), sb("slices_t", [128, KC, S])
        z_t, x_pad, bc_pad = sb("z_t", [128, KC, S]), sb("x_pad", [128, KC, S + 2]), sb("bc_pad", [S, 2, S + 2])
        x_t, bc_t, gate_x, gate_bc, gate_z = (
            sb("x_t", [128, KC, S]), sb("bc_t", [S, 2, S]), sb("gate_x", [128, KC, S]), sb("gate_bc", [S, 2, S]), sb("gate_z", [128, KC, S]))
        x_nat, z_nat = sb("x_nat", [S, HEADS, HP]), sb("z_nat", [S, HEADS, HP])
        raw_dt, dt, e_dt, l_dt, mask, w1, rate, over = (
            sb("raw_dt", [S, 16]), sb("dt", [S, 16]), sb("e_dt", [S, 16]), sb("l_dt", [S, 16]), sb("mask", [S, 16]), sb("w1", [S, 16]), sb("rate", [S, 16]), sb("over", [S, 16]))
        dA, dA_t = sb("dA", [S, 16]), sb("dA_t", [16, S])
        decay = sb("decay", [S, 2, HEADS, S])
        cb, mf, mb = sb("cb", [S, S]), sb("mf", [S, HEADS, S + 1]), sb("mb", [S, HEADS, S + 1])
        xf, xb = sb("xf", [S, HEADS, HP]), sb("xb", [S, HEADS, HP])
        fc, y, y2 = sb("fc", [S, HEADS]), sb("y", [S, HEADS, HP]), sb("y2", [S, HEADS, HP])
        ms, root, inv, spare = sb("ms", [S, 1]), sb("root", [S, 1]), sb("inv", [S, 1]), sb("spare", [S, 1])
        y_t, mixed = sb("y_t", [128, KC, S]), sb("mixed", [HP, HEADS, S])
        bank = m["bank"]
        ident, ones_row = m["ident"], m["ones_row"]
        row = lambda v: v.rearrange("(a d) -> a d", a=1)
        block = c.enter_context(nc.Block())

        @block.sync
        def _(sp):
            slow = dict(allow_slow_non_contiguous=True)
            sp.dma_start(cw_x[:], hy_conv_w[0:HID].rearrange("(k p) t -> p k t", p=128), **slow).then_inc(loaded, 16)
            sp.dma_start(cw_bc[:], hy_conv_w[HID:HID + 2 * S].rearrange("(k p) t -> p k t", p=S), **slow).then_inc(loaded, 16)
            sp.dma_start(cb_x[:], hy_conv_b[0:HID].rearrange("(k p) -> p k", p=128), **slow).then_inc(loaded, 16)
            sp.dma_start(cb_bc[:], hy_conv_b[HID:HID + 2 * S].rearrange("(k p) -> p k", p=S), **slow).then_inc(loaded, 16)
            sp.dma_start(nw[:], hy_norm_w.rearrange("(k p) -> p k", p=128), **slow).then_inc(loaded, 16)
            for h in range(2):
                sp.dma_start(dt_row[0:1, h * 8:h * 8 + 8], row(hy_dt_bias)).then_inc(loaded, 16)
                sp.dma_start(a_row[0:1, h * 8:h * 8 + 8], row(hy_A_log)).then_inc(loaded, 16)
            sp.dma_start(d_row[:], row(hy_D)).then_inc(loaded, 16)

        @block.tensor
        def _(pe):
            mm, turn = nc.tensor.matmul, nc.tensor.transpose
            loose = dict(skip_group_check=True)
            pe.wait_ge(dve_done, 1)
            for k in range(KC):
                i = turn(bank[0][:, k * 128:(k + 1) * 128], sums[:, k, 0:D], ident[:])
            for k in range(KC):
                i = mm(bank[1][0:1, k * 128:(k + 1) * 128], sums[:, k, D:DE], ident[:], start=(k == 0), stop=True, **loose)
            i.then_inc(pe_done, 1)
            pe.wait_ge(dve_done, 2)
            for h in range(HEADS):
                i = mm(bank[2][0:S, h:h + 1], n_row[0:1, h * S:(h + 1) * S], ones_row[0:1, 0:1], start=(h == 0), stop=True, **loose)
            for h in range(HEADS):
                mm(bank[3][0:S, h * HP:(h + 1) * HP], sums_t[:, h * S:(h + 1) * S], m["w_fx"][:, h * HP:(h + 1) * HP],
                   start=(h == 0), stop=False, **loose)
                i = mm(bank[3][0:S, h * HP:(h + 1) * HP], n_row[0:1, h * S:(h + 1) * S], m["b_fx"][0:1, h * HP:(h + 1) * HP],
                       start=False, stop=True, **loose)
            i.then_inc(pe_done, 1)
            pe.wait_ge(dve_done, 3)
            for k in range(KC):
                i = turn(bank[4][:, k * S:(k + 1) * S], slices[:].rearrange("p h c -> p (h c)")[:, k * 128:(k + 1) * 128], ident[0:S, 0:S])
            i.then_inc(pe_done, 1)
            pe.wait_ge(dve_done, 4)
            pe.wait_ge(loaded, 16 * 10)
            for r in range(2 * KC):
                for k in range(KC):
                    mm(bank[5][:, r * S:(r + 1) * S], m["w_in"][:, k, r * 128:(r + 1) * 128], slices_t[:, k, :],
                       start=(r == 0 and k == 0), stop=(k == KC - 1), **loose)
            for r in range(2):
                for k in range(KC):
                    mm(bank[6][0:S, r * S:(r + 1) * S], m["w_in"][:, k, 1024 + r * S:1024 + (r + 1) * S], slices_t[:, k, :],
                       start=(r == 0 and k == 0), stop=(k == KC - 1), **loose)
            for k in range(KC):
                mm(bank[6][0:S, 128:144], slices_t[:, k, :], m["w_in"][:, k, 1152:1168], start=False, stop=False, **loose)
            mm(bank[6][0:S, 128:144], ones_row[0:1, 0:S], dt_row[:], start=False, stop=True, **loose)
            i = mm(bank[6][0:S, 144:160], ones_row[0:1, 0:S], a_row[:], start=False, stop=True, **loose)
            i.then_inc(pe_done, 1)
            pe.wait_ge(dve_done, 6)
            for k in range(KC):
                turn(bank[0][0:S, k * 128:(k + 1) * 128], x_t[:, k, :], ident[:])
            for k in range(KC):
                turn(bank[1][0:S, k * 128:(k + 1) * 128], z_t[:, k, :], ident[:])
            mm(bank[2][0:S, 0:S], bc_t[:, 0, :], bc_t[:, 1, :], start=True, stop=True)
            for k in range(KC):
                mm(bank[2][0:S, 128:128 + HEADS], x_t[:, k, :], m["fcd"][:, k, :], start=False, stop=False, **loose)
            mm(bank[2][0:S, 128:128 + HEADS], ones_row[0:1, 0:S], d_row[:], start=False, stop=True, **loose)
            pe.wait_ge(act_done, 5)
            i = turn(bank[7][0:16, 0:S], dA[:], ident[0:S, 0:S])
            i.then_inc(pe_done, 1)
            pe.wait_ge(dve_done, 7)
            for d in range(2):
                for h in range(HEADS):
                    j = d * HEADS + h
                    i = mm(bank[3 + d][0:S, h * S:(h + 1) * S], ident[0:16, j:j + 1].to_broadcast([16, S]), dA_t[:],
                           start=(h == 0), stop=True, **loose)
            i.then_inc(pe_done, 1)
            pe.wait_ge(dve_done, 8)
            for h in range(HEADS):
                mm(bank[5][0:S, h * HP:(h + 1) * HP], mf[:, h, 0:S], xf[:, h, :], start=(h == 0), stop=False, **loose)
                i = mm(bank[5][0:S, h * HP:(h + 1) * HP], mb[:, h, 1:S + 1], xb[:, h, :], start=False, stop=True, **loose)
            i.then_inc(pe_done, 1)
            pe.wait_ge(dve_done, 10)
            for k in range(KC):
                i = turn(bank[0][:, k * S:(k + 1) * S], y2[:].rearrange("p h c -> p (h c)")[:, k * 128:(k + 1) * 128], ident[0:S, 0:S])
            i.then_inc(pe_done, 1)
            pe.wait_ge(dve_done, 11)
            for h in range(HEADS):
                for k in range(KC):
                    i = mm(bank[1][0:HP, h * S:(h + 1) * S], m["w_mix"][:, k, h * HP:(h + 1) * HP], y_t[:, k, :],
                           start=(h == 0 and k == 0), stop=(k == KC - 1), **loose)
            i.then_inc(pe_done, 1)
            pe.wait_ge(dve_done, 12)
            for h in range(HEADS):
                p = h % 2 * S
                i = mm(bank[3][p:p + S, h // 2 * D:(h // 2 + 1) * D], mixed[:, h, :], m["w_out"][:, h, :],
                       start=(h < 2), stop=True, **loose)
            i.then_inc(pe_done, 1)

        @block.scalar
        def _(act):
            act.wait_ge(dve_done, 5)
            nc.scalar.activation(gate_x[:], x_t[:], ACT.Exp, scale=-1.0)
            nc.scalar.activation(gate_bc[:], bc_t[:], ACT.Exp, scale=-1.0)
            nc.scalar.activation(gate_z[:], z_t[:], ACT.Exp, scale=-1.0).then_inc(act_done, 1)
            nc.scalar.activation(e_dt[:], w1[:], ACT.Exp, scale=-1.0).then_inc(act_done, 1)
            nc.scalar.activation(rate[:], rate[:], ACT.Exp, scale=0.5).then_inc(act_done, 1)
            act.wait_ge(dt_step, 1)
            nc.scalar.activation(l_dt[:], w1[:], ACT.Ln).then_inc(act_done, 1)
            act.wait_ge(dt_step, 2)
            nc.scalar.activation(dA[:], mask[:], ACT.Exp, scale=-1.0).then_inc(act_done, 1)
            act.wait_ge(dve_done, 9)
            nc.scalar.activation(root[:], ms[:], ACT.Sqrt).then_inc(act_done, 1)

        @block.vector
        def _(dve):
            v = nc.vector
            link = chain(dve, step)
            wide = lambda t: t.rearrange("p (h a) -> p h a", a=1).to_broadcast([S, HEADS, HP])
            v.tensor_copy(sums[:, 0:2, :], bank[6][:, 0:2 * DE].rearrange("p (q d) -> p q d", d=DE))
            v.tensor_copy(sums[:, 2:4, :], bank[7][:, 0:2 * DE].rearrange("p (q d) -> p q d", d=DE)).then_inc(dve_done, 1)
            dve.wait_ge(pe_done, 1)
            v.tensor_copy(sums_t[:], bank[0][:, :])
            v.tensor_copy(n_row[:], bank[1][0:1, :]).then_inc(dve_done, 1)
            dve.wait_ge(pe_done, 2)
            link(v.tensor_scalar(n_col[:], bank[2][0:S, 0:HEADS], 1e-5, None, ALU.add))
            link(v.reciprocal(n_col[:], n_col[:]))
            v.tensor_tensor(slices[:], bank[3][0:S, :].rearrange("p (h c) -> p h c", c=HP), wide(n_col[:]), ALU.mult).then_inc(dve_done, 1)
            dve.wait_ge(pe_done, 3)
            v.tensor_copy(slices_t[:], bank[4][:, 0:KC * S].rearrange("p (k s) -> p k s", s=S)).then_inc(dve_done, 1)
            v.memset(x_pad[:, :, 0:2], 0.0)
            v.memset(bc_pad[:, :, 0:2], 0.0)
            v.memset(mf[:, :, 0:1], 0.0)
            v.memset(mb[:, :, S:S + 1], 0.0)
            dve.wait_ge(pe_done, 4)
            dve.wait_ge(loaded, 16 * 10)
            v.tensor_copy(z_t[:], bank[5][:, 0:KC * S].rearrange("p (k s) -> p k s", s=S))
            v.tensor_copy(x_pad[:, :, 2:S + 2], bank[5][:, KC * S:2 * KC * S].rearrange("p (k s) -> p k s", s=S))
            v.tensor_copy(bc_pad[:, :, 2:S + 2], bank[6][0:S, 0:2 * S].rearrange("p (k s) -> p k s", s=S))
            link(v.tensor_copy(raw_dt[:], bank[6][0:S, 128:144]))
            v.tensor_scalar(over[:], bank[6][0:S, 144:160], 88.7228, 1e30, ALU.is_gt, ALU.mult)
            v.tensor_scalar(rate[:], bank[6][0:S, 144:160], 88.7228, None, ALU.min)
            link(v.scalar_tensor_tensor(w1[:], raw_dt[:], -1.0, raw_dt[:], ALU.mult, ALU.max))
            for pad, out, taps, bias, n in ((x_pad, x_t, cw_x, cb_x, KC), (bc_pad, bc_t, cw_bc, cb_bc, 2)):
                for k in range(n):
                    i = v.tensor_scalar(out[:, k, :], pad[:, k, 0:S], taps[:, k, 0:1], bias[:, k:k + 1], ALU.mult, ALU.add)
                link(i)
                for tap in (1, 2):
                    for k in range(n):
                        i = v.scalar_tensor_tensor(out[:, k, :], pad[:, k, tap:S + tap], taps[:, k, tap:tap + 1], out[:, k, :],
                                                   ALU.mult, ALU.add)
                    link(i)
            dve.sem_inc(dve_done, 1)
            dve.wait_ge(act_done, 1)
            for g in (gate_x, gate_bc, gate_z):
                i = v.tensor_scalar(g[:], g[:], 1.0, None, ALU.add)
            link(i)
            for g in (gate_x, gate_bc, gate_z):
                i = v.reciprocal(g[:], g[:])
            link(i)
            v.tensor_tensor(x_t[:], x_t[:], gate_x[:], ALU.mult)
            v.tensor_tensor(bc_t[:], bc_t[:], gate_bc[:], ALU.mult)
            v.tensor_tensor(z_t[:], z_t[:], gate_z[:], ALU.mult).then_inc(dve_done, 1)
            dve.wait_ge(act_done, 3)
            v.tensor_scalar(w1[:], e_dt[:], 1.0, None, ALU.add).then_inc(dt_step, 1)
            dve.wait_ge(dt_step, 1)
            link(v.tensor_scalar(mask[:], w1[:], 1.0, None, ALU.is_equal))
            link(v.tensor_tensor(mask[:], mask[:], e_dt[:], ALU.mult))
            link(v.tensor_scalar(dt[:], w1[:], -1.0, 1e-30, ALU.add, ALU.max))
            link(v.reciprocal(dt[:], dt[:]))
            link(v.tensor_tensor(dt[:], dt[:], e_dt[:], ALU.mult))
            dve.wait_ge(act_done, 4)
            link(v.tensor_tensor(dt[:], dt[:], l_dt[:], ALU.mult))
            link(v.tensor_tensor(dt[:], dt[:], mask[:], ALU.add))
            link(v.scalar_tensor_tensor(dt[:], raw_dt[:], 0.0, dt[:], ALU.max, ALU.add))
            link(v.tensor_tensor(mask[:], dt[:], rate[:], ALU.mult))
            link(v.scalar_tensor_tensor(mask[:], mask[:], 1e18, rate[:], ALU.min, ALU.mult))
            v.tensor_tensor(mask[:], mask[:], over[:], ALU.add).then_inc(dt_step, 1)
            dve.wait_ge(pe_done, 5)
            v.tensor_copy(x_nat[:], bank[0][0:S, :].rearrange("p (h c) -> p h c", c=HP))
            v.tensor_copy(z_nat[:], bank[1][0:S, :].rearrange("p (h c) -> p h c", c=HP))
            v.tensor_copy(cb[:], bank[2][0:S, 0:S])
            v.tensor_copy(fc[:], bank[2][0:S, 128:128 + HEADS])
            link(v.tensor_copy(dA_t[:], bank[7][0:16, 0:S]))
            dve.sem_inc(dve_done, 1)
            v.tensor_tensor(xf[:], x_nat[:], wide(dt[:, 0:HEADS]), ALU.mult)
            v.tensor_tensor(xb[:], x_nat[:], wide(dt[:, HEADS:]), ALU.mult)
            v.tensor_tensor(y[:], x_nat[:], wide(fc[:]), ALU.mult)
            dve.wait_ge(pe_done, 6)
            for h in range(HEADS):
                v.tensor_tensor_scan(decay[:, 0, h, :], bank[3][0:S, h * S:(h + 1) * S], ident[0:S, 0:S], 0.0, ALU.mult, ALU.add)
                i = v.tensor_tensor_scan(decay[:, 1, h, :][:, ::-1], bank[4][0:S, h * S:(h + 1) * S][:, ::-1],
                                         ident[0:S, 0:S][:, ::-1], 0.0, ALU.mult, ALU.add)
            link(i)
            cb_all = cb[:].rearrange("p (a t) -> p a t", a=1).to_broadcast([S, HEADS, S])
            v.tensor_tensor(mf[:, :, 1:S + 1], decay[:, 0], cb_all, ALU.mult)
            v.tensor_tensor(mb[:, :, 0:S], decay[:, 1], cb_all, ALU.mult).then_inc(dve_done, 1)
            dve.wait_ge(pe_done, 7)
            link(v.tensor_tensor(y[:], bank[5][0:S, :].rearrange("p (h c) -> p h c", c=HP), y[:], ALU.add))
            link(v.tensor_tensor(y[:], y[:], z_nat[:], ALU.mult))
            link(v.tensor_tensor(y2[:], y[:], y[:], ALU.mult))
            link(v.tensor_reduce(ms[:], y2[:].rearrange("p h c -> p (h c)"), AXX, ALU.add))
            link(v.tensor_scalar(ms[:], ms[:], 1.0 / HID, EPS, ALU.mult, ALU.add))
            dve.sem_inc(dve_done, 1)
            dve.wait_ge(act_done, 6)
            inverse_root(nc, link, inv[:], root[:], ms[:], spare[:])
            v.tensor_scalar(y2[:], y[:], inv[:], None, ALU.mult).then_inc(dve_done, 1)
            dve.wait_ge(pe_done, 8)
            v.tensor_tensor(y_t[:], bank[0][:, 0:KC * S].rearrange("p (k s) -> p k s", s=S),
                            nw[:].rearrange("p (k a) -> p k a", a=1).to_broadcast([128, KC, S]), ALU.mult).then_inc(dve_done, 1)
            dve.wait_ge(pe_done, 9)
            v.tensor_copy(mixed[:], bank[1][0:HP, :].rearrange("p (h s) -> p h s", s=S)).then_inc(dve_done, 1)
            dve.wait_ge(pe_done, 10)
            v.tensor_copy(m["proj"][:].rearrange("p k d -> p (k d)"), bank[3][:, :])


def gather_out(nc, m, scratch, out_b, out):
    with ExitStack() as c:
        sem = lambda n: c.enter_context(nc.semaphore(n + "_o"))
        sb = lambda n, s: c.enter_context(nc.sbuf_tensor(n + "_o", s, F32))
        w_loaded = [sem(f"w_loaded{k}") for k in range(2)]
        row_loaded, products, added, stored = sem("row_loaded"), sem("products"), sem("added"), sem("stored")
        weight = [sb(f"weight{k}", [128, GROUP, KC * T]) for k in range(2)]
        b_row = sb("b_row", [1, GROUP, D])
        bank = m["bank"]
        out_view = out.rearrange("(t p) d -> p t d", p=T)
        block = c.enter_context(nc.Block())

        @block.sync
        def _(sp):
            for q in range(GROUP):
                sp.dma_start(b_row[0:1, q, :], out_b.rearrange("(a d) -> a d", a=1)).then_inc(row_loaded, 16)

            def load(g, k):
                sp.dma_start(weight[k][:], scratch[bass.ds(g * GROUP, GROUP)].rearrange("t p c -> p t c")).then_inc(w_loaded[k], 16)

            load(0, 0)
            load(1, 1)
            with sp.Fori(0, GROUPS // 2 - 1) as i:
                for k in range(2):
                    sp.wait_ge(products, i * 2 + (k + 1))
                    load(i * 2 + (2 + k), k)

        @block.tensor
        def _(pe):
            pe.wait_ge(row_loaded, 16 * GROUP)

            def work(g, i, k, free):
                pe.wait_ge(w_loaded[k], (i + 1) * 16)
                if free is not None:
                    pe.wait_ge(added, free)
                nc.tensor.matmul(bank[k][0:T, 0:GD], m["ones_row"][0:1, 0:T], b_row[0:1].rearrange("a q d -> a (q d)"),
                                 start=True, stop=False, skip_group_check=True)
                for q in range(GROUP):
                    for r in range(KC):
                        t = nc.tensor.matmul(bank[k][0:T, q * D:(q + 1) * D], weight[k][:, q, r * T:(r + 1) * T],
                                             m["proj"][:, r, :], start=False, stop=(r == KC - 1), skip_group_check=True)
                t.then_inc(products, 1)
            work(0, 0, 0, None)
            work(1, 0, 1, None)
            with pe.Fori(1, GROUPS // 2) as i:
                for k in range(2):
                    work(i * 2 + k, i, k, i * 2 + (k - 1))

        @block.vector
        def _(dve):
            with dve.Fori(0, GROUPS // 2) as i:
                for k in range(2):
                    g = i * 2 + k
                    dve.wait_ge(products, g + 1)
                    here = m["stream"][:, bass.ds(g * GROUP, GROUP), :]
                    nc.vector.tensor_tensor(here, bank[k][0:T, 0:GD].rearrange("p (q d) -> p q d", d=D), here, ALU.add
                                            ).then_inc(added, 1)

        @block.scalar
        def _(act):
            with act.Fori(0, GROUPS) as g:
                act.wait_ge(added, g + 1)
                act.dma_start(out_view[:, bass.ds(g * GROUP, GROUP), :], m["stream"][:, bass.ds(g * GROUP, GROUP), :]
                              ).then_inc(stored, 16)
            act.wait_ge(stored, 16 * GROUPS)


NAMES = ['x', 'adj', 'L0_gnn_item_feat', 'L0_gnn_W_item', 'L0_gnn_b_item', 'L0_gnn_W_user', 'L0_gnn_b_user',
         'L0_ffn_W_ih', 'L0_ffn_W_hh', 'L0_ffn_b_ih', 'L0_ffn_b_hh', 'L0_ffn_W_lin', 'L0_ffn_b_lin', 'L0_ffn_fw_att',
         'L0_ffn_bw_att', 'L1_gnn_W', 'L1_ffn_W_fx', 'L1_ffn_b_fx', 'L1_ffn_W_x', 'L1_ffn_b_x', 'L1_ffn_W_slice',
         'L1_ffn_b_slice', 'L1_ffn_temperature', 'L1_ffn_hy_in_w', 'L1_ffn_hy_conv_w', 'L1_ffn_hy_conv_b',
         'L1_ffn_hy_dt_bias', 'L1_ffn_hy_A_log', 'L1_ffn_hy_D', 'L1_ffn_hy_fcD_w', 'L1_ffn_hy_norm_w',
         'L1_ffn_hy_out_w', 'L1_ffn_out_w', 'L1_ffn_out_b']


def build(nc, a, scratch, out):
    with ExitStack() as c:
        m = common(nc, c)
        setup(nc, m, a['L0_gnn_W_item'], a['L0_gnn_b_item'], a['L0_gnn_W_user'], a['L0_gnn_b_user'], a['L0_ffn_W_ih'],
              a['L0_ffn_W_hh'], a['L0_ffn_b_ih'], a['L0_ffn_b_hh'], a['L1_gnn_W'], a['x'], a['L0_gnn_item_feat'])
        norm_stats(nc, m, "_1")
        norm_transposed(nc, m, "_1")
        adjacency_pass(nc, m, a['adj'], True)
        norm_stats(nc, m, "_2")
        norm_transposed(nc, m, "_2")
        lstm(nc, m)
        mix(nc, m, a['L0_ffn_W_lin'], a['L0_ffn_b_lin'], a['L0_ffn_fw_att'], a['L0_ffn_bw_att'])
        norm_stats(nc, m, "_3")
        graph_features(nc, m)
        adjacency_pass(nc, m, a['adj'], False)
        norm_stats(nc, m, "_4")
        with ExitStack() as late:
            sb = lambda n, s: late.enter_context(nc.sbuf_tensor(n, s, F32))
            m["s_t"], m["w_fx"], m["fcd"] = sb("s_t", [HP, SL]), sb("w_fx", [D, HID]), sb("fcd", [128, KC, HEADS])
            m["w_mix"], m["w_out"] = sb("w_mix", [128, KC, HID]), sb("w_out", [HP, HEADS, D])
            m["w_logit"], m["b_logit"], m["b_fx"] = sb("w_logit", [D, HS]), sb("b_logit", [1, HS]), sb("b_fx", [1, HID])
            m["w_in"] = m["wide1"][:, 0:KC * 1168].rearrange("p (k c) -> p k c", c=1168)
            m["proj"] = sb("proj", [128, KC, D])
            slice_weights(nc, m, a['L1_ffn_W_fx'], a['L1_ffn_b_fx'], a['L1_ffn_W_x'], a['L1_ffn_b_x'], a['L1_ffn_W_slice'],
                          a['L1_ffn_b_slice'], a['L1_ffn_temperature'], a['L1_ffn_hy_fcD_w'], a['L1_ffn_hy_in_w'],
                          a['L1_ffn_hy_out_w'], a['L1_ffn_out_w'])
            slice_tokens(nc, m, scratch)
            mixer(nc, m, a['L1_ffn_hy_conv_w'], a['L1_ffn_hy_conv_b'], a['L1_ffn_hy_dt_bias'], a['L1_ffn_hy_A_log'],
                  a['L1_ffn_hy_D'], a['L1_ffn_hy_norm_w'])
            gather_out(nc, m, scratch, a['L1_ffn_out_b'], out)


def kernel(**inputs):
    from concourse import bacc
    from concourse.bass_utils import run_bass_kernel_spmd

    nc = bacc.Bacc("TRN2", target_bir_lowering=False, num_devices=1)
    arrays, aps = {}, {}
    for name in NAMES:
        a = np.ascontiguousarray(inputs[name])
        arrays[f"in_{name}_dram"] = a
        aps[name] = nc.dram_tensor(f"in_{name}_dram", a.shape, mybir.dt.from_np(a.dtype), kind="ExternalInput").ap()
    scratch = nc.dram_tensor("slice_weights_dram", (TILES, 128, KC * T), F32, kind="Internal").ap()
    out = nc.dram_tensor("out_0_dram", (N, D), F32, kind="ExternalOutput").ap()
    build(nc, aps, scratch, out)
    r = run_bass_kernel_spmd(nc, [arrays], core_ids=[0])
    return r.results[0]["out_0_dram"]
```

```python
from contextlib import ExitStack

import numpy as np

import concourse.bass as bass
from concourse import mybir

F32 = mybir.dt.float32
F32R = mybir.dt.float32r
I32 = mybir.dt.int32
ALU = mybir.AluOpType
ACT = mybir.ActivationFunctionType
AXX = mybir.AxisListType.X

N, D = 10000, 128
T = 125
TILES = N // T
GROUP = 4
GROUPS = TILES // GROUP
GT = GROUP * T
GD = GROUP * D
EPS = 1e-5
DE = D + 1

SLOTS = 4
PB = 4
PCOLS = PB * T
PANELS = TILES // PB
STAGES = 4
AHEAD = 3


def chain(engine, sem, start=0):
    count = [start]

    def link(instruction):
        count[0] = count[0] + 1
        instruction.then_inc(sem, 1)
        engine.wait_ge(sem, count[0])
    return link


def inverse_root(nc, link, out, root, value, spare):
    link(nc.vector.reciprocal(out, root))
    link(nc.vector.tensor_tensor(spare, value, out, ALU.mult))
    link(nc.vector.tensor_tensor(spare, spare, out, ALU.mult))
    link(nc.vector.tensor_scalar(spare, spare, -0.5, 1.5, ALU.mult, ALU.add))
    link(nc.vector.tensor_tensor(out, out, spare, ALU.mult))


def setup(nc, m, W_item, b_item, W_user, W_ih, W_hh, b_ih, b_hh, gnn_w, x, item):
    with ExitStack() as c:
        sem = lambda n: c.enter_context(nc.semaphore(n))
        sb = lambda n, s: c.enter_context(nc.sbuf_tensor(n, s, F32))
        x_loaded, w_loaded, rows_loaded = sem("x_loaded"), sem("w_loaded"), sem("rows_loaded")
        item_loaded = [sem(f"item_loaded{k}") for k in range(2)]
        id_zero, id_done, ones_set = sem("id_zero"), sem("id_done"), sem("ones_set")
        w_turned, w_kept = sem("w_turned"), sem("w_kept")
        item_turned, item_staged, item_done, item_high, item_kept = (
            sem("item_turned"), sem("item_staged"), sem("item_done"), sem("item_high"), sem("item_kept"))
        wraw = sb("wraw", [128, 10, 128])
        item_in = [sb(f"item_in{k}", [T, GROUP, D]) for k in range(2)]
        item_t = [sb(f"item_t{k}", [D, GT]) for k in range(2)]
        brow = sb("brow", [1, GROUP, D])
        b2 = sb("b2", [128, 4])
        bank = m["bank"]
        x_view = x.rearrange("(t p) d -> p t d", p=T)
        item_view = item.rearrange("(t p) d -> p t d", p=T)
        row = lambda v: v.rearrange("(a d) -> a d", a=1)
        block = c.enter_context(nc.Block())

        @block.sync
        def _(sp):
            sp.dma_start(wraw[:, 0, :], W_item).then_inc(w_loaded, 16)
            sp.dma_start(wraw[:, 1, :], W_user).then_inc(w_loaded, 16)
            sp.dma_start(wraw[:, 2:6, :], W_ih.rearrange("(k p) d -> p k d", p=128)).then_inc(w_loaded, 16)
            sp.dma_start(wraw[:, 6:10, :], W_hh.rearrange("(k p) d -> p k d", p=128)).then_inc(w_loaded, 16)
            for q in range(GROUP):
                sp.dma_start(brow[0:1, q, :], row(b_item)).then_inc(rows_loaded, 16)
            sp.dma_start(m["gnn_w"][:], gnn_w).then_inc(rows_loaded, 16)
            sp.dma_start(m["gate_b"][:], b_ih.rearrange("(k p) -> p k", p=128), allow_slow_non_contiguous=True).then_inc(rows_loaded, 16)
            sp.dma_start(b2[:], b_hh.rearrange("(k p) -> p k", p=128), allow_slow_non_contiguous=True).then_inc(rows_loaded, 16)
            for k in range(2):
                sp.dma_start(item_in[k][:], item_view[:, k * GROUP:(k + 1) * GROUP, :]).then_inc(item_loaded[k], 16)
            for k in range(4):
                sp.dma_start(m["stream"][:, k * 20:(k + 1) * 20, :],
                             x_view[:, k * 20:(k + 1) * 20, :]).then_inc(x_loaded, 16)
            with sp.Fori(0, GROUPS // 2 - 1) as i:
                for k in range(2):
                    sp.wait_ge(item_turned, i * 2 + (k + 1))
                    sp.dma_start(item_in[k][:], item_view[:, bass.ds((i * 2 + 2 + k) * GROUP, GROUP), :]
                                 ).then_inc(item_loaded[k], 16)
            sp.wait_ge(x_loaded, 64)
            sp.wait_ge(rows_loaded, 16 * 7)

        @block.gpsimd
        def _(pool):
            nc.gpsimd.memset(m["ident"][:], 0.0).then_inc(id_zero, 1)
            pool.wait_ge(id_zero, 1)
            nc.gpsimd.affine_select(out=m["ident"][:], in_=m["ident"][:], compare_op=ALU.not_equal, fill=1.0,
                                    base=0, pattern=[[-1, 128]], channel_multiplier=1).then_inc(id_done, 1)

        @block.tensor
        def _(pe):
            pe.wait_ge(id_done, 1)
            pe.wait_ge(w_loaded, 64)
            for k in range(10):
                nc.tensor.transpose(bank[k // 4][:, (k % 4) * 128:(k % 4 + 1) * 128], wraw[:, k, :],
                                    m["ident"][:]).then_inc(w_turned, 1)
            pe.wait_ge(w_kept, 3)
            pe.wait_ge(rows_loaded, 16 * 7)
            pe.wait_ge(ones_set, 1)

            def turn(k, turns):
                pe.wait_ge(item_loaded[k], (turns + 1) * 16)
                for q in range(GROUP):
                    t = nc.tensor.transpose(bank[k][:, q * T:(q + 1) * T], item_in[k][:, q, :],
                                            m["ident"][0:T, 0:T])
                t.then_inc(item_turned, 1)

            def multiply(k, turns):
                pe.wait_ge(item_kept, turns * 2 + (k + 1))
                nc.tensor.matmul(bank[2 + k][0:T, 0:GD], m["ones_row"][0:1, 0:T],
                                 brow[0:1].rearrange("a q d -> a (q d)"),
                                 start=True, stop=False, skip_group_check=True)
                pe.wait_ge(item_staged, turns * 2 + (k + 1))
                for q in range(GROUP):
                    t = nc.tensor.matmul(bank[2 + k][0:T, q * D:(q + 1) * D], item_t[k][:, q * T:(q + 1) * T],
                                         m["w_item"][:], start=False, stop=(q == GROUP - 1),
                                         skip_group_check=True)
                t.then_inc(item_done, 1)

            turn(0, 0)
            with pe.Fori(0, GROUPS // 2 - 1) as i:
                turn(1, i)
                multiply(0, i)
                turn(0, i + 1)
                multiply(1, i)
            last = GROUPS // 2 - 1
            turn(1, last)
            multiply(0, last)
            multiply(1, last)

        @block.scalar
        def _(act):
            with act.Fori(0, GROUPS // 2) as i:
                for k in range(2):
                    act.wait_ge(item_turned, i * 2 + (k + 1))
                    nc.scalar.activation(item_t[k][:], bank[k][:, 0:GT], ACT.Copy).then_inc(item_staged, 1)

        @block.vector
        def _(dve):
            nc.vector.memset(m["ones_row"][:], 1.0).then_inc(ones_set, 1)
            nc.vector.memset(m["zero_row"][:], 0.0)
            dve.wait_ge(w_turned, 10)
            nc.vector.tensor_copy(m["w_item"][:], bank[0][:, 0:128]).then_inc(w_kept, 1)
            nc.vector.tensor_copy(m["w_user"][:], bank[0][:, 128:256])
            nc.vector.tensor_copy(m["w_ih"][:, 0:256], bank[0][:, 256:512])
            nc.vector.tensor_copy(m["w_ih"][:, 256:512], bank[1][:, 0:256])
            nc.vector.tensor_copy(m["w_hh"][:, 0:256], bank[1][:, 256:512]).then_inc(w_kept, 1)
            dve.sem_inc(item_kept, 2)
            nc.vector.tensor_copy(m["w_hh"][:, 256:512], bank[2][:, 0:256]).then_inc(w_kept, 1)
            dve.wait_ge(rows_loaded, 16 * 7)
            nc.vector.tensor_tensor(m["gate_b"][:], m["gate_b"][:], b2[:], ALU.add)
            dve.wait_ge(x_loaded, 64)
            with dve.Fori(0, GROUPS // 2) as i:
                for k in range(2):
                    here = bass.ds((i * 2 + k) * GROUP, GROUP)
                    sums = bank[2 + k][0:T, 0:GD].rearrange("p (q d) -> p q d", d=D)
                    dve.wait_ge(item_done, i * 2 + (k + 1))
                    nc.vector.tensor_copy(m["feats_high"][:, here, :], sums).then_inc(item_high, 1)
                    dve.wait_ge(item_high, i * 2 + (k + 1))
                    nc.vector.tensor_tensor(m["feats_low"][:, here, :], sums, m["feats_high"][:, here, :].bitcast(F32),
                                            ALU.subtract).then_inc(item_kept, 1)
                    row_statistics(nc, m, (i * 2 + k) * GROUP)


def row_statistics(nc, m, first, count=GROUP):
    for q in range(count):
        i = nc.vector.bn_stats(m["parts"][:, bass.ds(first + q, 1), :], m["stream"][:, bass.ds(first + q, 1), :])
    return i


def norm_stats(nc, m, tag):
    with ExitStack() as c:
        sem = lambda n: c.enter_context(nc.semaphore(n + tag))
        sb = lambda n, s: c.enter_context(nc.sbuf_tensor(n + tag, s, F32))
        var_done, root_done, step = sem("var_done"), sem("root_done"), sem("nstep")
        var, root, corr = sb("var", [T, TILES]), sb("root", [T, TILES]), sb("corr", [T, TILES])
        parts = m["parts"]
        block = c.enter_context(nc.Block())

        @block.vector
        def _(dve):
            link = chain(dve, step)
            link(nc.vector.tensor_tensor(corr[:], parts[:, :, 1], parts[:, :, 4], ALU.subtract))
            link(nc.vector.tensor_tensor(root[:], corr[:], corr[:], ALU.mult))
            link(nc.vector.tensor_tensor(m["mean"][:], parts[:, :, 1], parts[:, :, 4], ALU.add))
            link(nc.vector.tensor_scalar(m["mean"][:], m["mean"][:], 0.5, None, ALU.mult))
            link(nc.vector.tensor_tensor(var[:], parts[:, :, 2], parts[:, :, 5], ALU.add))
            link(nc.vector.tensor_scalar(var[:], var[:], 1.0 / D, EPS, ALU.mult, ALU.add))
            nc.vector.scalar_tensor_tensor(var[:], root[:], 0.25, var[:], ALU.mult, ALU.add).then_inc(var_done, 1)
            dve.wait_ge(root_done, 1)
            inverse_root(nc, link, m["rstd"][:], root[:], var[:], corr[:])

        @block.scalar
        def _(act):
            act.wait_ge(var_done, 1)
            nc.scalar.activation(root[:], var[:], ACT.Sqrt).then_inc(root_done, 1)


def norm_transposed(nc, m, tag):
    with ExitStack() as c:
        sem = lambda n: c.enter_context(nc.semaphore(n + tag))
        rows_ready, turned, kept = sem("rows_ready"), sem("turned"), sem("kept")
        rows = [c.enter_context(nc.sbuf_tensor(f"rows{k}{tag}", [T, GROUP, D], F32)) for k in range(2)]
        bank = m["bank"]
        block = c.enter_context(nc.Block())

        def normalise(dve, g, k):
            for q in range(GROUP):
                i = nc.vector.tensor_scalar(rows[k][:, q, :], m["stream"][:, bass.ds(g * GROUP + q, 1), :],
                                            m["mean"][:, bass.ds(g * GROUP + q, 1)],
                                            m["rstd"][:, bass.ds(g * GROUP + q, 1)], ALU.subtract, ALU.mult)
            i.then_inc(rows_ready, 1)

        @block.vector
        def _(dve):
            for k in range(2):
                normalise(dve, k, k)
            with dve.Fori(1, GROUPS // 2) as i:
                for k in range(2):
                    dve.wait_ge(turned, i * 2 + (k - 1))
                    normalise(dve, i * 2 + k, k)

        @block.tensor
        def _(pe):
            def turn(n, k):
                pe.wait_ge(rows_ready, n + 1)
                for q in range(GROUP):
                    t = nc.tensor.transpose(bank[k][:, q * T:(q + 1) * T], rows[k][:, q, :], m["ident"][0:T, 0:T])
                t.then_inc(turned, 1)
            for k in range(2):
                turn(k, k)
            with pe.Fori(1, GROUPS // 2) as i:
                for k in range(2):
                    pe.wait_ge(kept, i * 2 + (k - 1))
                    turn(i * 2 + k, k)

        @block.scalar
        def _(act):
            with act.Fori(0, GROUPS // 2) as i:
                for k in range(2):
                    act.wait_ge(turned, i * 2 + (k + 1))
                    nc.scalar.activation(m["wide2"][:, bass.ds((i * 2 + k) * GT, GT)], bank[k][:, 0:GT],
                                         ACT.Copy).then_inc(kept, 1)


def adjacency_pass(nc, m, adj, W_user_bias, first):
    tag = "_a" if first else "_b"
    with ExitStack() as c:
        sem = lambda n: c.enter_context(nc.semaphore(n + tag))
        sb = lambda n, s, d=F32: c.enter_context(nc.sbuf_tensor(n + tag, s, d))
        panel_loaded = [sem(f"panel_loaded{k}") for k in range(SLOTS)]
        panel_read, turned, high_staged, low_staged = sem("panel_read"), sem("turned"), sem("high_staged"), sem("low_staged")
        head_done, head_kept, body_done, body_taken = sem("head_done"), sem("head_kept"), sem("body_done"), sem("body_taken")
        relu_done, back_turned, added = sem("relu_done"), sem("back_turned"), sem("added")
        rows_ready, rows_turned, user_staged = sem("rows_ready"), sem("rows_turned"), sem("user_staged")
        act_summed, dve_summed, degree_done, bias_loaded = (
            sem("act_summed"), sem("dve_summed"), sem("degree_done"), sem("bias_loaded"))
        panel = [sb(f"panel{k}", [T, GROUP, PCOLS]) for k in range(SLOTS)]
        high = [sb(f"high{k}", [T, GT], F32R) for k in range(STAGES)]
        low = [sb(f"low{k}", [T, GT], F32R) for k in range(STAGES)]
        head_sums, total, relu_t = sb("head_sums", [D, GT]), sb("total", [D, GT]), sb("relu_t", [D, GT])
        if first:
            rows, user_t, bias = sb("rows", [T, GROUP, D]), sb("user_t", [D, GT]), sb("bias", [D, 1])
            shares, unread = sb("shares", [T, GROUP, PANELS]), [sb(f"unread{q}", [T, PCOLS]) for q in range(2)]
        bank = m["bank"]
        body, head, scratch, back = bank[4], bank[5], bank[6], bank[7]
        rows_of = adj.rearrange("(t p) c -> p t c", p=T)
        feats_high, feats_low = m["feats_high"], m["feats_low"]
        HEAD = 2 * PB
        LAST = TILES - HEAD - 1
        SPARE = HEAD // PB + 1
        NORM, TURN_ROWS, USER = 8, 14, 20
        block = c.enter_context(nc.Block())


        @block.sync
        def _(sp):
            if first:
                sp.dma_start(bias[:], W_user_bias.rearrange("(d a) -> d a", a=1), allow_slow_non_contiguous=True
                             ).then_inc(bias_loaded, 16)

            def load(g, p):
                sp.dma_start(panel[p % SLOTS][:], rows_of[:, bass.ds(g * GROUP, GROUP), p * PCOLS:(p + 1) * PCOLS]
                             ).then_inc(panel_loaded[p % SLOTS], 16)

            def slot_free(g, p):
                for reader in (panel_read, act_summed, dve_summed) if first else (panel_read,):
                    sp.wait_ge(reader, g * PANELS + (p + 1))

            for p in range(SLOTS):
                load(0, p)
            with sp.Fori(0, GROUPS - 1) as g:
                for p in range(PANELS):
                    slot_free(g, p)
                    if p < PANELS - SLOTS:
                        load(g, p + SLOTS)
                    else:
                        load(g + 1, p + SLOTS - PANELS)
            for p in range(PANELS - SLOTS):
                slot_free(GROUPS - 1, p)
                load(GROUPS - 1, p + SLOTS)
            for p in range(SPARE):
                slot_free(GROUPS - 1, PANELS - SLOTS + p)
                load(0, p)
            for s in range(SLOTS):
                sp.wait_ge(panel_loaded[s], 16 * (GROUPS * PANELS // SLOTS + (s < SPARE)))

        def panel_ready(engine, g, p):
            engine.wait_ge(panel_loaded[p % SLOTS], (g * (PANELS // SLOTS) + (p // SLOTS + 1)) * 16)

        @block.tensor
        def _(pe):
            def transposes(g, bb):
                b = bb % TILES
                if b % PB == 0:
                    panel_ready(pe, g, bb // PB)
                for q in range(GROUP):
                    t = nc.tensor.transpose(bank[b % STAGES][0:T, q * T:(q + 1) * T],
                                            panel[b // PB % SLOTS][:, q, b % PB * T:(b % PB + 1) * T], m["ident"][0:T, 0:T])
                t.then_inc(turned, 1)

            def products(n, b, sums, start, stop, signal):
                pe.wait_ge(high_staged, n + 1)
                nc.tensor.matmul(sums[:, 0:GT], feats_high[:, b, :], high[b % STAGES][:], start=start, stop=False,
                                 skip_group_check=True)
                i = nc.tensor.matmul(sums[:, 0:GT], feats_low[:, b, :], high[b % STAGES][:], start=False, stop=False,
                                     skip_group_check=True)
                if (b + AHEAD) % PB == PB - 1:
                    i.then_inc(panel_read, 1)
                pe.wait_ge(low_staged, n + 1)
                i = nc.tensor.matmul(sums[:, 0:GT], feats_high[:, b, :], low[b % STAGES][:], start=False, stop=stop,
                                     skip_group_check=True)
                if signal is not None:
                    i.then_inc(signal, 1)

            for b in range(AHEAD):
                transposes(0, b)
            for b in range(HEAD):
                transposes(0, b + AHEAD)
                products(b, b, head, b == 0, b == HEAD - 1, head_done if b == HEAD - 1 else None)
            with pe.Fori(0, GROUPS) as g:
                for b in range(TILES):
                    transposes(g, b + HEAD + AHEAD)
                    if b == 0:
                        pe.wait_ge(body_taken, g + 1)
                    if b == LAST + 1:
                        pe.wait_ge(head_kept, g + 1)
                    at = (b + HEAD) % TILES
                    n = g * TILES + (b + HEAD)
                    if b <= LAST:
                        products(n, at, body, b == 0, b == LAST, body_done if b == LAST else None)
                    else:
                        products(n, at, head, at == 0, at == HEAD - 1, head_done if at == HEAD - 1 else None)
                    if first and b == TURN_ROWS:
                        pe.wait_ge(rows_ready, g + 1)
                        for q in range(GROUP):
                            t = nc.tensor.transpose(scratch[:, q * T:(q + 1) * T], rows[:, q, :], m["ident"][0:T, 0:T])
                        t.then_inc(rows_turned, 1)
                    if first and b == USER:
                        pe.wait_ge(user_staged, g + 1)
                        nc.tensor.matmul(body[:, 0:GT], m["w_user"][:], user_t[:], start=False, stop=False,
                                         skip_group_check=True)
                    if b == LAST + 3:
                        pe.wait_ge(relu_done, g + 1)
                        for q in range(GROUP):
                            t = nc.tensor.transpose(back[0:T, q * D:(q + 1) * D], relu_t[:, q * T:(q + 1) * T], m["ident"][:])
                        t.then_inc(back_turned, 1)

        @block.scalar
        def _(act):
            def stage(g, b):
                act.wait_ge(turned, g * TILES + (b + 1))
                nc.scalar.activation(high[b % STAGES][:], bank[b % STAGES][0:T, 0:GT], ACT.Copy).then_inc(high_staged, 1)
                if first and b % PB in (0, 2):
                    q, p = b % PB // 2, b // PB
                    if not (isinstance(g, int) and p == 0):
                        act.wait_ge(act_summed, g * PANELS + p)
                    i = nc.scalar.activation(unread[q][:], panel[p % SLOTS][:, q, :], ACT.Copy,
                                             accum_out=shares[:, q, p:p + 1])
                    if q == 1:
                        i.then_inc(act_summed, 1)

            if first:
                act.wait_ge(bias_loaded, 16)
            for b in range(HEAD):
                stage(0, b)
            with act.Fori(0, GROUPS) as g:
                for b in range(TILES):
                    if first and b == LAST + 1:
                        act.wait_ge(degree_done, g + 1)
                    stage(g + 1 if b > LAST else g, (b + HEAD) % TILES)
                    if first and b == TURN_ROWS + 1:
                        act.wait_ge(rows_turned, g + 1)
                        nc.scalar.activation(user_t[:], scratch[:, 0:GT], ACT.Copy).then_inc(user_staged, 1)
                    if b == LAST + 3:
                        act.wait_ge(body_taken, g + 2)
                        if first:
                            nc.scalar.activation(relu_t[:], total[:], ACT.Relu, bias=bias[:]).then_inc(relu_done, 1)
                        else:
                            nc.scalar.activation(relu_t[:], total[:], ACT.Relu).then_inc(relu_done, 1)

        @block.vector
        def _(dve):
            def stage(n, b):
                dve.wait_ge(high_staged, n + 1)
                nc.vector.tensor_tensor(low[b % STAGES][:], bank[b % STAGES][0:T, 0:GT], high[b % STAGES][:].bitcast(F32),
                                        ALU.subtract).then_inc(low_staged, 1)
                if first and b % PB in (1, 3):
                    q, p = 2 + b % PB // 2, b // PB
                    i = nc.vector.tensor_reduce(shares[:, q, p:p + 1], panel[p % SLOTS][:, q, :], AXX, ALU.add)
                    if q == 3:
                        i.then_inc(dve_summed, 1)

            dve.sem_inc(body_taken, 1)
            for b in range(HEAD):
                stage(b, b)
            with dve.Fori(0, GROUPS) as g:
                for b in range(TILES):
                    stage(g * TILES + (b + HEAD), (b + HEAD) % TILES)
                    if first and b == LAST:
                        dve.wait_ge(act_summed, (g + 1) * PANELS)
                        dve.wait_ge(dve_summed, (g + 1) * PANELS)
                        nc.vector.tensor_reduce(m["degree"][:, bass.ds(g * GROUP, GROUP)], shares[:], AXX, ALU.add
                                                ).then_inc(degree_done, 1)
                    if b == 1:
                        dve.wait_ge(head_done, g + 1)
                        nc.vector.tensor_copy(head_sums[:], head[:, 0:GT]).then_inc(head_kept, 1)
                    if first and b == NORM:
                        for q in range(GROUP):
                            i = nc.vector.tensor_scalar(rows[:, q, :], m["stream"][:, bass.ds(g * GROUP + q, 1), :],
                                                        m["mean"][:, bass.ds(g * GROUP + q, 1)],
                                                        m["rstd"][:, bass.ds(g * GROUP + q, 1)], ALU.subtract, ALU.mult)
                        i.then_inc(rows_ready, 1)
                    if b == LAST + 2:
                        dve.wait_ge(body_done, g + 1)
                        dve.wait_ge(head_kept, g + 1)
                        nc.vector.tensor_tensor(total[:], body[:, 0:GT], head_sums[:], ALU.add).then_inc(body_taken, 1)
                    if b == LAST + 4:
                        dve.wait_ge(back_turned, g + 1)
                        here = m["stream"][:, bass.ds(g * GROUP, GROUP), :]
                        if first:
                            i = nc.vector.tensor_tensor(here, back[0:T, 0:GD].rearrange("p (q d) -> p q d", d=D), here, ALU.add)
                        else:
                            for q in range(GROUP):
                                one = m["stream"][:, bass.ds(g * GROUP + q, 1), :].rearrange("p q d -> p (q d)")
                                i = nc.vector.scalar_tensor_tensor(one, back[0:T, q * D:(q + 1) * D],
                                                                   m["dinv"][:, bass.ds(g * GROUP + q, 1)], one,
                                                                   ALU.mult, ALU.add)
                        i.then_inc(added, 1)
                    if LAST + 4 < b <= LAST + 4 + GROUP:
                        if b == LAST + 5:
                            dve.wait_ge(added, g + 1)
                        row_statistics(nc, m, g * GROUP + (b - LAST - 5), 1)


def common(nc, c):
    sb = lambda n, s: c.enter_context(nc.sbuf_tensor(n, s, F32))
    return {
        "bank": [c.enter_context(nc.psum_tensor(f"bank{k}", [128, 512], F32)) for k in range(8)],
        "ident": sb("ident", [128, 128]),
        "stream": sb("stream", [T, TILES, D]),
        "parts": sb("parts", [T, TILES, 6]), "mean": sb("mean", [T, TILES]), "rstd": sb("rstd", [T, TILES]),
        "degree": sb("degree", [T, TILES]), "dinv": sb("dinv", [T, TILES]),
        "w_item": sb("w_item", [D, D]), "w_user": sb("w_user", [D, D]), "gnn_w": sb("gnn_w", [D, D]),
        "w_ih": sb("w_ih", [D, 512]), "w_hh": sb("w_hh", [D, 512]), "gate_b": sb("gate_b", [D, 4]),
        "ones_row": sb("ones_row", [1, 128]), "zero_row": sb("zero_row", [1, 2, DE]),
    }


CHUNKS = 200
STEPS = N // CHUNKS
LANES = [(0, CHUNKS // 2), (CHUNKS // 2, CHUNKS)]
TOLERANCE = 1e-6
SURE = 2


def lstm(nc, m):
    with ExitStack() as c:
        sem = lambda n: c.enter_context(nc.semaphore(n + "_l"))
        sb = lambda n, s, d=F32: c.enter_context(nc.sbuf_tensor(n + "_l", s, d))
        prepared, sweep_open, compared = sem("prepared"), sem("sweep_open"), sem("compared")
        gates_summed = [sem(f"gates_summed{k}") for k in range(2)]
        gates_read = [sem(f"gates_read{k}") for k in range(2)]
        gates_done = [sem(f"gates_done{k}") for k in range(2)]
        parts_done = [sem(f"parts_done{k}") for k in range(2)]
        cell_done = [sem(f"cell_done{k}") for k in range(2)]
        tanh_done = [sem(f"tanh_done{k}") for k in range(2)]
        u_done = [sem(f"u_done{k}") for k in range(2)]
        marked, counted, flag_set = sem("marked"), sem("counted"), sem("flag_set")
        W = [hi - lo for lo, hi in LANES]
        pre = [sb(f"pre{k}", [D, 4, W[k]]) for k in range(2)]
        gate = [sb(f"gate{k}", [D, 4, W[k]]) for k in range(2)]
        keep = [sb(f"keep{k}", [D, W[k]]) for k in range(2)]
        put = [sb(f"put{k}", [D, W[k]]) for k in range(2)]
        tc = [sb(f"tc{k}", [D, W[k]]) for k in range(2)]
        cell = sb("cell", [D, CHUNKS])
        cell_start, u_start = sb("cell_start", [D, CHUNKS]), sb("u_start", [D, CHUNKS])
        near = sb("near", [D, 2, CHUNKS - 1])
        ones_col, total, flag = sb("ones_col", [D, 1]), sb("total", [1, 1]), sb("flag", [1, 1], I32)
        sums = [[m["bank"][0], m["bank"][1]], [m["bank"][2], m["bank"][3]]]
        tally = m["bank"][4]
        inputs = m["wide2"][:, 0:N].rearrange("p (c l) -> p c l", l=STEPS)
        u_before = m["wide1"][:, 0:N].rearrange("p (c l) -> p c l", l=STEPS)
        u_now = m["wide1"][:, 1:N + 1].rearrange("p (c l) -> p c l", l=STEPS)
        I, F, G, O = range(4)
        block = c.enter_context(nc.Block())

        @block.tensor
        def _(pe):
            def sweep(s):
                with pe.Fori(0, STEPS // 2) as pair:
                    for odd in range(2):
                        t = pair * 2 + odd
                        for k, (lo, hi) in enumerate(LANES):
                            bank = sums[k][odd][:, 0:4 * W[k]].rearrange("p (g c) -> p g c", g=4)
                            for g in range(4):
                                nc.tensor.matmul(bank[:, g, :], m["w_ih"][:, g * D:(g + 1) * D],
                                                 inputs[:, lo:hi, bass.ds(t, 1)],
                                                 start=(g == 0), stop=False, skip_group_check=True)
                            pe.wait_ge(u_done[k], s * (STEPS + 1) + t + 1)
                            for g in range(4):
                                i = nc.tensor.matmul(bank[:, g, :], m["w_hh"][:, g * D:(g + 1) * D],
                                                     u_before[:, lo:hi, bass.ds(t, 1)],
                                                     start=False, stop=(g == 3), skip_group_check=True)
                            i.then_inc(gates_summed[k], 1)
                pe.wait_ge(marked, s + 1)
                nc.tensor.matmul(tally[0:1, 0:2 * (CHUNKS - 1)], ones_col[:], near[:].rearrange("p a c -> p (a c)"),
                                 start=True, stop=True).then_inc(counted, 1)

            pe.wait_ge(prepared, 1)
            with pe.Fori(0, SURE) as s:
                sweep(s)
            pe.wait_ge(flag_set, 1)
            unsettled = pe.value_load(flag[0:1, 0:1])
            with pe.If(unsettled > 0):
                sweep(SURE)
            pe.wait_ge(flag_set, 2)
            still_unsettled = pe.value_load(flag[0:1, 0:1])
            with pe.If(still_unsettled > 0):
                with pe.Fori(SURE + 1, CHUNKS) as s:
                    sweep(s)

        @block.scalar
        def _(act):
            def gates(k, n):
                act.wait_ge(gates_read[k], n + 1)
                nc.scalar.activation(gate[k][:], pre[k][:], ACT.Tanh).then_inc(gates_done[k], 1)

            def squash(k, n):
                lo, hi = LANES[k]
                act.wait_ge(cell_done[k], n + 1)
                nc.scalar.activation(tc[k][:], cell[:, lo:hi], ACT.Tanh, scale=0.5).then_inc(tanh_done[k], 1)

            def sweep(s):
                gates(0, s * STEPS)
                squash(0, s * STEPS)
                gates(1, s * STEPS)
                with act.Fori(1, STEPS) as t:
                    squash(1, s * STEPS + t - 1)
                    gates(0, s * STEPS + t)
                    squash(0, s * STEPS + t)
                    gates(1, s * STEPS + t)
                squash(1, s * STEPS + (STEPS - 1))

            with act.Fori(0, SURE) as s:
                sweep(s)
            act.wait_ge(flag_set, 1)
            unsettled = act.value_load(flag[0:1, 0:1])
            with act.If(unsettled > 0):
                sweep(SURE)
            act.wait_ge(flag_set, 2)
            still_unsettled = act.value_load(flag[0:1, 0:1])
            with act.If(still_unsettled > 0):
                with act.Fori(SURE + 1, CHUNKS) as s:
                    sweep(s)

        @block.vector
        def _(dve):
            for w, gain in ((m["w_ih"], 0.5), (m["w_hh"], 0.25)):
                nc.vector.tensor_scalar(w[:, 0:2 * D], w[:, 0:2 * D], gain, None, ALU.mult)
                nc.vector.tensor_scalar(w[:, 3 * D:4 * D], w[:, 3 * D:4 * D], gain, None, ALU.mult)
            nc.vector.tensor_scalar(m["w_hh"][:, 2 * D:3 * D], m["w_hh"][:, 2 * D:3 * D], 0.5, None, ALU.mult)
            nc.vector.tensor_scalar(m["gate_b"][:, 0:2], m["gate_b"][:, 0:2], 0.5, None, ALU.mult)
            nc.vector.tensor_scalar(m["gate_b"][:, 3:4], m["gate_b"][:, 3:4], 0.5, None, ALU.mult)
            nc.vector.memset(u_before[:, :, 0], 0.0)
            nc.vector.memset(cell_start[:], 0.0)
            nc.vector.memset(u_start[:], 0.0)
            nc.vector.memset(ones_col[:], 1.0).then_inc(prepared, 1)
            dve.wait_ge(prepared, 1)

            def take(k, n, odd):
                dve.wait_ge(gates_summed[k], n + 1)
                bank = sums[k][odd][:, 0:4 * W[k]].rearrange("p (g c) -> p g c", g=4)
                bias = m["gate_b"][:].rearrange("p (g a) -> p g a", a=1).to_broadcast([D, 4, W[k]])
                nc.vector.tensor_tensor(pre[k][:], bank, bias, ALU.add).then_inc(gates_read[k], 1)

            def update(k, n):
                lo, hi = LANES[k]
                dve.wait_ge(gates_done[k], n + 1)
                nc.vector.scalar_tensor_tensor(put[k][:], gate[k][:, I, :], 1.0, gate[k][:, G, :], ALU.add, ALU.mult)
                nc.vector.scalar_tensor_tensor(keep[k][:], gate[k][:, F, :], 1.0, cell[:, lo:hi], ALU.add, ALU.mult
                                               ).then_inc(parts_done[k], 1)
                dve.wait_ge(parts_done[k], n + 1)
                nc.vector.scalar_tensor_tensor(cell[:, lo:hi], keep[k][:], 0.5, put[k][:], ALU.mult, ALU.add
                                               ).then_inc(cell_done[k], 1)

            def emit(k, n, t):
                lo, hi = LANES[k]
                dve.wait_ge(tanh_done[k], n + 1)
                nc.vector.scalar_tensor_tensor(u_now[:, lo:hi, t] if isinstance(t, int) else u_now[:, lo:hi, bass.ds(t, 1)],
                                               gate[k][:, O, :], 1.0, tc[k][:], ALU.add, ALU.mult).then_inc(u_done[k], 1)

            def sweep(s):
                nc.vector.tensor_copy(cell[:], cell_start[:]).then_inc(sweep_open, 1)
                dve.wait_ge(sweep_open, s + 1)
                dve.sem_inc(u_done[0], 1)
                dve.sem_inc(u_done[1], 1)
                n = s * STEPS
                take(0, n, 0)
                update(0, n)
                take(1, n, 0)
                emit(0, n, 0)

                def step_of(t, odd):
                    n = s * STEPS + t
                    update(1, n - 1)
                    take(0, n, odd)
                    emit(1, n - 1, t - 1)
                    update(0, n)
                    take(1, n, odd)
                    emit(0, n, t)
                with dve.Fori(0, STEPS // 2 - 1) as pair:
                    step_of(pair * 2 + 1, 1)
                    step_of(pair * 2 + 2, 0)
                step_of(STEPS - 1, 1)
                n = s * STEPS + (STEPS - 1)
                update(1, n)
                emit(1, n, STEPS - 1)
                dve.wait_ge(u_done[1], n + s + 2)
                step = [0]

                def after(i):
                    step[0] = step[0] + 1
                    i.then_inc(compared, 1)
                    dve.wait_ge(compared, s * 8 + step[0])
                last = CHUNKS - 1
                after(nc.vector.tensor_tensor(near[:, 0, :], u_before[:, 1:CHUNKS, 0], u_start[:, 1:CHUNKS], ALU.subtract))
                after(nc.vector.tensor_tensor(near[:, 1, :], cell[:, 0:last], cell_start[:, 1:CHUNKS], ALU.subtract))
                after(nc.vector.tensor_tensor(near[:], near[:], near[:], ALU.mult))
                after(nc.vector.tensor_copy(u_start[:, 1:CHUNKS], u_before[:, 1:CHUNKS, 0]))
                after(nc.vector.tensor_copy(cell_start[:, 1:CHUNKS], cell[:, 0:last]))
                nc.vector.tensor_scalar(near[:], near[:], TOLERANCE * TOLERANCE, None, ALU.is_le).then_inc(marked, 1)
                dve.wait_ge(counted, s + 1)
                after(nc.vector.tensor_reduce(total[:], tally[0:1, 0:2 * last], AXX, ALU.add))
                after(nc.vector.tensor_scalar(total[:], total[:], -1.0, float(2 * last * D), ALU.mult, ALU.add))
                after(nc.vector.tensor_copy(flag[:], total[:]))

            with dve.Fori(0, SURE) as s:
                sweep(s)
            dve.sem_inc(flag_set, 1)
            unsettled = dve.value_load(flag[0:1, 0:1])
            with dve.If(unsettled > 0):
                sweep(SURE)
            dve.sem_inc(flag_set, 1)
            still_unsettled = dve.value_load(flag[0:1, 0:1])
            with dve.If(still_unsettled > 0):
                with dve.Fori(SURE + 1, CHUNKS) as s:
                    sweep(s)


def mix(nc, m, W_lin, b_lin, fw_att, bw_att):
    with ExitStack() as c:
        sem = lambda n: c.enter_context(nc.semaphore(n + "_m"))
        sb = lambda n, s: c.enter_context(nc.sbuf_tensor(n + "_m", s, F32))
        loaded, prepared, thr_made, step = sem("loaded"), sem("prepared"), sem("thr_made"), sem("step")
        logits, gated, scanned, summed = sem("logits"), sem("gated"), sem("scanned"), sem("summed")
        shifted, turned, added, total_known = sem("shifted"), sem("turned"), sem("added"), sem("total_known")
        w_lin, fw, bw, b_row = sb("w_lin", [D, 2]), sb("fw", [D, 1]), sb("bw", [D, 1]), sb("b_row", [1, 2])
        w_diff, thr = sb("w_diff", [D, 128]), sb("thr", [D, 1])
        k_inc, k_own, k_total = sb("k_inc", [D, 1]), sb("k_own", [D, 1]), sb("k_total", [D, 1])
        ones = sb("ones", [D, GT])
        own = [sb(f"own{k}", [D, GT]) for k in range(2)]
        inc = [sb(f"inc{k}", [D, GT]) for k in range(2)]
        part = [sb(f"part{k}", [D, GT]) for k in range(2)]
        moved = [sb(f"moved{k}", [D, GT]) for k in range(2)]
        bank = m["bank"]
        u = m["wide1"][:, 1:N + 1]
        block = c.enter_context(nc.Block())

        @block.sync
        def _(sp):
            sp.dma_start(w_lin[:], W_lin.rearrange("l d -> d l"), allow_slow_non_contiguous=True).then_inc(loaded, 16)
            sp.dma_start(fw[:], fw_att.rearrange("a d -> d a"), allow_slow_non_contiguous=True).then_inc(loaded, 16)
            sp.dma_start(bw[:], bw_att.rearrange("a d -> d a"), allow_slow_non_contiguous=True).then_inc(loaded, 16)
            sp.dma_start(b_row[:], b_lin.rearrange("(a l) -> a l", a=1)).then_inc(loaded, 16)

        @block.tensor
        def _(pe):
            pe.wait_ge(prepared, 2)
            nc.tensor.matmul(bank[2][:, 0:1], m["ones_row"][0:1, :], b_row[0:1, 0:1],
                             start=True, stop=True).then_inc(thr_made, 1)
            with pe.Fori(0, GROUPS // 2) as i:
                for k in range(2):
                    pe.wait_ge(gated, i * 2 + (k + 1))
                    nc.tensor.matmul(bank[k][:, 0:GT], w_diff[:], u[:, bass.ds((i * 2 + k) * GT, GT)],
                                     start=True, stop=True).then_inc(logits, 1)
            with pe.Fori(0, GROUPS // 2) as i:
                for k in range(2):
                    pe.wait_ge(shifted, i * 2 + (k + 1))
                    pe.wait_ge(added, i * 2 + (k + 1))
                    for q in range(GROUP):
                        t = nc.tensor.transpose(bank[3 + k][0:T, q * D:(q + 1) * D], moved[k][:, q * T:(q + 1) * T],
                                                m["ident"][:])
                    t.then_inc(turned, 1)

        @block.vector
        def _(dve):
            link = chain(dve, step)
            dve.wait_ge(loaded, 64)
            link(nc.vector.memset(ones[:], 1.0))
            link(nc.vector.tensor_tensor(w_lin[:, 0:1], w_lin[:, 1:2], w_lin[:, 0:1], ALU.subtract))
            nc.vector.tensor_scalar(w_diff[:], ones[:, 0:128], w_lin[:, 0:1], None, ALU.mult).then_inc(prepared, 1)
            link(nc.vector.tensor_tensor(b_row[0:1, 0:1], b_row[0:1, 0:1], b_row[0:1, 1:2], ALU.subtract))
            nc.vector.tensor_scalar(b_row[0:1, 0:1], b_row[0:1, 0:1], 2.0, None, ALU.mult).then_inc(prepared, 1)
            link(nc.vector.tensor_tensor(k_inc[:], fw[:], bw[:], ALU.subtract))
            nc.vector.tensor_scalar(k_inc[:], k_inc[:], 0.5, None, ALU.mult)
            nc.vector.tensor_scalar(k_own[:], fw[:], -0.5, None, ALU.mult)
            nc.vector.tensor_scalar(k_total[:], bw[:], 0.5, None, ALU.mult)
            nc.vector.memset(inc[1][:], 0.0)
            dve.wait_ge(thr_made, 1)
            link(nc.vector.tensor_copy(thr[:], bank[2][:, 0:1]))
            dve.sem_inc(gated, 2)
            dve.sem_inc(added, 2)
            with dve.Fori(0, GROUPS // 2) as i:
                for k in range(2):
                    n = i * 2 + k
                    here = u[:, bass.ds(n * GT, GT)]
                    dve.wait_ge(logits, n + 1)
                    nc.vector.scalar_tensor_tensor(own[k][:], bank[k][:, 0:GT], thr[:], here, ALU.is_gt, ALU.mult
                                                   ).then_inc(gated, 1)
                    dve.wait_ge(gated, n + 3)
                    nc.vector.tensor_tensor_scan(inc[k][:], ones[:], own[k][:], inc[1 - k][:, GT - 1:GT], ALU.mult, ALU.add
                                                 ).then_inc(scanned, 1)
                    dve.wait_ge(scanned, n + 1)
                    nc.vector.scalar_tensor_tensor(part[k][:], inc[k][:], k_inc[:], here, ALU.mult, ALU.add
                                                   ).then_inc(summed, 1)
                    dve.wait_ge(summed, 2 * n + 1)
                    nc.vector.scalar_tensor_tensor(here, own[k][:], k_own[:], part[k][:], ALU.mult, ALU.add
                                                   ).then_inc(summed, 1)
            nc.vector.tensor_tensor(k_total[:], k_total[:], inc[1][:, GT - 1:GT], ALU.mult).then_inc(total_known, 1)
            with dve.Fori(0, GROUPS // 2) as i:
                for k in range(2):
                    n = i * 2 + k
                    dve.wait_ge(turned, n + 1)
                    here = m["stream"][:, bass.ds(n * GROUP, GROUP), :]
                    nc.vector.tensor_tensor(here, bank[3 + k][0:T, 0:GD].rearrange("p (q d) -> p q d", d=D), here, ALU.add
                                            ).then_inc(added, 1)
                    dve.wait_ge(added, n + 3)
                    row_statistics(nc, m, n * GROUP)

        @block.scalar
        def _(act):
            act.wait_ge(total_known, 1)
            with act.Fori(0, GROUPS // 2) as i:
                for k in range(2):
                    n = i * 2 + k
                    act.wait_ge(added, n + 1)
                    nc.scalar.activation(moved[k][:], u[:, bass.ds(n * GT, GT)], ACT.Identity, bias=k_total[:]
                                         ).then_inc(shifted, 1)


def graph_features(nc, m):
    with ExitStack() as c:
        sem = lambda n: c.enter_context(nc.semaphore(n + "_f"))
        sb = lambda n, s: c.enter_context(nc.sbuf_tensor(n + "_f", s, F32))
        rooted, step, rows_ready, turned, kept, made, stored = (
            sem("rooted"), sem("step"), sem("rows_ready"), sem("turned"), sem("kept"), sem("made"), sem("stored"))
        rows = [sb(f"rows{k}", [T, GROUP, D]) for k in range(2)]
        norm_t = [sb(f"norm_t{k}", [D, GT]) for k in range(2)]
        root, spare = sb("root", [T, TILES]), sb("spare", [T, TILES])
        bank = m["bank"]
        feats = [sb(f"feats{k}", [T, GROUP, D]) for k in range(2)]
        scaled, high_made = sem("scaled"), sem("high_made")
        block = c.enter_context(nc.Block())

        @block.vector
        def _(dve):
            link = chain(dve, step)
            dve.wait_ge(rooted, 1)
            inverse_root(nc, link, m["dinv"][:], root[:], m["degree"][:], spare[:])

            def normalise(g, k):
                for q in range(GROUP):
                    i = nc.vector.tensor_scalar(rows[k][:, q, :], m["stream"][:, bass.ds(g * GROUP + q, 1), :],
                                                m["mean"][:, bass.ds(g * GROUP + q, 1)],
                                                m["rstd"][:, bass.ds(g * GROUP + q, 1)], ALU.subtract, ALU.mult)
                i.then_inc(rows_ready, 1)

            def scale_rows(g, k):
                dve.wait_ge(made, g + 1)
                scale = m["dinv"][:, bass.ds(g * GROUP, GROUP)].rearrange("p (q a) -> p q a", a=1).to_broadcast([T, GROUP, D])
                nc.vector.tensor_tensor(feats[k][:], bank[2 + k][0:T, 0:GD].rearrange("p (q d) -> p q d", d=D), scale, ALU.mult
                                        ).then_inc(scaled, 1)

            def store(g, k):
                here = bass.ds(g * GROUP, GROUP)
                dve.wait_ge(high_made, g + 1)
                nc.vector.tensor_tensor(m["feats_low"][:, here, :], feats[k][:], m["feats_high"][:, here, :].bitcast(F32),
                                        ALU.subtract).then_inc(stored, 1)

            normalise(0, 0)
            normalise(1, 1)
            with dve.Fori(0, GROUPS // 2 - 1) as i:
                for k in range(2):
                    scale_rows(i * 2 + k, k)
                    normalise(i * 2 + (2 + k), k)
                    store(i * 2 + k, k)
            for k in range(2):
                scale_rows(GROUPS - 2 + k, k)
                store(GROUPS - 2 + k, k)

        @block.tensor
        def _(pe):
            def turn(n, k):
                pe.wait_ge(rows_ready, n + 1)
                for q in range(GROUP):
                    t = nc.tensor.transpose(bank[k][:, q * T:(q + 1) * T], rows[k][:, q, :], m["ident"][0:T, 0:T])
                t.then_inc(turned, 1)

            def multiply(n, k, free):
                pe.wait_ge(kept, n + 1)
                if free is not None:
                    pe.wait_ge(scaled, free)
                for q in range(GROUP):
                    t = nc.tensor.matmul(bank[2 + k][0:T, q * D:(q + 1) * D], norm_t[k][:, q * T:(q + 1) * T], m["gnn_w"][:],
                                         start=(q == 0), stop=(q == GROUP - 1), skip_group_check=True)
                t.then_inc(made, 1)

            turn(0, 0)
            turn(1, 1)
            multiply(0, 0, None)
            with pe.Fori(0, GROUPS // 2 - 1) as i:
                turn(i * 2 + 2, 0)
                multiply(i * 2 + 1, 1, i * 2 + 1)
                turn(i * 2 + 3, 1)
                multiply(i * 2 + 2, 0, i * 2 + 1)
            multiply(GROUPS - 1, 1, GROUPS - 2)

        @block.scalar
        def _(act):
            nc.scalar.activation(root[:], m["degree"][:], ACT.Sqrt).then_inc(rooted, 1)

            def keep(n, k):
                act.wait_ge(turned, n + 1)
                nc.scalar.activation(norm_t[k][:], bank[k][:, 0:GT], ACT.Copy).then_inc(kept, 1)

            def round_half(n, k):
                act.wait_ge(scaled, n + 1)
                nc.scalar.activation(m["feats_high"][:, bass.ds(n * GROUP, GROUP), :], feats[k][:], ACT.Copy
                                     ).then_inc(high_made, 1)
            keep(0, 0)
            keep(1, 1)
            with act.Fori(0, GROUPS // 2 - 1) as i:
                for k in range(2):
                    round_half(i * 2 + k, k)
                    keep(i * 2 + (2 + k), k)
            for k in range(2):
                round_half(GROUPS - 2 + k, k)


HEADS, HP, SL = 8, 64, 64
HID = HEADS * HP
HS = HEADS * SL
KC = HID // 128


def slice_weights(nc, m, W_fx, b_fx, W_x, b_x, W_slice, b_slice, temperature, fcD_w, hy_in_w, hy_out_w, out_w):
    with ExitStack() as c:
        sem = lambda n: c.enter_context(nc.semaphore(n + "_w"))
        sb = lambda n, s: c.enter_context(nc.sbuf_tensor(n + "_w", s, F32))
        loaded, turned, kept, step, temp_ready, temp_made, products = (
            sem("loaded"), sem("turned"), sem("kept"), sem("step"), sem("temp_ready"), sem("temp_made"), sem("products"))
        in_raw, in_last = sb("in_raw", [128, 9, HID]), sb("in_last", [16, HID])
        out_raw, o_raw, fx_raw = sb("out_raw", [128, KC, HID]), sb("o_raw", [128, HID]), sb("fx_raw", [128, KC, D])
        fcd_raw, x_raw, s_raw, s_t = sb("fcd_raw", [HEADS, HID]), sb("x_raw", [HP, HEADS, D]), sb("s_raw", [SL, HP]), sb("s_t", [HP, SL])
        bx, t_row, t_wide, bs_row = sb("bx", [HP, HEADS]), sb("t_row", [1, HEADS]), sb("t_wide", [1, HS]), sb("bs_row", [1, HS])
        t_all = sb("t_all", [128, HS])
        bank = m["bank"]
        row = lambda v: v.rearrange("(a d) -> a d", a=1)
        turns = [(s_t[:], s_raw[:], SL, HP)]
        for k in range(KC):
            turns.append((m["w_fx"][:, k * 128:(k + 1) * 128], fx_raw[:, k, :], 128, D))
            turns.append((m["fcd"][:, k, :], fcd_raw[:, k * 128:(k + 1) * 128], HEADS, 128))
            for r in range(9):
                turns.append((m["w_in"][:, k, r * 128:(r + 1) * 128], in_raw[:, r, k * 128:(k + 1) * 128], 128, 128))
            turns.append((m["w_in"][:, k, 1152:1168], in_last[:, k * 128:(k + 1) * 128], 16, 128))
            for r in range(KC):
                turns.append((m["w_mix"][:, k, r * 128:(r + 1) * 128], out_raw[:, r, k * 128:(k + 1) * 128], 128, 128))
        for h in range(HEADS):
            turns.append((m["w_out"][:, h, :], o_raw[:, h * HP:(h + 1) * HP], 128, HP))
        loads = 9 + 2
        block = c.enter_context(nc.Block())

        @block.sync
        def _(sp):
            sp.dma_start(s_raw[:], W_slice).then_inc(loaded, 16)
            sp.dma_start(fx_raw[:], W_fx.rearrange("(k p) d -> p k d", p=128)).then_inc(loaded, 16)
            sp.dma_start(fcd_raw[:], fcD_w).then_inc(loaded, 16)
            sp.dma_start(in_raw[:], hy_in_w[0:1152].rearrange("(r p) d -> p r d", p=128)).then_inc(loaded, 16)
            sp.dma_start(in_last[:], hy_in_w[1152:1168]).then_inc(loaded, 16)
            sp.dma_start(out_raw[:], hy_out_w.rearrange("(r p) d -> p r d", p=128)).then_inc(loaded, 16)
            sp.dma_start(o_raw[:], out_w).then_inc(loaded, 16)
            sp.dma_start(x_raw[:], W_x.rearrange("(h p) d -> p h d", p=HP)).then_inc(loaded, 16)
            sp.dma_start(bx[:], b_x.rearrange("(h p) -> p h", p=HP), allow_slow_non_contiguous=True).then_inc(loaded, 16)
            sp.dma_start(t_row[:], temperature.rearrange("a h b c -> a (h b c)")).then_inc(loaded, 16)
            sp.dma_start(m["b_fx"][:], row(b_fx)).then_inc(loaded, 16)
            for h in range(HEADS):
                sp.dma_start(bs_row[0:1, h * SL:(h + 1) * SL], row(b_slice)).then_inc(loaded, 16)

        @block.tensor
        def _(pe):
            pe.wait_ge(loaded, 16 * (loads + HEADS))
            for n, (dst, src, r, cc) in enumerate(turns):
                if n >= 4:
                    pe.wait_ge(kept, n - 3)
                nc.tensor.transpose(bank[n % 4][0:cc, 0:r], src, m["ident"][0:r, 0:r]).then_inc(turned, 1)
            pe.wait_ge(kept, len(turns))
            pe.wait_ge(temp_ready, 1)
            nc.tensor.matmul(bank[4][:, :], m["ones_row"][:], t_wide[:], start=True, stop=True).then_inc(temp_made, 1)
            for h in range(HEADS):
                nc.tensor.matmul(bank[5][:, h * SL:(h + 1) * SL], x_raw[:, h, :], s_t[:],
                                 start=(h == 0), stop=(h == HEADS - 1), skip_group_check=True)
            for h in range(HEADS):
                i = nc.tensor.matmul(bank[6][0:1, h * SL:(h + 1) * SL], bx[:, h:h + 1], s_t[:],
                                     start=(h == 0), stop=(h == HEADS - 1), skip_group_check=True)
            i.then_inc(products, 1)

        @block.vector
        def _(dve):
            for n, (dst, src, r, cc) in enumerate(turns):
                dve.wait_ge(turned, n + 1)
                nc.vector.tensor_copy(dst, bank[n % 4][0:cc, 0:r]).then_inc(kept, 1)
            link = chain(dve, step)
            link(nc.vector.tensor_scalar(t_row[:], t_row[:], 1e-6, None, ALU.max))
            link(nc.vector.reciprocal(t_row[:], t_row[:]))
            nc.vector.tensor_copy(t_wide[:].rearrange("a (h g) -> a h g", g=SL),
                                  t_row[:].rearrange("a (h b) -> a h b", b=1).to_broadcast([1, HEADS, SL])).then_inc(temp_ready, 1)
            dve.wait_ge(temp_made, 1)
            link(nc.vector.tensor_copy(t_all[:], bank[4][:, :]))
            dve.wait_ge(products, 1)
            nc.vector.tensor_tensor(m["w_logit"][:], bank[5][:, :], t_all[:], ALU.mult)
            link(nc.vector.tensor_tensor(bs_row[:], bank[6][0:1, :], bs_row[:], ALU.add))
            nc.vector.tensor_tensor(m["b_logit"][:], bs_row[:], t_wide[:], ALU.mult)


def slice_tokens(nc, m, scratch):
    with ExitStack() as c:
        sem = lambda n: c.enter_context(nc.semaphore(n + "_s"))
        sb = lambda n, s: c.enter_context(nc.sbuf_tensor(n + "_s", s, F32))
        rows_ready, turned, kept, logits, maxed, lessened, exped, summed, inverted, weighed = (
            sem("rows_ready"), sem("turned"), sem("kept"), sem("logits"), sem("maxed"), sem("lessened"), sem("exped"),
            sem("summed"), sem("inverted"), sem("weighed"))
        w_turned, w_kept = sem("w_turned"), sem("w_kept")
        w_stored = [sem(f"w_stored{k}") for k in range(2)]
        rows = [sb(f"rows{k}", [T, GROUP, DE]) for k in range(2)]
        norm_t = [sb(f"norm_t{k}", [D, GT]) for k in range(2)]
        less = [sb(f"less{k}", [T, HEADS, SL]) for k in range(GROUP)]
        weight = [sb(f"weight{k}", [T, HEADS, SL]) for k in range(2)]
        peak = [sb(f"peak{k}", [T, HEADS]) for k in range(2)]
        share = [sb(f"share{k}", [T, HEADS]) for k in range(GROUP)]
        weight_t = [sb(f"weight_t{k}", [128, KC, T]) for k in range(2)]
        bank = m["bank"]
        block = c.enter_context(nc.Block())
        wide = lambda v: v[:].rearrange("p (h a) -> p h a", a=1).to_broadcast([T, HEADS, SL])

        def two_groups(i, engine, tile, ahead):
            for k in range(2):
                g = i * 2 + k
                for q in range(GROUP):
                    tile(g * GROUP + q, g, k, q)
                    if not (isinstance(g, int) and g == GROUPS - 1):
                        ahead(g + 1, 1 - k, q)

        def all_groups(engine, tile, ahead):
            two_groups(0, engine, tile, ahead)
            with engine.Fori(1, GROUPS // 2 - 1) as i:
                two_groups(i, engine, tile, ahead)
            two_groups(GROUPS // 2 - 1, engine, tile, ahead)

        def exists(n):
            return not isinstance(n, int) or n >= 0

        def wait_from(engine, s, value):
            if not isinstance(value, int) or value > 0:
                engine.wait_ge(s, value)

        @block.vector
        def _(dve):
            for k in range(2):
                nc.vector.memset(rows[k][:, :, D:DE], 1.0)

            def normalise(g, k):
                wait_from(dve, w_turned, (g - 1) * GROUP)
                for q in range(GROUP):
                    i = nc.vector.tensor_scalar(rows[k][:, q, 0:D], m["stream"][:, bass.ds(g * GROUP + q, 1), :],
                                                m["mean"][:, bass.ds(g * GROUP + q, 1)],
                                                m["rstd"][:, bass.ds(g * GROUP + q, 1)], ALU.subtract, ALU.mult)
                i.then_inc(rows_ready, 1)

            def finish(n, q):
                dve.wait_ge(exped, n + 1)
                nc.vector.tensor_reduce(share[q][:], less[q][:], AXX, ALU.add).then_inc(summed, 1)
                dve.wait_ge(summed, n + 1)
                nc.vector.reciprocal(share[q][:], share[q][:]).then_inc(inverted, 1)

            def tile(n, g, k, q):
                b = q % 2
                sums = bank[2 + b][0:T, :].rearrange("p (h g) -> p h g", g=SL)
                dve.wait_ge(logits, n + 1)
                nc.vector.tensor_reduce(peak[b][:], sums, AXX, ALU.max).then_inc(maxed, 1)
                wait_from(dve, weighed, n - 3)
                dve.wait_ge(maxed, n + 1)
                nc.vector.tensor_tensor(less[q][:], sums, wide(peak[b]), ALU.subtract).then_inc(lessened, 1)
                if exists(n - 1):
                    finish(n - 1, (q - 1) % GROUP)

            def ahead(g, k, q):
                if q == 1:
                    normalise(g, k)
            normalise(0, 0)
            all_groups(dve, tile, ahead)
            finish(TILES - 1, GROUP - 1)

        @block.gpsimd
        def _(pool):
            def tile(n, g, k, q):
                pool.wait_ge(inverted, n + 1)
                wait_from(pool, w_turned, n - 1)
                nc.gpsimd.tensor_tensor(weight[q % 2][:], less[q][:], wide(share[q]), ALU.mult).then_inc(weighed, 1)
            all_groups(pool, tile, lambda g, k, q: None)

        @block.scalar
        def _(act):
            def keep_rows(g, k):
                act.wait_ge(turned, g + 1)
                nc.scalar.activation(norm_t[k][:], bank[k][:, 0:GT], ACT.Copy).then_inc(kept, 1)

            def keep_weights(n, b, stores):
                act.wait_ge(w_turned, n + 1)
                wait_from(act, w_stored[b], stores * 16)
                nc.scalar.activation(weight_t[b][:].rearrange("p k t -> p (k t)"), bank[4 + b][:, 0:KC * T],
                                     ACT.Copy).then_inc(w_kept, 1)

            def tile(n, g, k, q):
                act.wait_ge(lessened, n + 1)
                nc.scalar.activation(less[q][:], less[q][:], ACT.Exp).then_inc(exped, 1)
                if exists(n - 2):
                    keep_weights(n - 2, q % 2, g * 2 + (q // 2 - 1))

            def ahead(g, k, q):
                if q == 2:
                    keep_rows(g, k)
            keep_rows(0, 0)
            all_groups(act, tile, ahead)
            for b in range(2):
                keep_weights(TILES - 2 + b, b, TILES // 2 - 1)

        @block.sync
        def _(sp):
            with sp.Fori(0, GROUPS) as g:
                for q in range(GROUP):
                    b = q % 2
                    sp.wait_ge(w_kept, g * GROUP + (q + 1))
                    sp.dma_start(scratch[bass.ds(g * GROUP + q, 1)].rearrange("a p c -> p (a c)"),
                                 weight_t[b][:].rearrange("p k t -> p (k t)")).then_inc(w_stored[b], 16)
            for b in range(2):
                sp.wait_ge(w_stored[b], 16 * (TILES // 2))

        @block.tensor
        def _(pe):
            zeros = m["zero_row"][0:1].rearrange("a q d -> a (q d)")
            for h in range(2):
                nc.tensor.matmul(bank[6 + h][:, 0:2 * DE], m["ones_row"][0:1, :], zeros, start=True, stop=False,
                                 skip_group_check=True)

            def turn_rows(g, k):
                pe.wait_ge(rows_ready, g + 1)
                for q in range(GROUP):
                    t = nc.tensor.transpose(bank[k][:, q * T:(q + 1) * T], rows[k][:, q, 0:D], m["ident"][0:T, 0:T])
                t.then_inc(turned, 1)

            def apply(n, k, q):
                b = q % 2
                pe.wait_ge(weighed, n + 1)
                flat = weight[b][:].rearrange("p h g -> p (h g)")
                for r in range(KC):
                    nc.tensor.matmul(bank[6 + r // 2][:, r % 2 * DE:(r % 2 + 1) * DE], flat[:, r * 128:(r + 1) * 128],
                                     rows[k][:, q, :], start=False, stop=False, skip_group_check=True)
                wait_from(pe, w_kept, n - 1)
                for r in range(KC):
                    t = nc.tensor.transpose(bank[4 + b][:, r * T:(r + 1) * T], flat[:, r * 128:(r + 1) * 128],
                                            m["ident"][0:T, 0:T])
                t.then_inc(w_turned, 1)

            def tile(n, g, k, q):
                b = q % 2
                if q == 0:
                    pe.wait_ge(kept, g + 1)
                wait_from(pe, lessened, n - 1)
                nc.tensor.matmul(bank[2 + b][0:T, :], m["ones_row"][0:1, 0:T], m["b_logit"][:], start=True, stop=False)
                nc.tensor.matmul(bank[2 + b][0:T, :], norm_t[k][:, q * T:(q + 1) * T], m["w_logit"][:],
                                 start=False, stop=True).then_inc(logits, 1)
                if exists(n - 2):
                    apply(n - 2, k if q >= 2 else 1 - k, (q - 2) % GROUP)

            def ahead(g, k, q):
                if q == 2:
                    turn_rows(g, k)
            turn_rows(0, 0)
            all_groups(pe, tile, ahead)
            for q in range(2, GROUP):
                apply(TILES - GROUP + q, 1, q)
            for h in range(2):
                nc.tensor.matmul(bank[6 + h][:, 0:2 * DE], m["ones_row"][0:1, :], zeros, start=False, stop=True,
                                 skip_group_check=True)


def mixer(nc, m, hy_conv_w, hy_conv_b, hy_dt_bias, hy_A_log, hy_D, hy_norm_w):
    with ExitStack() as c:
        sem = lambda n: c.enter_context(nc.semaphore(n + "_x"))
        sb = lambda n, s: c.enter_context(nc.sbuf_tensor(n + "_x", s, F32))
        loaded, pe_done, dve_done, act_done, step, dt_step = (
            sem("loaded"), sem("pe_done"), sem("dve_done"), sem("act_done"), sem("step"), sem("dt_step"))
        S = SL
        cw_x, cw_bc, cb_x, cb_bc = sb("cw_x", [128, KC, 3]), sb("cw_bc", [S, 2, 3]), sb("cb_x", [128, KC]), sb("cb_bc", [S, 2])
        dt_row, a_row, d_row, nw = sb("dt_row", [1, 16]), sb("a_row", [1, 16]), sb("d_row", [1, HEADS]), sb("nw", [128, KC])
        sums, sums_t, n_row, n_col = sb("sums", [128, KC, DE]), sb("sums_t", [D, HS]), sb("n_row", [1, HS]), sb("n_col", [S, HEADS])
        slices, slices_t = sb("slices", [S, HEADS, HP]), sb("slices_t", [128, KC, S])
        z_t, x_pad, bc_pad = sb("z_t", [128, KC, S]), sb("x_pad", [128, KC, S + 2]), sb("bc_pad", [S, 2, S + 2])
        x_t, bc_t, gate_x, gate_bc, gate_z = (
            sb("x_t", [128, KC, S]), sb("bc_t", [S, 2, S]), sb("gate_x", [128, KC, S]), sb("gate_bc", [S, 2, S]), sb("gate_z", [128, KC, S]))
        x_nat, z_nat = sb("x_nat", [S, HEADS, HP]), sb("z_nat", [S, HEADS, HP])
        raw_dt, dt, e_dt, l_dt, mask, w1, rate, over = (
            sb("raw_dt", [S, 16]), sb("dt", [S, 16]), sb("e_dt", [S, 16]), sb("l_dt", [S, 16]), sb("mask", [S, 16]), sb("w1", [S, 16]), sb("rate", [S, 16]), sb("over", [S, 16]))
        dA, dA_t = sb("dA", [S, 16]), sb("dA_t", [16, S])
        decay = sb("decay", [S, 2, HEADS, S])
        cb, mf, mb = sb("cb", [S, S]), sb("mf", [S, HEADS, S + 1]), sb("mb", [S, HEADS, S + 1])
        xf, xb = sb("xf", [S, HEADS, HP]), sb("xb", [S, HEADS, HP])
        fc, y, y2 = sb("fc", [S, HEADS]), sb("y", [S, HEADS, HP]), sb("y2", [S, HEADS, HP])
        ms, root, inv, spare = sb("ms", [S, 1]), sb("root", [S, 1]), sb("inv", [S, 1]), sb("spare", [S, 1])
        y_t, mixed = sb("y_t", [128, KC, S]), sb("mixed", [HP, HEADS, S])
        bank = m["bank"]
        ident, ones_row = m["ident"], m["ones_row"]
        row = lambda v: v.rearrange("(a d) -> a d", a=1)
        block = c.enter_context(nc.Block())

        @block.sync
        def _(sp):
            slow = dict(allow_slow_non_contiguous=True)
            sp.dma_start(cw_x[:], hy_conv_w[0:HID].rearrange("(k p) t -> p k t", p=128), **slow).then_inc(loaded, 16)
            sp.dma_start(cw_bc[:], hy_conv_w[HID:HID + 2 * S].rearrange("(k p) t -> p k t", p=S), **slow).then_inc(loaded, 16)
            sp.dma_start(cb_x[:], hy_conv_b[0:HID].rearrange("(k p) -> p k", p=128), **slow).then_inc(loaded, 16)
            sp.dma_start(cb_bc[:], hy_conv_b[HID:HID + 2 * S].rearrange("(k p) -> p k", p=S), **slow).then_inc(loaded, 16)
            sp.dma_start(nw[:], hy_norm_w.rearrange("(k p) -> p k", p=128), **slow).then_inc(loaded, 16)
            for h in range(2):
                sp.dma_start(dt_row[0:1, h * 8:h * 8 + 8], row(hy_dt_bias)).then_inc(loaded, 16)
                sp.dma_start(a_row[0:1, h * 8:h * 8 + 8], row(hy_A_log)).then_inc(loaded, 16)
            sp.dma_start(d_row[:], row(hy_D)).then_inc(loaded, 16)

        @block.tensor
        def _(pe):
            mm, turn = nc.tensor.matmul, nc.tensor.transpose
            loose = dict(skip_group_check=True)
            pe.wait_ge(dve_done, 1)
            for k in range(KC):
                i = turn(bank[0][:, k * 128:(k + 1) * 128], sums[:, k, 0:D], ident[:])
            for k in range(KC):
                i = mm(bank[1][0:1, k * 128:(k + 1) * 128], sums[:, k, D:DE], ident[:], start=(k == 0), stop=True, **loose)
            i.then_inc(pe_done, 1)
            pe.wait_ge(dve_done, 2)
            for h in range(HEADS):
                i = mm(bank[2][0:S, h:h + 1], n_row[0:1, h * S:(h + 1) * S], ones_row[0:1, 0:1], start=(h == 0), stop=True, **loose)
            for h in range(HEADS):
                mm(bank[3][0:S, h * HP:(h + 1) * HP], sums_t[:, h * S:(h + 1) * S], m["w_fx"][:, h * HP:(h + 1) * HP],
                   start=(h == 0), stop=False, **loose)
                i = mm(bank[3][0:S, h * HP:(h + 1) * HP], n_row[0:1, h * S:(h + 1) * S], m["b_fx"][0:1, h * HP:(h + 1) * HP],
                       start=False, stop=True, **loose)
            i.then_inc(pe_done, 1)
            pe.wait_ge(dve_done, 3)
            for k in range(KC):
                i = turn(bank[4][:, k * S:(k + 1) * S], slices[:].rearrange("p h c -> p (h c)")[:, k * 128:(k + 1) * 128], ident[0:S, 0:S])
            i.then_inc(pe_done, 1)
            pe.wait_ge(dve_done, 4)
            pe.wait_ge(loaded, 16 * 10)
            for r in range(2 * KC):
                for k in range(KC):
                    mm(bank[5][:, r * S:(r + 1) * S], m["w_in"][:, k, r * 128:(r + 1) * 128], slices_t[:, k, :],
                       start=(r == 0 and k == 0), stop=(k == KC - 1), **loose)
            for r in range(2):
                for k in range(KC):
                    mm(bank[6][0:S, r * S:(r + 1) * S], m["w_in"][:, k, 1024 + r * S:1024 + (r + 1) * S], slices_t[:, k, :],
                       start=(r == 0 and k == 0), stop=(k == KC - 1), **loose)
            for k in range(KC):
                mm(bank[6][0:S, 128:144], slices_t[:, k, :], m["w_in"][:, k, 1152:1168], start=False, stop=False, **loose)
            mm(bank[6][0:S, 128:144], ones_row[0:1, 0:S], dt_row[:], start=False, stop=True, **loose)
            i = mm(bank[6][0:S, 144:160], ones_row[0:1, 0:S], a_row[:], start=False, stop=True, **loose)
            i.then_inc(pe_done, 1)
            pe.wait_ge(dve_done, 6)
            for k in range(KC):
                turn(bank[0][0:S, k * 128:(k + 1) * 128], x_t[:, k, :], ident[:])
            for k in range(KC):
                turn(bank[1][0:S, k * 128:(k + 1) * 128], z_t[:, k, :], ident[:])
            mm(bank[2][0:S, 0:S], bc_t[:, 0, :], bc_t[:, 1, :], start=True, stop=True)
            for k in range(KC):
                mm(bank[2][0:S, 128:128 + HEADS], x_t[:, k, :], m["fcd"][:, k, :], start=False, stop=False, **loose)
            mm(bank[2][0:S, 128:128 + HEADS], ones_row[0:1, 0:S], d_row[:], start=False, stop=True, **loose)
            pe.wait_ge(act_done, 5)
            i = turn(bank[7][0:16, 0:S], dA[:], ident[0:S, 0:S])
            i.then_inc(pe_done, 1)
            pe.wait_ge(dve_done, 7)
            for d in range(2):
                for h in range(HEADS):
                    j = d * HEADS + h
                    i = mm(bank[3 + d][0:S, h * S:(h + 1) * S], ident[0:16, j:j + 1].to_broadcast([16, S]), dA_t[:],
                           start=(h == 0), stop=True, **loose)
            i.then_inc(pe_done, 1)
            pe.wait_ge(dve_done, 8)
            for h in range(HEADS):
                mm(bank[5][0:S, h * HP:(h + 1) * HP], mf[:, h, 0:S], xf[:, h, :], start=(h == 0), stop=False, **loose)
                i = mm(bank[5][0:S, h * HP:(h + 1) * HP], mb[:, h, 1:S + 1], xb[:, h, :], start=False, stop=True, **loose)
            i.then_inc(pe_done, 1)
            pe.wait_ge(dve_done, 10)
            for k in range(KC):
                i = turn(bank[0][:, k * S:(k + 1) * S], y2[:].rearrange("p h c -> p (h c)")[:, k * 128:(k + 1) * 128], ident[0:S, 0:S])
            i.then_inc(pe_done, 1)
            pe.wait_ge(dve_done, 11)
            for h in range(HEADS):
                for k in range(KC):
                    i = mm(bank[1][0:HP, h * S:(h + 1) * S], m["w_mix"][:, k, h * HP:(h + 1) * HP], y_t[:, k, :],
                           start=(h == 0 and k == 0), stop=(k == KC - 1), **loose)
            i.then_inc(pe_done, 1)
            pe.wait_ge(dve_done, 12)
            for h in range(HEADS):
                p = h % 2 * S
                i = mm(bank[3][p:p + S, h // 2 * D:(h // 2 + 1) * D], mixed[:, h, :], m["w_out"][:, h, :],
                       start=(h < 2), stop=True, **loose)
            i.then_inc(pe_done, 1)

        @block.scalar
        def _(act):
            act.wait_ge(dve_done, 5)
            nc.scalar.activation(gate_x[:], x_t[:], ACT.Exp, scale=-1.0)
            nc.scalar.activation(gate_bc[:], bc_t[:], ACT.Exp, scale=-1.0)
            nc.scalar.activation(gate_z[:], z_t[:], ACT.Exp, scale=-1.0).then_inc(act_done, 1)
            nc.scalar.activation(e_dt[:], w1[:], ACT.Exp, scale=-1.0).then_inc(act_done, 1)
            nc.scalar.activation(rate[:], rate[:], ACT.Exp, scale=0.5).then_inc(act_done, 1)
            act.wait_ge(dt_step, 1)
            nc.scalar.activation(l_dt[:], w1[:], ACT.Ln).then_inc(act_done, 1)
            act.wait_ge(dt_step, 2)
            nc.scalar.activation(dA[:], mask[:], ACT.Exp, scale=-1.0).then_inc(act_done, 1)
            act.wait_ge(dve_done, 9)
            nc.scalar.activation(root[:], ms[:], ACT.Sqrt).then_inc(act_done, 1)

        @block.vector
        def _(dve):
            v = nc.vector
            link = chain(dve, step)
            wide = lambda t: t.rearrange("p (h a) -> p h a", a=1).to_broadcast([S, HEADS, HP])
            v.tensor_copy(sums[:, 0:2, :], bank[6][:, 0:2 * DE].rearrange("p (q d) -> p q d", d=DE))
            v.tensor_copy(sums[:, 2:4, :], bank[7][:, 0:2 * DE].rearrange("p (q d) -> p q d", d=DE)).then_inc(dve_done, 1)
            dve.wait_ge(pe_done, 1)
            v.tensor_copy(sums_t[:], bank[0][:, :])
            v.tensor_copy(n_row[:], bank[1][0:1, :]).then_inc(dve_done, 1)
            dve.wait_ge(pe_done, 2)
            link(v.tensor_scalar(n_col[:], bank[2][0:S, 0:HEADS], 1e-5, None, ALU.add))
            link(v.reciprocal(n_col[:], n_col[:]))
            v.tensor_tensor(slices[:], bank[3][0:S, :].rearrange("p (h c) -> p h c", c=HP), wide(n_col[:]), ALU.mult).then_inc(dve_done, 1)
            dve.wait_ge(pe_done, 3)
            v.tensor_copy(slices_t[:], bank[4][:, 0:KC * S].rearrange("p (k s) -> p k s", s=S)).then_inc(dve_done, 1)
            v.memset(x_pad[:, :, 0:2], 0.0)
            v.memset(bc_pad[:, :, 0:2], 0.0)
            v.memset(mf[:, :, 0:1], 0.0)
            v.memset(mb[:, :, S:S + 1], 0.0)
            dve.wait_ge(pe_done, 4)
            dve.wait_ge(loaded, 16 * 10)
            v.tensor_copy(z_t[:], bank[5][:, 0:KC * S].rearrange("p (k s) -> p k s", s=S))
            v.tensor_copy(x_pad[:, :, 2:S + 2], bank[5][:, KC * S:2 * KC * S].rearrange("p (k s) -> p k s", s=S))
            v.tensor_copy(bc_pad[:, :, 2:S + 2], bank[6][0:S, 0:2 * S].rearrange("p (k s) -> p k s", s=S))
            link(v.tensor_copy(raw_dt[:], bank[6][0:S, 128:144]))
            v.tensor_scalar(over[:], bank[6][0:S, 144:160], 88.7228, 1e30, ALU.is_gt, ALU.mult)
            v.tensor_scalar(rate[:], bank[6][0:S, 144:160], 88.7228, None, ALU.min)
            link(v.scalar_tensor_tensor(w1[:], raw_dt[:], -1.0, raw_dt[:], ALU.mult, ALU.max))
            for pad, out, taps, bias, n in ((x_pad, x_t, cw_x, cb_x, KC), (bc_pad, bc_t, cw_bc, cb_bc, 2)):
                for k in range(n):
                    i = v.tensor_scalar(out[:, k, :], pad[:, k, 0:S], taps[:, k, 0:1], bias[:, k:k + 1], ALU.mult, ALU.add)
                link(i)
                for tap in (1, 2):
                    for k in range(n):
                        i = v.scalar_tensor_tensor(out[:, k, :], pad[:, k, tap:S + tap], taps[:, k, tap:tap + 1], out[:, k, :],
                                                   ALU.mult, ALU.add)
                    link(i)
            dve.sem_inc(dve_done, 1)
            dve.wait_ge(act_done, 1)
            for g in (gate_x, gate_bc, gate_z):
                i = v.tensor_scalar(g[:], g[:], 1.0, None, ALU.add)
            link(i)
            for g in (gate_x, gate_bc, gate_z):
                i = v.reciprocal(g[:], g[:])
            link(i)
            v.tensor_tensor(x_t[:], x_t[:], gate_x[:], ALU.mult)
            v.tensor_tensor(bc_t[:], bc_t[:], gate_bc[:], ALU.mult)
            v.tensor_tensor(z_t[:], z_t[:], gate_z[:], ALU.mult).then_inc(dve_done, 1)
            dve.wait_ge(act_done, 3)
            v.tensor_scalar(w1[:], e_dt[:], 1.0, None, ALU.add).then_inc(dt_step, 1)
            dve.wait_ge(dt_step, 1)
            link(v.tensor_scalar(mask[:], w1[:], 1.0, None, ALU.is_equal))
            link(v.tensor_tensor(mask[:], mask[:], e_dt[:], ALU.mult))
            link(v.tensor_scalar(dt[:], w1[:], -1.0, 1e-30, ALU.add, ALU.max))
            link(v.reciprocal(dt[:], dt[:]))
            link(v.tensor_tensor(dt[:], dt[:], e_dt[:], ALU.mult))
            dve.wait_ge(act_done, 4)
            link(v.tensor_tensor(dt[:], dt[:], l_dt[:], ALU.mult))
            link(v.tensor_tensor(dt[:], dt[:], mask[:], ALU.add))
            link(v.scalar_tensor_tensor(dt[:], raw_dt[:], 0.0, dt[:], ALU.max, ALU.add))
            link(v.tensor_tensor(mask[:], dt[:], rate[:], ALU.mult))
            link(v.scalar_tensor_tensor(mask[:], mask[:], 1e18, rate[:], ALU.min, ALU.mult))
            v.tensor_tensor(mask[:], mask[:], over[:], ALU.add).then_inc(dt_step, 1)
            dve.wait_ge(pe_done, 5)
            v.tensor_copy(x_nat[:], bank[0][0:S, :].rearrange("p (h c) -> p h c", c=HP))
            v.tensor_copy(z_nat[:], bank[1][0:S, :].rearrange("p (h c) -> p h c", c=HP))
            v.tensor_copy(cb[:], bank[2][0:S, 0:S])
            v.tensor_copy(fc[:], bank[2][0:S, 128:128 + HEADS])
            link(v.tensor_copy(dA_t[:], bank[7][0:16, 0:S]))
            dve.sem_inc(dve_done, 1)
            v.tensor_tensor(xf[:], x_nat[:], wide(dt[:, 0:HEADS]), ALU.mult)
            v.tensor_tensor(xb[:], x_nat[:], wide(dt[:, HEADS:]), ALU.mult)
            v.tensor_tensor(y[:], x_nat[:], wide(fc[:]), ALU.mult)
            dve.wait_ge(pe_done, 6)
            for h in range(HEADS):
                v.tensor_tensor_scan(decay[:, 0, h, :], bank[3][0:S, h * S:(h + 1) * S], ident[0:S, 0:S], 0.0, ALU.mult, ALU.add)
                i = v.tensor_tensor_scan(decay[:, 1, h, :][:, ::-1], bank[4][0:S, h * S:(h + 1) * S][:, ::-1],
                                         ident[0:S, 0:S][:, ::-1], 0.0, ALU.mult, ALU.add)
            link(i)
            cb_all = cb[:].rearrange("p (a t) -> p a t", a=1).to_broadcast([S, HEADS, S])
            v.tensor_tensor(mf[:, :, 1:S + 1], decay[:, 0], cb_all, ALU.mult)
            v.tensor_tensor(mb[:, :, 0:S], decay[:, 1], cb_all, ALU.mult).then_inc(dve_done, 1)
            dve.wait_ge(pe_done, 7)
            link(v.tensor_tensor(y[:], bank[5][0:S, :].rearrange("p (h c) -> p h c", c=HP), y[:], ALU.add))
            link(v.tensor_tensor(y[:], y[:], z_nat[:], ALU.mult))
            link(v.tensor_tensor(y2[:], y[:], y[:], ALU.mult))
            link(v.tensor_reduce(ms[:], y2[:].rearrange("p h c -> p (h c)"), AXX, ALU.add))
            link(v.tensor_scalar(ms[:], ms[:], 1.0 / HID, EPS, ALU.mult, ALU.add))
            dve.sem_inc(dve_done, 1)
            dve.wait_ge(act_done, 6)
            inverse_root(nc, link, inv[:], root[:], ms[:], spare[:])
            v.tensor_scalar(y2[:], y[:], inv[:], None, ALU.mult).then_inc(dve_done, 1)
            dve.wait_ge(pe_done, 8)
            v.tensor_tensor(y_t[:], bank[0][:, 0:KC * S].rearrange("p (k s) -> p k s", s=S),
                            nw[:].rearrange("p (k a) -> p k a", a=1).to_broadcast([128, KC, S]), ALU.mult).then_inc(dve_done, 1)
            dve.wait_ge(pe_done, 9)
            v.tensor_copy(mixed[:], bank[1][0:HP, :].rearrange("p (h s) -> p h s", s=S)).then_inc(dve_done, 1)
            dve.wait_ge(pe_done, 10)
            v.tensor_copy(m["proj"][:].rearrange("p k d -> p (k d)"), bank[3][:, :])


def gather_out(nc, m, scratch, out_b, out):
    with ExitStack() as c:
        sem = lambda n: c.enter_context(nc.semaphore(n + "_o"))
        sb = lambda n, s: c.enter_context(nc.sbuf_tensor(n + "_o", s, F32))
        w_loaded = [sem(f"w_loaded{k}") for k in range(2)]
        row_loaded, products, added, stored = sem("row_loaded"), sem("products"), sem("added"), sem("stored")
        weight = [sb(f"weight{k}", [128, GROUP, KC * T]) for k in range(2)]
        b_row = sb("b_row", [1, GROUP, D])
        bank = m["bank"]
        out_view = out.rearrange("(t p) d -> p t d", p=T)
        block = c.enter_context(nc.Block())

        @block.sync
        def _(sp):
            for q in range(GROUP):
                sp.dma_start(b_row[0:1, q, :], out_b.rearrange("(a d) -> a d", a=1)).then_inc(row_loaded, 16)

            def load(g, k):
                sp.dma_start(weight[k][:], scratch[bass.ds(g * GROUP, GROUP)].rearrange("t p c -> p t c")).then_inc(w_loaded[k], 16)

            load(0, 0)
            load(1, 1)
            with sp.Fori(0, GROUPS // 2 - 1) as i:
                for k in range(2):
                    sp.wait_ge(products, i * 2 + (k + 1))
                    load(i * 2 + (2 + k), k)

        @block.tensor
        def _(pe):
            pe.wait_ge(row_loaded, 16 * GROUP)

            def work(g, i, k, free):
                pe.wait_ge(w_loaded[k], (i + 1) * 16)
                if free is not None:
                    pe.wait_ge(added, free)
                nc.tensor.matmul(bank[k][0:T, 0:GD], m["ones_row"][0:1, 0:T], b_row[0:1].rearrange("a q d -> a (q d)"),
                                 start=True, stop=False, skip_group_check=True)
                for q in range(GROUP):
                    for r in range(KC):
                        t = nc.tensor.matmul(bank[k][0:T, q * D:(q + 1) * D], weight[k][:, q, r * T:(r + 1) * T],
                                             m["proj"][:, r, :], start=False, stop=(r == KC - 1), skip_group_check=True)
                t.then_inc(products, 1)
            work(0, 0, 0, None)
            work(1, 0, 1, None)
            with pe.Fori(1, GROUPS // 2) as i:
                for k in range(2):
                    work(i * 2 + k, i, k, i * 2 + (k - 1))

        @block.vector
        def _(dve):
            with dve.Fori(0, GROUPS // 2) as i:
                for k in range(2):
                    g = i * 2 + k
                    dve.wait_ge(products, g + 1)
                    here = m["stream"][:, bass.ds(g * GROUP, GROUP), :]
                    nc.vector.tensor_tensor(here, bank[k][0:T, 0:GD].rearrange("p (q d) -> p q d", d=D), here, ALU.add
                                            ).then_inc(added, 1)

        @block.scalar
        def _(act):
            with act.Fori(0, GROUPS) as g:
                act.wait_ge(added, g + 1)
                act.dma_start(out_view[:, bass.ds(g * GROUP, GROUP), :], m["stream"][:, bass.ds(g * GROUP, GROUP), :]
                              ).then_inc(stored, 16)
            act.wait_ge(stored, 16 * GROUPS)


NAMES = ['x', 'adj', 'L0_gnn_item_feat', 'L0_gnn_W_item', 'L0_gnn_b_item', 'L0_gnn_W_user', 'L0_gnn_b_user',
         'L0_ffn_W_ih', 'L0_ffn_W_hh', 'L0_ffn_b_ih', 'L0_ffn_b_hh', 'L0_ffn_W_lin', 'L0_ffn_b_lin', 'L0_ffn_fw_att',
         'L0_ffn_bw_att', 'L1_gnn_W', 'L1_ffn_W_fx', 'L1_ffn_b_fx', 'L1_ffn_W_x', 'L1_ffn_b_x', 'L1_ffn_W_slice',
         'L1_ffn_b_slice', 'L1_ffn_temperature', 'L1_ffn_hy_in_w', 'L1_ffn_hy_conv_w', 'L1_ffn_hy_conv_b',
         'L1_ffn_hy_dt_bias', 'L1_ffn_hy_A_log', 'L1_ffn_hy_D', 'L1_ffn_hy_fcD_w', 'L1_ffn_hy_norm_w',
         'L1_ffn_hy_out_w', 'L1_ffn_out_w', 'L1_ffn_out_b']


def build(nc, a, scratch, out):
    with ExitStack() as c:
        m = common(nc, c)

        def split_features(stack, tag):
            for half in ("feats_high", "feats_low"):
                m[half] = stack.enter_context(nc.sbuf_tensor(half + tag, [T, TILES, D], F32R))

        with ExitStack() as graph0:
            split_features(graph0, "_a")
            setup(nc, m, a['L0_gnn_W_item'], a['L0_gnn_b_item'], a['L0_gnn_W_user'], a['L0_ffn_W_ih'],
                  a['L0_ffn_W_hh'], a['L0_ffn_b_ih'], a['L0_ffn_b_hh'], a['L1_gnn_W'], a['x'], a['L0_gnn_item_feat'])
            norm_stats(nc, m, "_1")
            adjacency_pass(nc, m, a['adj'], a['L0_gnn_b_user'], True)
        norm_stats(nc, m, "_2")
        with ExitStack() as sequence:
            m["wide1"] = sequence.enter_context(nc.sbuf_tensor("wide1", [128, N + 1], F32))
            m["wide2"] = sequence.enter_context(nc.sbuf_tensor("wide2", [128, N], F32))
            norm_transposed(nc, m, "_2")
            lstm(nc, m)
            mix(nc, m, a['L0_ffn_W_lin'], a['L0_ffn_b_lin'], a['L0_ffn_fw_att'], a['L0_ffn_bw_att'])
        norm_stats(nc, m, "_3")
        with ExitStack() as graph1:
            split_features(graph1, "_b")
            graph_features(nc, m)
            adjacency_pass(nc, m, a['adj'], None, False)
        norm_stats(nc, m, "_4")
        with ExitStack() as late:
            sb = lambda n, s: late.enter_context(nc.sbuf_tensor(n, s, F32))
            m["w_fx"], m["fcd"] = sb("w_fx", [D, HID]), sb("fcd", [128, KC, HEADS])
            m["w_mix"], m["w_out"] = sb("w_mix", [128, KC, HID]), sb("w_out", [HP, HEADS, D])
            m["w_logit"], m["b_logit"], m["b_fx"] = sb("w_logit", [D, HS]), sb("b_logit", [1, HS]), sb("b_fx", [1, HID])
            m["w_in"] = sb("w_in", [128, KC, 1168])
            m["proj"] = sb("proj", [128, KC, D])
            slice_weights(nc, m, a['L1_ffn_W_fx'], a['L1_ffn_b_fx'], a['L1_ffn_W_x'], a['L1_ffn_b_x'], a['L1_ffn_W_slice'],
                          a['L1_ffn_b_slice'], a['L1_ffn_temperature'], a['L1_ffn_hy_fcD_w'], a['L1_ffn_hy_in_w'],
                          a['L1_ffn_hy_out_w'], a['L1_ffn_out_w'])
            slice_tokens(nc, m, scratch)
            mixer(nc, m, a['L1_ffn_hy_conv_w'], a['L1_ffn_hy_conv_b'], a['L1_ffn_hy_dt_bias'], a['L1_ffn_hy_A_log'],
                  a['L1_ffn_hy_D'], a['L1_ffn_hy_norm_w'])
            gather_out(nc, m, scratch, a['L1_ffn_out_b'], out)


def kernel(**inputs):
    from concourse import bacc
    from concourse.bass_utils import run_bass_kernel_spmd

    nc = bacc.Bacc("TRN2", target_bir_lowering=False, num_devices=1)
    arrays, aps = {}, {}
    for name in NAMES:
        a = np.ascontiguousarray(inputs[name])
        arrays[f"in_{name}_dram"] = a
        aps[name] = nc.dram_tensor(f"in_{name}_dram", a.shape, mybir.dt.from_np(a.dtype), kind="ExternalInput").ap()
    scratch = nc.dram_tensor("slice_weights_dram", (TILES, 128, KC * T), F32, kind="Internal").ap()
    out = nc.dram_tensor("out_0_dram", (N, D), F32, kind="ExternalOutput").ap()
    build(nc, aps, scratch, out)
    r = run_bass_kernel_spmd(nc, [arrays], core_ids=[0])
    return r.results[0]["out_0_dram"]
```

```python
from contextlib import ExitStack

import numpy as np

import concourse.bass as bass
from concourse import mybir

F32 = mybir.dt.float32
F32R = mybir.dt.float32r
I32 = mybir.dt.int32
ALU = mybir.AluOpType
ACT = mybir.ActivationFunctionType
AXX = mybir.AxisListType.X

N, D = 10000, 128
T = 125
TILES = N // T
GROUP = 4
GROUPS = TILES // GROUP
GT = GROUP * T
GD = GROUP * D
EPS = 1e-5
DE = D + 1

SLOTS = 4
PB = 4
PCOLS = PB * T
PANELS = TILES // PB
STAGES = 4
AHEAD = 3


def chain(engine, sem, start=0):
    count = [start]

    def link(instruction):
        count[0] = count[0] + 1
        instruction.then_inc(sem, 1)
        engine.wait_ge(sem, count[0])
    return link


def inverse_root(nc, link, out, root, value, spare):
    link(nc.vector.reciprocal(out, root))
    link(nc.vector.tensor_tensor(spare, value, out, ALU.mult))
    link(nc.vector.tensor_tensor(spare, spare, out, ALU.mult))
    link(nc.vector.tensor_scalar(spare, spare, -0.5, 1.5, ALU.mult, ALU.add))
    link(nc.vector.tensor_tensor(out, out, spare, ALU.mult))


X_PARTS = 5


def setup(nc, m, W_item, b_item, W_user, W_ih, W_hh, b_ih, b_hh, gnn_w, x, item, adj):
    with ExitStack() as c:
        sem = lambda n: c.enter_context(nc.semaphore(n))
        sb = lambda n, s: c.enter_context(nc.sbuf_tensor(n, s, F32))
        w_loaded, rows_loaded = sem("w_loaded"), sem("rows_loaded")
        x_loaded = [sem(f"x_loaded{k}") for k in range(X_PARTS)]
        x_parts = [slice(k * TILES // X_PARTS, (k + 1) * TILES // X_PARTS) for k in range(X_PARTS)]
        item_loaded = [sem(f"item_loaded{k}") for k in range(2)]
        id_zero, id_done, ones_set = sem("id_zero"), sem("id_done"), sem("ones_set")
        w_turned, w_kept = sem("w_turned"), sem("w_kept")
        item_turned, item_staged, item_done, item_high, item_kept = (
            sem("item_turned"), sem("item_staged"), sem("item_done"), sem("item_high"), sem("item_kept"))
        wraw = sb("wraw", [128, 10, 128])
        item_in = [sb(f"item_in{k}", [T, GROUP, D]) for k in range(2)]
        item_t = [sb(f"item_t{k}", [D, GT]) for k in range(2)]
        brow, bias = sb("brow", [1, GROUP, D]), sb("bias", [T, GROUP, D])
        items = [sb(f"items{k}", [T, GROUP, D]) for k in range(2)]
        bias_spread, bias_kept, item_summed = sem("bias_spread"), sem("bias_kept"), sem("item_summed")
        b2 = sb("b2", [128, 4])
        bank = m["bank"]
        x_view = x.rearrange("(t p) d -> p t d", p=T)
        item_view = item.rearrange("(t p) d -> p t d", p=T)
        row = lambda v: v.rearrange("(a d) -> a d", a=1)
        block = c.enter_context(nc.Block())

        @block.sync
        def _(sp):
            sp.dma_start(wraw[:, 0, :], W_item).then_inc(w_loaded, 16)
            sp.dma_start(wraw[:, 1, :], W_user).then_inc(w_loaded, 16)
            sp.dma_start(wraw[:, 2:6, :], W_ih.rearrange("(k p) d -> p k d", p=128)).then_inc(w_loaded, 16)
            sp.dma_start(wraw[:, 6:10, :], W_hh.rearrange("(k p) d -> p k d", p=128)).then_inc(w_loaded, 16)
            for q in range(GROUP):
                sp.dma_start(brow[0:1, q, :], row(b_item)).then_inc(rows_loaded, 16)
            sp.dma_start(m["gnn_w"][:], gnn_w).then_inc(rows_loaded, 16)
            sp.dma_start(m["gate_b"][:], b_ih.rearrange("(k p) -> p k", p=128), allow_slow_non_contiguous=True).then_inc(rows_loaded, 16)
            sp.dma_start(b2[:], b_hh.rearrange("(k p) -> p k", p=128), allow_slow_non_contiguous=True).then_inc(rows_loaded, 16)
            for k in range(2):
                sp.dma_start(item_in[k][:], item_view[:, k * GROUP:(k + 1) * GROUP, :]).then_inc(item_loaded[k], 16)
            with sp.Fori(0, GROUPS // 2 - 1) as i:
                for k in range(2):
                    sp.wait_ge(item_turned, i * 2 + (k + 1))
                    sp.dma_start(item_in[k][:], item_view[:, bass.ds((i * 2 + 2 + k) * GROUP, GROUP), :]
                                 ).then_inc(item_loaded[k], 16)
            first_panels(sp, m, adj)
            for k in range(X_PARTS):
                sp.wait_ge(x_loaded[k], 16)
            sp.wait_ge(rows_loaded, 16 * 7)

        @block.gpsimd
        def _(pool):
            nc.gpsimd.memset(m["ident"][:], 0.0).then_inc(id_zero, 1)
            pool.wait_ge(id_zero, 1)
            nc.gpsimd.affine_select(out=m["ident"][:], in_=m["ident"][:], compare_op=ALU.not_equal, fill=1.0,
                                    base=0, pattern=[[-1, 128]], channel_multiplier=1).then_inc(id_done, 1)

        @block.tensor
        def _(pe):
            pe.wait_ge(id_done, 1)
            pe.wait_ge(w_loaded, 64)
            for k in range(10):
                nc.tensor.transpose(bank[k // 4][:, (k % 4) * 128:(k % 4 + 1) * 128], wraw[:, k, :],
                                    m["ident"][:]).then_inc(w_turned, 1)
            pe.wait_ge(w_kept, 3)
            pe.wait_ge(rows_loaded, 16 * 7)
            pe.wait_ge(ones_set, 1)

            def turn(k, turns):
                pe.wait_ge(item_loaded[k], (turns + 1) * 16)
                for q in range(GROUP):
                    t = nc.tensor.transpose(bank[k][:, q * T:(q + 1) * T], item_in[k][:, q, :],
                                            m["ident"][0:T, 0:T])
                t.then_inc(item_turned, 1)

            def multiply(k, turns):
                pe.wait_ge(item_kept, turns * 2 + (k + 1))
                pe.wait_ge(item_staged, turns * 2 + (k + 1))
                for q in range(GROUP):
                    t = nc.tensor.matmul(bank[2 + k][0:T, q * D:(q + 1) * D], item_t[k][:, q * T:(q + 1) * T],
                                         m["w_item"][:], start=(q == 0), stop=(q == GROUP - 1),
                                         skip_group_check=True)
                t.then_inc(item_done, 1)

            nc.tensor.matmul(bank[4][0:T, 0:GD], m["ones_row"][0:1, 0:T], brow[0:1].rearrange("a q d -> a (q d)"),
                             start=True, stop=True).then_inc(bias_spread, 1)
            turn(0, 0)
            with pe.Fori(0, GROUPS // 2 - 1) as i:
                turn(1, i)
                multiply(0, i)
                turn(0, i + 1)
                multiply(1, i)
            last = GROUPS // 2 - 1
            turn(1, last)
            multiply(0, last)
            multiply(1, last)

        @block.scalar
        def _(act):
            for k, part in enumerate(x_parts):
                act.dma_start(m["stream"][:, part, :], x_view[:, part, :]).then_inc(x_loaded[k], 16)

            def stage(n, k):
                act.wait_ge(item_turned, n + 1)
                nc.scalar.activation(item_t[k][:], bank[k][:, 0:GT], ACT.Copy).then_inc(item_staged, 1)

            def round_half(n, k):
                act.wait_ge(item_summed, n + 1)
                nc.scalar.activation(m["feats_high"][:, bass.ds(n * GROUP, GROUP), :], items[k][:], ACT.Copy
                                     ).then_inc(item_high, 1)
            stage(0, 0)
            stage(1, 1)
            with act.Fori(0, GROUPS // 2 - 1) as i:
                for k in range(2):
                    round_half(i * 2 + k, k)
                    stage(i * 2 + (2 + k), k)
            for k in range(2):
                round_half(GROUPS - 2 + k, k)

        @block.vector
        def _(dve):
            nc.vector.memset(m["ones_row"][:], 1.0).then_inc(ones_set, 1)
            nc.vector.memset(m["zero_row"][:], 0.0)
            dve.wait_ge(w_turned, 10)
            nc.vector.tensor_copy(m["w_item"][:], bank[0][:, 0:128]).then_inc(w_kept, 1)
            nc.vector.tensor_copy(m["w_user"][:], bank[0][:, 128:256])
            nc.vector.tensor_copy(m["w_ih"][:, 0:256], bank[0][:, 256:512])
            nc.vector.tensor_copy(m["w_ih"][:, 256:512], bank[1][:, 0:256])
            nc.vector.tensor_copy(m["w_hh"][:, 0:256], bank[1][:, 256:512]).then_inc(w_kept, 1)
            dve.sem_inc(item_kept, 2)
            nc.vector.tensor_copy(m["w_hh"][:, 256:512], bank[2][:, 0:256]).then_inc(w_kept, 1)
            dve.wait_ge(rows_loaded, 16 * 7)
            nc.vector.tensor_tensor(m["gate_b"][:], m["gate_b"][:], b2[:], ALU.add)
            dve.wait_ge(bias_spread, 1)
            nc.vector.tensor_copy(bias[:].rearrange("p q d -> p (q d)"), bank[4][0:T, 0:GD]).then_inc(bias_kept, 1)
            dve.wait_ge(bias_kept, 1)
            for part in range(X_PARTS):
                turns = GROUPS // 2 // X_PARTS
                dve.wait_ge(x_loaded[part], 16)
                with dve.Fori(part * turns, (part + 1) * turns) as i:
                    for k in range(2):
                        here = bass.ds((i * 2 + k) * GROUP, GROUP)
                        dve.wait_ge(item_done, i * 2 + (k + 1))
                        nc.vector.tensor_tensor(items[k][:], bank[2 + k][0:T, 0:GD].rearrange("p (q d) -> p q d", d=D), bias[:],
                                                ALU.add).then_inc(item_summed, 1)
                        row_statistics(nc, m, (i * 2 + k) * GROUP)
                        dve.wait_ge(item_high, i * 2 + (k + 1))
                        nc.vector.tensor_tensor(m["feats_low"][:, here, :], items[k][:], m["feats_high"][:, here, :].bitcast(F32),
                                                ALU.subtract).then_inc(item_kept, 1)


def row_statistics(nc, m, first, count=GROUP):
    for q in range(count):
        i = nc.vector.bn_stats(m["parts"][:, bass.ds(first + q, 1), :], m["stream"][:, bass.ds(first + q, 1), :])
    return i


def norm_stats(nc, m, turn):
    with ExitStack() as c:
        sb = lambda n, s: c.enter_context(nc.sbuf_tensor(n + f"_{turn}", s, F32))
        var_done, root_done, step = m["stats_sems"]
        var, root, corr = sb("var", [T, TILES]), sb("root", [T, TILES]), sb("corr", [T, TILES])
        parts = m["parts"]
        block = c.enter_context(nc.Block())

        @block.vector
        def _(dve):
            link = chain(dve, step, turn * 11)
            link(nc.vector.tensor_tensor(corr[:], parts[:, :, 1], parts[:, :, 4], ALU.subtract))
            link(nc.vector.tensor_tensor(root[:], corr[:], corr[:], ALU.mult))
            link(nc.vector.tensor_tensor(m["mean"][:], parts[:, :, 1], parts[:, :, 4], ALU.add))
            link(nc.vector.tensor_scalar(m["mean"][:], m["mean"][:], 0.5, None, ALU.mult))
            link(nc.vector.tensor_tensor(var[:], parts[:, :, 2], parts[:, :, 5], ALU.add))
            link(nc.vector.tensor_scalar(var[:], var[:], 1.0 / D, EPS, ALU.mult, ALU.add))
            nc.vector.scalar_tensor_tensor(var[:], root[:], 0.25, var[:], ALU.mult, ALU.add).then_inc(var_done, 1)
            dve.wait_ge(root_done, turn + 1)
            inverse_root(nc, link, m["rstd"][:], root[:], var[:], corr[:])

        @block.scalar
        def _(act):
            act.wait_ge(var_done, turn + 1)
            nc.scalar.activation(root[:], var[:], ACT.Sqrt).then_inc(root_done, 1)


def norm_transposed(nc, m, tag):
    with ExitStack() as c:
        sem = lambda n: c.enter_context(nc.semaphore(n + tag))
        rows_ready, turned, kept = sem("rows_ready"), sem("turned"), sem("kept")
        rows = [c.enter_context(nc.sbuf_tensor(f"rows{k}{tag}", [T, GROUP, D], F32)) for k in range(2)]
        bank = m["bank"]
        block = c.enter_context(nc.Block())

        def normalise(dve, g, k):
            for q in range(GROUP):
                i = nc.vector.tensor_scalar(rows[k][:, q, :], m["stream"][:, bass.ds(g * GROUP + q, 1), :],
                                            m["mean"][:, bass.ds(g * GROUP + q, 1)],
                                            m["rstd"][:, bass.ds(g * GROUP + q, 1)], ALU.subtract, ALU.mult)
            i.then_inc(rows_ready, 1)

        @block.vector
        def _(dve):
            for k in range(2):
                normalise(dve, k, k)
            with dve.Fori(1, GROUPS // 2) as i:
                for k in range(2):
                    dve.wait_ge(turned, i * 2 + (k - 1))
                    normalise(dve, i * 2 + k, k)

        @block.tensor
        def _(pe):
            def turn(n, k):
                pe.wait_ge(rows_ready, n + 1)
                for q in range(GROUP):
                    t = nc.tensor.transpose(bank[k][:, q * T:(q + 1) * T], rows[k][:, q, :], m["ident"][0:T, 0:T])
                t.then_inc(turned, 1)
            for k in range(2):
                turn(k, k)
            with pe.Fori(1, GROUPS // 2) as i:
                for k in range(2):
                    pe.wait_ge(kept, i * 2 + (k - 1))
                    turn(i * 2 + k, k)

        @block.scalar
        def _(act):
            with act.Fori(0, GROUPS // 2) as i:
                for k in range(2):
                    act.wait_ge(turned, i * 2 + (k + 1))
                    nc.scalar.activation(m["norm_t"][:, bass.ds((i * 2 + k) * GT, GT)], bank[k][:, 0:GT],
                                         ACT.Copy).then_inc(kept, 1)


def load_panel(sp, m, adj, g, p):
    rows = adj.rearrange("(t p) c -> p t c", p=T)
    sp.dma_start(m["panel"][p % SLOTS][:], rows[:, bass.ds(g * GROUP, GROUP), p * PCOLS:(p + 1) * PCOLS]
                 ).then_inc(m["panel_loaded"][p % SLOTS], 16)


def first_panels(sp, m, adj):
    for p in range(SLOTS):
        load_panel(sp, m, adj, 0, p)


def adjacency_pass(nc, m, adj, b_user, first):
    tag = "_a" if first else "_b"
    with ExitStack() as c:
        sem = lambda n: c.enter_context(nc.semaphore(n + tag))
        sb = lambda n, s, d=F32: c.enter_context(nc.sbuf_tensor(n + tag, s, d))
        panel, panel_loaded = m["panel"], m["panel_loaded"]
        panel_read, turned, high_staged, low_staged = sem("panel_read"), sem("turned"), sem("high_staged"), sem("low_staged")
        head_done, head_kept, body_done, body_taken = sem("head_done"), sem("head_kept"), sem("body_done"), sem("body_taken")
        relu_done, back_turned, added = sem("relu_done"), sem("back_turned"), sem("added")
        rows_ready, rows_turned, user_staged = sem("rows_ready"), sem("rows_turned"), sem("user_staged")
        act_summed, dve_summed, degree_done, bias_loaded = (
            sem("act_summed"), sem("dve_summed"), sem("degree_done"), sem("bias_loaded"))
        high = [sb(f"high{k}", [T, GT], F32R) for k in range(STAGES)]
        low = [sb(f"low{k}", [T, GT], F32R) for k in range(STAGES)]
        head_sums, total, relu_t = sb("head_sums", [D, GT]), sb("total", [D, GT]), sb("relu_t", [D, GT])
        if first:
            rows, user_t, bias = sb("rows", [T, GROUP, D]), sb("user_t", [D, GT]), sb("bias", [D, 1])
            shares, unread = sb("shares", [T, GROUP, PANELS]), [sb(f"unread{q}", [T, PCOLS]) for q in range(2)]
        bank = m["bank"]
        body, head, scratch, back = bank[4], bank[5], bank[6], bank[7]
        feats_high, feats_low = m["feats_high"], m["feats_low"]
        HEAD = 2 * PB
        LAST = TILES - HEAD - 1
        SPARE = HEAD // PB + 1
        NORM, TURN_ROWS, USER = 8, 14, 20
        KEEP_HEAD = 5
        SUM, RELU, BACK, ADD = 3, 4, 5, 7
        block = c.enter_context(nc.Block())


        @block.sync
        def _(sp):
            if first:
                sp.dma_start(bias[:], b_user.rearrange("(d a) -> d a", a=1), allow_slow_non_contiguous=True
                             ).then_inc(bias_loaded, 16)

            def load(g, p):
                load_panel(sp, m, adj, g, p)

            def slot_free(g, p):
                for reader in (panel_read, act_summed, dve_summed) if first else (panel_read,):
                    sp.wait_ge(reader, g * PANELS + (p + 1))

            with sp.Fori(0, GROUPS - 1) as g:
                for p in range(PANELS):
                    slot_free(g, p)
                    if p < PANELS - SLOTS:
                        load(g, p + SLOTS)
                    else:
                        load(g + 1, p + SLOTS - PANELS)
            for p in range(PANELS - SLOTS):
                slot_free(GROUPS - 1, p)
                load(GROUPS - 1, p + SLOTS)
            for p in range(SPARE):
                slot_free(GROUPS - 1, PANELS - SLOTS + p)
                load(0, p)
            for s in range(SLOTS):
                sp.wait_ge(panel_loaded[s], 16 * (GROUPS * PANELS // SLOTS + (s < SPARE)))

        def panel_ready(engine, g, p):
            engine.wait_ge(panel_loaded[p % SLOTS], (g * (PANELS // SLOTS) + (p // SLOTS + 1)) * 16)

        @block.tensor
        def _(pe):
            def transposes(g, bb):
                b = bb % TILES
                if b % PB == 0:
                    panel_ready(pe, g, bb // PB)
                for q in range(GROUP):
                    t = nc.tensor.transpose(bank[b % STAGES][0:T, q * T:(q + 1) * T],
                                            panel[b // PB % SLOTS][:, q, b % PB * T:(b % PB + 1) * T], m["ident"][0:T, 0:T])
                t.then_inc(turned, 1)

            def products(n, b, sums, start, stop, signal):
                pe.wait_ge(high_staged, n + 1)
                nc.tensor.matmul(sums[:, 0:GT], feats_high[:, b, :], high[b % STAGES][:], start=start, stop=False,
                                 skip_group_check=True)
                i = nc.tensor.matmul(sums[:, 0:GT], feats_low[:, b, :], high[b % STAGES][:], start=False, stop=False,
                                     skip_group_check=True)
                if (b + AHEAD) % PB == PB - 1:
                    i.then_inc(panel_read, 1)
                pe.wait_ge(low_staged, n + 1)
                i = nc.tensor.matmul(sums[:, 0:GT], feats_high[:, b, :], low[b % STAGES][:], start=False, stop=stop,
                                     skip_group_check=True)
                if signal is not None:
                    i.then_inc(signal, 1)

            for b in range(AHEAD):
                transposes(0, b)
            for b in range(HEAD):
                transposes(0, b + AHEAD)
                products(b, b, head, b == 0, b == HEAD - 1, head_done if b == HEAD - 1 else None)
            with pe.Fori(0, GROUPS) as g:
                for b in range(TILES):
                    transposes(g, b + HEAD + AHEAD)
                    if b == 0:
                        pe.wait_ge(body_taken, g + 1)
                    if b == LAST + 1:
                        pe.wait_ge(head_kept, g + 1)
                    at = (b + HEAD) % TILES
                    n = g * TILES + (b + HEAD)
                    if b <= LAST:
                        products(n, at, body, b == 0, b == LAST, body_done if b == LAST else None)
                    else:
                        products(n, at, head, at == 0, at == HEAD - 1, head_done if at == HEAD - 1 else None)
                    if first and b == TURN_ROWS:
                        pe.wait_ge(rows_ready, g + 1)
                        for q in range(GROUP):
                            t = nc.tensor.transpose(scratch[:, q * T:(q + 1) * T], rows[:, q, :], m["ident"][0:T, 0:T])
                        t.then_inc(rows_turned, 1)
                    if first and b == USER:
                        pe.wait_ge(user_staged, g + 1)
                        nc.tensor.matmul(body[:, 0:GT], m["w_user"][:], user_t[:], start=False, stop=False,
                                         skip_group_check=True)
                    if b == LAST + BACK:
                        pe.wait_ge(relu_done, g + 1)
                        for q in range(GROUP):
                            t = nc.tensor.transpose(back[0:T, q * D:(q + 1) * D], relu_t[:, q * T:(q + 1) * T], m["ident"][:])
                        t.then_inc(back_turned, 1)

        @block.scalar
        def _(act):
            def stage(g, b):
                act.wait_ge(turned, g * TILES + (b + 1))
                nc.scalar.activation(high[b % STAGES][:], bank[b % STAGES][0:T, 0:GT], ACT.Copy).then_inc(high_staged, 1)
                if first and b % PB in (0, 2):
                    q, p = b % PB // 2, b // PB
                    if not (isinstance(g, int) and p == 0):
                        act.wait_ge(act_summed, g * PANELS + p)
                    i = nc.scalar.activation(unread[q][:], panel[p % SLOTS][:, q, :], ACT.Copy,
                                             accum_out=shares[:, q, p:p + 1])
                    if q == 1:
                        i.then_inc(act_summed, 1)

            if first:
                act.wait_ge(bias_loaded, 16)
            for b in range(HEAD):
                stage(0, b)
            with act.Fori(0, GROUPS) as g:
                for b in range(TILES):
                    if first and b == LAST + 1:
                        act.wait_ge(degree_done, g + 1)
                    stage(g + 1 if b > LAST else g, (b + HEAD) % TILES)
                    if b == KEEP_HEAD:
                        act.wait_ge(head_done, g + 1)
                        act.wait_ge(body_taken, g + 1)
                        nc.scalar.activation(head_sums[:], head[:, 0:GT], ACT.Copy).then_inc(head_kept, 1)
                    if first and b == TURN_ROWS + 1:
                        act.wait_ge(rows_turned, g + 1)
                        nc.scalar.activation(user_t[:], scratch[:, 0:GT], ACT.Copy).then_inc(user_staged, 1)
                    if b == LAST + RELU:
                        act.wait_ge(body_taken, g + 2)
                        if first:
                            nc.scalar.activation(relu_t[:], total[:], ACT.Relu, bias=bias[:]).then_inc(relu_done, 1)
                        else:
                            nc.scalar.activation(relu_t[:], total[:], ACT.Relu).then_inc(relu_done, 1)

        @block.vector
        def _(dve):
            def stage(n, b):
                dve.wait_ge(high_staged, n + 1)
                nc.vector.tensor_tensor(low[b % STAGES][:], bank[b % STAGES][0:T, 0:GT], high[b % STAGES][:].bitcast(F32),
                                        ALU.subtract).then_inc(low_staged, 1)
                if first and b % PB in (1, 3):
                    q, p = 2 + b % PB // 2, b // PB
                    i = nc.vector.tensor_reduce(shares[:, q, p:p + 1], panel[p % SLOTS][:, q, :], AXX, ALU.add)
                    if q == 3:
                        i.then_inc(dve_summed, 1)

            dve.sem_inc(body_taken, 1)
            for b in range(HEAD):
                stage(b, b)
            with dve.Fori(0, GROUPS) as g:
                for b in range(TILES):
                    stage(g * TILES + (b + HEAD), (b + HEAD) % TILES)
                    if first and b == LAST:
                        dve.wait_ge(act_summed, (g + 1) * PANELS)
                        dve.wait_ge(dve_summed, (g + 1) * PANELS)
                        nc.vector.tensor_reduce(m["degree"][:, bass.ds(g * GROUP, GROUP)], shares[:], AXX, ALU.add
                                                ).then_inc(degree_done, 1)
                    if first and b == NORM:
                        for q in range(GROUP):
                            i = nc.vector.tensor_scalar(rows[:, q, :], m["stream"][:, bass.ds(g * GROUP + q, 1), :],
                                                        m["mean"][:, bass.ds(g * GROUP + q, 1)],
                                                        m["rstd"][:, bass.ds(g * GROUP + q, 1)], ALU.subtract, ALU.mult)
                        i.then_inc(rows_ready, 1)
                    if b == LAST + SUM:
                        dve.wait_ge(body_done, g + 1)
                        dve.wait_ge(head_kept, g + 1)
                        nc.vector.tensor_tensor(total[:], body[:, 0:GT], head_sums[:], ALU.add).then_inc(body_taken, 1)
                    if b == LAST + ADD:
                        dve.wait_ge(back_turned, g + 1)
                        here = m["stream"][:, bass.ds(g * GROUP, GROUP), :]
                        if first:
                            i = nc.vector.tensor_tensor(here, back[0:T, 0:GD].rearrange("p (q d) -> p q d", d=D), here, ALU.add)
                        else:
                            for q in range(GROUP):
                                one = m["stream"][:, bass.ds(g * GROUP + q, 1), :].rearrange("p q d -> p (q d)")
                                i = nc.vector.scalar_tensor_tensor(one, back[0:T, q * D:(q + 1) * D],
                                                                   m["dinv"][:, bass.ds(g * GROUP + q, 1)], one,
                                                                   ALU.mult, ALU.add)
                        i.then_inc(added, 1)
                    if b == LAST + ADD + 1:
                        dve.wait_ge(added, g + 1)
                        row_statistics(nc, m, g * GROUP)


def common(nc, c):
    sb = lambda n, s: c.enter_context(nc.sbuf_tensor(n, s, F32))
    return {
        "stats_sems": [c.enter_context(nc.semaphore(n)) for n in ("var_done", "root_done", "stats_step")],
        "bank": [c.enter_context(nc.psum_tensor(f"bank{k}", [128, 512], F32)) for k in range(8)],
        "ident": sb("ident", [128, 128]),
        "stream": sb("stream", [T, TILES, D]),
        "parts": sb("parts", [T, TILES, 6]), "mean": sb("mean", [T, TILES]), "rstd": sb("rstd", [T, TILES]),
        "degree": sb("degree", [T, TILES]), "dinv": sb("dinv", [T, TILES]),
        "w_item": sb("w_item", [D, D]), "w_user": sb("w_user", [D, D]), "gnn_w": sb("gnn_w", [D, D]),
        "w_ih": sb("w_ih", [D, 512]), "w_hh": sb("w_hh", [D, 512]), "gate_b": sb("gate_b", [D, 4]),
        "ones_row": sb("ones_row", [1, 128]), "zero_row": sb("zero_row", [1, 2, DE]),
    }


CHUNKS = 200
STEPS = N // CHUNKS
LANES = [(0, CHUNKS // 2), (CHUNKS // 2, CHUNKS)]
TOLERANCE = 1e-6
SURE = 2


def lstm(nc, m):
    with ExitStack() as c:
        sem = lambda n: c.enter_context(nc.semaphore(n + "_l"))
        sb = lambda n, s, d=F32: c.enter_context(nc.sbuf_tensor(n + "_l", s, d))
        prepared, sweep_open, compared = sem("prepared"), sem("sweep_open"), sem("compared")
        gates_summed = [sem(f"gates_summed{k}") for k in range(2)]
        gates_read = [sem(f"gates_read{k}") for k in range(2)]
        gates_done = [sem(f"gates_done{k}") for k in range(2)]
        parts_done = [sem(f"parts_done{k}") for k in range(2)]
        cell_done = [sem(f"cell_done{k}") for k in range(2)]
        tanh_done = [sem(f"tanh_done{k}") for k in range(2)]
        u_done = [sem(f"u_done{k}") for k in range(2)]
        marked, counted, flag_set = sem("marked"), sem("counted"), sem("flag_set")
        W = [hi - lo for lo, hi in LANES]
        pre = [sb(f"pre{k}", [D, 4, W[k]]) for k in range(2)]
        gate = [sb(f"gate{k}", [D, 4, W[k]]) for k in range(2)]
        keep = [sb(f"keep{k}", [D, W[k]]) for k in range(2)]
        put = [sb(f"put{k}", [D, W[k]]) for k in range(2)]
        tc = [sb(f"tc{k}", [D, W[k]]) for k in range(2)]
        cell = sb("cell", [D, CHUNKS])
        cell_start, u_start = sb("cell_start", [D, CHUNKS]), sb("u_start", [D, CHUNKS])
        near = sb("near", [D, 2, CHUNKS - 1])
        ones_col, total, flag = sb("ones_col", [D, 1]), sb("total", [1, 1]), sb("flag", [1, 1], I32)
        sums = [[m["bank"][0], m["bank"][1]], [m["bank"][2], m["bank"][3]]]
        tally = m["bank"][4]
        inputs = m["norm_t"][:].rearrange("p (c l) -> p c l", l=STEPS)
        u_before = m["doubled_t"][:, 0:N].rearrange("p (c l) -> p c l", l=STEPS)
        u_now = m["doubled_t"][:, 1:N + 1].rearrange("p (c l) -> p c l", l=STEPS)
        I, F, G, O = range(4)
        block = c.enter_context(nc.Block())

        @block.tensor
        def _(pe):
            def sweep(s):
                with pe.Fori(0, STEPS // 2) as pair:
                    for odd in range(2):
                        t = pair * 2 + odd
                        for k, (lo, hi) in enumerate(LANES):
                            bank = sums[k][odd][:, 0:4 * W[k]].rearrange("p (g c) -> p g c", g=4)
                            for g in range(4):
                                nc.tensor.matmul(bank[:, g, :], m["w_ih"][:, g * D:(g + 1) * D],
                                                 inputs[:, lo:hi, bass.ds(t, 1)],
                                                 start=(g == 0), stop=False, skip_group_check=True)
                            pe.wait_ge(u_done[k], s * (STEPS + 1) + t + 1)
                            for g in range(4):
                                i = nc.tensor.matmul(bank[:, g, :], m["w_hh"][:, g * D:(g + 1) * D],
                                                     u_before[:, lo:hi, bass.ds(t, 1)],
                                                     start=False, stop=(g == 3), skip_group_check=True)
                            i.then_inc(gates_summed[k], 1)
                pe.wait_ge(marked, s + 1)
                nc.tensor.matmul(tally[0:1, 0:2 * (CHUNKS - 1)], ones_col[:], near[:].rearrange("p a c -> p (a c)"),
                                 start=True, stop=True).then_inc(counted, 1)

            pe.wait_ge(prepared, 1)
            with pe.Fori(0, SURE) as s:
                sweep(s)
            pe.wait_ge(flag_set, 1)
            unsettled = pe.value_load(flag[0:1, 0:1])
            with pe.If(unsettled > 0):
                sweep(SURE)
            pe.wait_ge(flag_set, 2)
            still_unsettled = pe.value_load(flag[0:1, 0:1])
            with pe.If(still_unsettled > 0):
                with pe.Fori(SURE + 1, CHUNKS) as s:
                    sweep(s)

        @block.scalar
        def _(act):
            def gates(k, n):
                act.wait_ge(gates_read[k], n + 1)
                nc.scalar.activation(gate[k][:], pre[k][:], ACT.Tanh).then_inc(gates_done[k], 1)

            def squash(k, n):
                lo, hi = LANES[k]
                act.wait_ge(cell_done[k], n + 1)
                nc.scalar.activation(tc[k][:], cell[:, lo:hi], ACT.Tanh, scale=0.5).then_inc(tanh_done[k], 1)

            def sweep(s):
                gates(0, s * STEPS)
                squash(0, s * STEPS)
                gates(1, s * STEPS)
                with act.Fori(1, STEPS) as t:
                    squash(1, s * STEPS + t - 1)
                    gates(0, s * STEPS + t)
                    squash(0, s * STEPS + t)
                    gates(1, s * STEPS + t)
                squash(1, s * STEPS + (STEPS - 1))

            with act.Fori(0, SURE) as s:
                sweep(s)
            act.wait_ge(flag_set, 1)
            unsettled = act.value_load(flag[0:1, 0:1])
            with act.If(unsettled > 0):
                sweep(SURE)
            act.wait_ge(flag_set, 2)
            still_unsettled = act.value_load(flag[0:1, 0:1])
            with act.If(still_unsettled > 0):
                with act.Fori(SURE + 1, CHUNKS) as s:
                    sweep(s)

        @block.vector
        def _(dve):
            for w, gain in ((m["w_ih"], 0.5), (m["w_hh"], 0.25)):
                nc.vector.tensor_scalar(w[:, 0:2 * D], w[:, 0:2 * D], gain, None, ALU.mult)
                nc.vector.tensor_scalar(w[:, 3 * D:4 * D], w[:, 3 * D:4 * D], gain, None, ALU.mult)
            nc.vector.tensor_scalar(m["w_hh"][:, 2 * D:3 * D], m["w_hh"][:, 2 * D:3 * D], 0.5, None, ALU.mult)
            nc.vector.tensor_scalar(m["gate_b"][:, 0:2], m["gate_b"][:, 0:2], 0.5, None, ALU.mult)
            nc.vector.tensor_scalar(m["gate_b"][:, 3:4], m["gate_b"][:, 3:4], 0.5, None, ALU.mult)
            nc.vector.memset(u_before[:, :, 0], 0.0)
            nc.vector.memset(cell_start[:], 0.0)
            nc.vector.memset(u_start[:], 0.0)
            nc.vector.memset(ones_col[:], 1.0).then_inc(prepared, 1)
            dve.wait_ge(prepared, 1)

            def take(k, n, odd):
                dve.wait_ge(gates_summed[k], n + 1)
                bank = sums[k][odd][:, 0:4 * W[k]].rearrange("p (g c) -> p g c", g=4)
                bias = m["gate_b"][:].rearrange("p (g a) -> p g a", a=1).to_broadcast([D, 4, W[k]])
                nc.vector.tensor_tensor(pre[k][:], bank, bias, ALU.add).then_inc(gates_read[k], 1)

            def update(k, n):
                lo, hi = LANES[k]
                dve.wait_ge(gates_done[k], n + 1)
                nc.vector.scalar_tensor_tensor(put[k][:], gate[k][:, I, :], 1.0, gate[k][:, G, :], ALU.add, ALU.mult)
                nc.vector.scalar_tensor_tensor(keep[k][:], gate[k][:, F, :], 1.0, cell[:, lo:hi], ALU.add, ALU.mult
                                               ).then_inc(parts_done[k], 1)
                dve.wait_ge(parts_done[k], n + 1)
                nc.vector.scalar_tensor_tensor(cell[:, lo:hi], keep[k][:], 0.5, put[k][:], ALU.mult, ALU.add
                                               ).then_inc(cell_done[k], 1)

            def emit(k, n, t):
                lo, hi = LANES[k]
                dve.wait_ge(tanh_done[k], n + 1)
                nc.vector.scalar_tensor_tensor(u_now[:, lo:hi, t] if isinstance(t, int) else u_now[:, lo:hi, bass.ds(t, 1)],
                                               gate[k][:, O, :], 1.0, tc[k][:], ALU.add, ALU.mult).then_inc(u_done[k], 1)

            def sweep(s):
                nc.vector.tensor_copy(cell[:], cell_start[:]).then_inc(sweep_open, 1)
                dve.wait_ge(sweep_open, s + 1)
                dve.sem_inc(u_done[0], 1)
                dve.sem_inc(u_done[1], 1)
                n = s * STEPS
                take(0, n, 0)
                update(0, n)
                take(1, n, 0)
                emit(0, n, 0)

                def step_of(t, odd):
                    n = s * STEPS + t
                    update(1, n - 1)
                    take(0, n, odd)
                    emit(1, n - 1, t - 1)
                    update(0, n)
                    take(1, n, odd)
                    emit(0, n, t)
                with dve.Fori(0, STEPS // 2 - 1) as pair:
                    step_of(pair * 2 + 1, 1)
                    step_of(pair * 2 + 2, 0)
                step_of(STEPS - 1, 1)
                n = s * STEPS + (STEPS - 1)
                update(1, n)
                emit(1, n, STEPS - 1)
                dve.wait_ge(u_done[1], n + s + 2)
                step = [0]

                def after(i):
                    step[0] = step[0] + 1
                    i.then_inc(compared, 1)
                    dve.wait_ge(compared, s * 8 + step[0])
                last = CHUNKS - 1
                after(nc.vector.tensor_tensor(near[:, 0, :], u_before[:, 1:CHUNKS, 0], u_start[:, 1:CHUNKS], ALU.subtract))
                after(nc.vector.tensor_tensor(near[:, 1, :], cell[:, 0:last], cell_start[:, 1:CHUNKS], ALU.subtract))
                after(nc.vector.tensor_tensor(near[:], near[:], near[:], ALU.mult))
                after(nc.vector.tensor_copy(u_start[:, 1:CHUNKS], u_before[:, 1:CHUNKS, 0]))
                after(nc.vector.tensor_copy(cell_start[:, 1:CHUNKS], cell[:, 0:last]))
                nc.vector.tensor_scalar(near[:], near[:], TOLERANCE * TOLERANCE, None, ALU.is_le).then_inc(marked, 1)
                dve.wait_ge(counted, s + 1)
                after(nc.vector.tensor_reduce(total[:], tally[0:1, 0:2 * last], AXX, ALU.add))
                after(nc.vector.tensor_scalar(total[:], total[:], -1.0, float(2 * last * D), ALU.mult, ALU.add))
                after(nc.vector.tensor_copy(flag[:], total[:]))

            with dve.Fori(0, SURE) as s:
                sweep(s)
            dve.sem_inc(flag_set, 1)
            unsettled = dve.value_load(flag[0:1, 0:1])
            with dve.If(unsettled > 0):
                sweep(SURE)
            dve.sem_inc(flag_set, 1)
            still_unsettled = dve.value_load(flag[0:1, 0:1])
            with dve.If(still_unsettled > 0):
                with dve.Fori(SURE + 1, CHUNKS) as s:
                    sweep(s)


def mix(nc, m, W_lin, b_lin, fw_att, bw_att):
    with ExitStack() as c:
        sem = lambda n: c.enter_context(nc.semaphore(n + "_m"))
        sb = lambda n, s: c.enter_context(nc.sbuf_tensor(n + "_m", s, F32))
        loaded, prepared, thr_made, step = sem("loaded"), sem("prepared"), sem("thr_made"), sem("step")
        logits, gated, scanned, summed = sem("logits"), sem("gated"), sem("scanned"), sem("summed")
        shifted, turned, added, total_known = sem("shifted"), sem("turned"), sem("added"), sem("total_known")
        parted, own_scaled = sem("parted"), sem("own_scaled")
        k_times_own = [sb(f"k_times_own{k}", [D, GT]) for k in range(2)]
        w_lin, fw, bw, b_row = sb("w_lin", [D, 2]), sb("fw", [D, 1]), sb("bw", [D, 1]), sb("b_row", [1, 2])
        w_diff, thr = sb("w_diff", [D, 128]), sb("thr", [D, 1])
        k_inc, k_own, k_total = sb("k_inc", [D, 1]), sb("k_own", [D, 1]), sb("k_total", [D, 1])
        ones = sb("ones", [D, GT])
        own = [sb(f"own{k}", [D, GT]) for k in range(2)]
        inc = [sb(f"inc{k}", [D, GT]) for k in range(2)]
        part = [sb(f"part{k}", [D, GT]) for k in range(2)]
        moved = [sb(f"moved{k}", [D, GT]) for k in range(2)]
        bank = m["bank"]
        u = m["doubled_t"][:, 1:N + 1]
        block = c.enter_context(nc.Block())

        @block.sync
        def _(sp):
            sp.dma_start(w_lin[:], W_lin.rearrange("l d -> d l"), allow_slow_non_contiguous=True).then_inc(loaded, 16)
            sp.dma_start(fw[:], fw_att.rearrange("a d -> d a"), allow_slow_non_contiguous=True).then_inc(loaded, 16)
            sp.dma_start(bw[:], bw_att.rearrange("a d -> d a"), allow_slow_non_contiguous=True).then_inc(loaded, 16)
            sp.dma_start(b_row[:], b_lin.rearrange("(a l) -> a l", a=1)).then_inc(loaded, 16)

        @block.tensor
        def _(pe):
            pe.wait_ge(prepared, 2)
            nc.tensor.matmul(bank[2][:, 0:1], m["ones_row"][0:1, :], b_row[0:1, 0:1],
                             start=True, stop=True).then_inc(thr_made, 1)
            with pe.Fori(0, GROUPS // 2) as i:
                for k in range(2):
                    pe.wait_ge(gated, i * 2 + (k + 1))
                    nc.tensor.matmul(bank[k][:, 0:GT], w_diff[:], u[:, bass.ds((i * 2 + k) * GT, GT)],
                                     start=True, stop=True).then_inc(logits, 1)
            with pe.Fori(0, GROUPS // 2) as i:
                for k in range(2):
                    pe.wait_ge(shifted, i * 2 + (k + 1))
                    pe.wait_ge(added, i * 2 + (k + 1))
                    for q in range(GROUP):
                        t = nc.tensor.transpose(bank[3 + k][0:T, q * D:(q + 1) * D], moved[k][:, q * T:(q + 1) * T],
                                                m["ident"][:])
                    t.then_inc(turned, 1)

        @block.vector
        def _(dve):
            link = chain(dve, step)
            dve.wait_ge(loaded, 64)
            link(nc.vector.memset(ones[:], 1.0))
            link(nc.vector.tensor_tensor(w_lin[:, 0:1], w_lin[:, 1:2], w_lin[:, 0:1], ALU.subtract))
            nc.vector.tensor_scalar(w_diff[:], ones[:, 0:128], w_lin[:, 0:1], None, ALU.mult).then_inc(prepared, 1)
            link(nc.vector.tensor_tensor(b_row[0:1, 0:1], b_row[0:1, 0:1], b_row[0:1, 1:2], ALU.subtract))
            nc.vector.tensor_scalar(b_row[0:1, 0:1], b_row[0:1, 0:1], 2.0, None, ALU.mult).then_inc(prepared, 1)
            link(nc.vector.tensor_tensor(k_inc[:], fw[:], bw[:], ALU.subtract))
            nc.vector.tensor_scalar(k_inc[:], k_inc[:], 0.5, None, ALU.mult)
            nc.vector.tensor_scalar(k_own[:], fw[:], -0.5, None, ALU.mult)
            nc.vector.tensor_scalar(k_total[:], bw[:], 0.5, None, ALU.mult)
            nc.vector.memset(inc[1][:], 0.0)
            dve.wait_ge(thr_made, 1)
            link(nc.vector.tensor_copy(thr[:], bank[2][:, 0:1]))
            dve.sem_inc(gated, 2)
            dve.sem_inc(summed, 2)
            dve.sem_inc(parted, 2)
            dve.sem_inc(added, 2)
            dve.sem_inc(turned, 2)
            def gate_and_scan(n, k):
                dve.wait_ge(logits, n + 1)
                nc.vector.scalar_tensor_tensor(own[k][:], bank[k][:, 0:GT], thr[:], u[:, bass.ds(n * GT, GT)],
                                               ALU.is_gt, ALU.mult).then_inc(gated, 1)
                dve.wait_ge(gated, n + 3)
                nc.vector.tensor_tensor_scan(inc[k][:], ones[:], own[k][:], inc[1 - k][:, GT - 1:GT], ALU.mult, ALU.add
                                             ).then_inc(scanned, 1)

            def finish(n, k):
                dve.wait_ge(parted, n + 3)
                dve.wait_ge(scanned, n + 1)
                nc.vector.scalar_tensor_tensor(u[:, bass.ds(n * GT, GT)], inc[k][:], k_inc[:], part[k][:],
                                               ALU.mult, ALU.add).then_inc(summed, 1)

            gate_and_scan(0, 0)
            with dve.Fori(0, GROUPS // 2 - 1) as i:
                gate_and_scan(i * 2 + 1, 1)
                finish(i * 2, 0)
                gate_and_scan(i * 2 + 2, 0)
                finish(i * 2 + 1, 1)
            gate_and_scan(GROUPS - 1, 1)
            finish(GROUPS - 2, 0)
            finish(GROUPS - 1, 1)
            nc.vector.tensor_tensor(k_total[:], k_total[:], inc[1][:, GT - 1:GT], ALU.mult).then_inc(total_known, 1)
            with dve.Fori(0, GROUPS // 2) as i:
                for k in range(2):
                    n = i * 2 + k
                    dve.wait_ge(turned, n + 3)
                    here = m["stream"][:, bass.ds(n * GROUP, GROUP), :]
                    nc.vector.tensor_tensor(here, bank[3 + k][0:T, 0:GD].rearrange("p (q d) -> p q d", d=D), here, ALU.add
                                            ).then_inc(added, 1)
                    dve.wait_ge(added, n + 3)
                    row_statistics(nc, m, n * GROUP)

        @block.gpsimd
        def _(pool):
            with pool.Fori(0, GROUPS // 2) as i:
                for k in range(2):
                    n = i * 2 + k
                    pool.wait_ge(summed, n + 1)
                    pool.wait_ge(own_scaled, n + 1)
                    nc.gpsimd.tensor_tensor(part[k][:], k_times_own[k][:], u[:, bass.ds(n * GT, GT)], ALU.add
                                            ).then_inc(parted, 1)

        @block.scalar
        def _(act):
            with act.Fori(0, GROUPS // 2) as i:
                for k in range(2):
                    n = i * 2 + k
                    act.wait_ge(parted, n + 1)
                    act.wait_ge(gated, n + 3)
                    nc.scalar.activation(k_times_own[k][:], own[k][:], ACT.Copy, scale=k_own[:]).then_inc(own_scaled, 1)
            act.wait_ge(total_known, 1)
            with act.Fori(0, GROUPS // 2) as i:
                for k in range(2):
                    n = i * 2 + k
                    act.wait_ge(turned, n + 1)
                    nc.scalar.activation(moved[k][:], u[:, bass.ds(n * GT, GT)], ACT.Identity, bias=k_total[:]
                                         ).then_inc(shifted, 1)


def graph_features(nc, m, adj):
    with ExitStack() as c:
        sem = lambda n: c.enter_context(nc.semaphore(n + "_f"))
        sb = lambda n, s: c.enter_context(nc.sbuf_tensor(n + "_f", s, F32))
        rooted, step, rows_ready, turned, kept, made, stored = (
            sem("rooted"), sem("step"), sem("rows_ready"), sem("turned"), sem("kept"), sem("made"), sem("stored"))
        rows = [sb(f"rows{k}", [T, GROUP, D]) for k in range(2)]
        norm_t = [sb(f"norm_t{k}", [D, GT]) for k in range(2)]
        root, spare = sb("root", [T, TILES]), sb("spare", [T, TILES])
        bank = m["bank"]
        feats = [sb(f"feats{k}", [T, GROUP, D]) for k in range(2)]
        scaled, high_made = sem("scaled"), sem("high_made")
        block = c.enter_context(nc.Block())

        @block.sync
        def _(sp):
            first_panels(sp, m, adj)

        @block.vector
        def _(dve):
            link = chain(dve, step)
            dve.wait_ge(rooted, 1)
            inverse_root(nc, link, m["dinv"][:], root[:], m["degree"][:], spare[:])

            def normalise(g, k):
                for q in range(GROUP):
                    i = nc.vector.tensor_scalar(rows[k][:, q, :], m["stream"][:, bass.ds(g * GROUP + q, 1), :],
                                                m["mean"][:, bass.ds(g * GROUP + q, 1)],
                                                m["rstd"][:, bass.ds(g * GROUP + q, 1)], ALU.subtract, ALU.mult)
                i.then_inc(rows_ready, 1)

            def scale_rows(g, k):
                dve.wait_ge(made, g + 1)
                scale = m["dinv"][:, bass.ds(g * GROUP, GROUP)].rearrange("p (q a) -> p q a", a=1).to_broadcast([T, GROUP, D])
                nc.vector.tensor_tensor(feats[k][:], bank[2 + k][0:T, 0:GD].rearrange("p (q d) -> p q d", d=D), scale, ALU.mult
                                        ).then_inc(scaled, 1)

            def store(g, k):
                here = bass.ds(g * GROUP, GROUP)
                dve.wait_ge(high_made, g + 1)
                nc.vector.tensor_tensor(m["feats_low"][:, here, :], feats[k][:], m["feats_high"][:, here, :].bitcast(F32),
                                        ALU.subtract).then_inc(stored, 1)

            normalise(0, 0)
            normalise(1, 1)
            scale_rows(0, 0)
            with dve.Fori(0, GROUPS // 2 - 1) as i:
                for k in range(2):
                    dve.wait_ge(turned, i * 2 + (k + 1))
                    normalise(i * 2 + (2 + k), k)
                    store(i * 2 + k, k)
                    scale_rows(i * 2 + (1 + k), 1 - k)
            store(GROUPS - 2, 0)
            scale_rows(GROUPS - 1, 1)
            store(GROUPS - 1, 1)

        @block.tensor
        def _(pe):
            def turn(n, k):
                pe.wait_ge(rows_ready, n + 1)
                for q in range(GROUP):
                    t = nc.tensor.transpose(bank[k][:, q * T:(q + 1) * T], rows[k][:, q, :], m["ident"][0:T, 0:T])
                t.then_inc(turned, 1)

            def multiply(n, k, free):
                pe.wait_ge(kept, n + 1)
                if free is not None:
                    pe.wait_ge(scaled, free)
                for q in range(GROUP):
                    t = nc.tensor.matmul(bank[2 + k][0:T, q * D:(q + 1) * D], norm_t[k][:, q * T:(q + 1) * T], m["gnn_w"][:],
                                         start=(q == 0), stop=(q == GROUP - 1), skip_group_check=True)
                t.then_inc(made, 1)

            turn(0, 0)
            turn(1, 1)
            multiply(0, 0, None)
            with pe.Fori(0, GROUPS // 2 - 1) as i:
                multiply(i * 2 + 1, 1, i * 2 + 1)
                turn(i * 2 + 2, 0)
                multiply(i * 2 + 2, 0, i * 2 + 1)
                turn(i * 2 + 3, 1)
            multiply(GROUPS - 1, 1, GROUPS - 2)

        @block.scalar
        def _(act):
            nc.scalar.activation(root[:], m["degree"][:], ACT.Sqrt).then_inc(rooted, 1)

            def keep(n, k):
                act.wait_ge(turned, n + 1)
                nc.scalar.activation(norm_t[k][:], bank[k][:, 0:GT], ACT.Copy).then_inc(kept, 1)

            def round_half(n, k):
                act.wait_ge(scaled, n + 1)
                nc.scalar.activation(m["feats_high"][:, bass.ds(n * GROUP, GROUP), :], feats[k][:], ACT.Copy
                                     ).then_inc(high_made, 1)
            keep(0, 0)
            keep(1, 1)
            with act.Fori(0, GROUPS // 2 - 1) as i:
                for k in range(2):
                    round_half(i * 2 + k, k)
                    keep(i * 2 + (2 + k), k)
            for k in range(2):
                round_half(GROUPS - 2 + k, k)


HEADS, HP, SL = 8, 64, 64
HID = HEADS * HP
HS = HEADS * SL
KC = HID // 128


def slice_weights(nc, m, W_fx, b_fx, W_x, b_x, W_slice, b_slice, temperature, fcD_w, hy_in_w, hy_out_w, out_w):
    with ExitStack() as c:
        sem = lambda n: c.enter_context(nc.semaphore(n + "_w"))
        sb = lambda n, s: c.enter_context(nc.sbuf_tensor(n + "_w", s, F32))
        loaded, turned, kept, step, temp_ready, temp_made, products = (
            sem("loaded"), sem("turned"), sem("kept"), sem("step"), sem("temp_ready"), sem("temp_made"), sem("products"))
        in_raw, in_last = sb("in_raw", [128, 9, HID]), sb("in_last", [16, HID])
        out_raw, o_raw, fx_raw = sb("out_raw", [128, KC, HID]), sb("o_raw", [128, HID]), sb("fx_raw", [128, KC, D])
        fcd_raw, x_raw, s_raw, s_t = sb("fcd_raw", [HEADS, HID]), sb("x_raw", [HP, HEADS, D]), sb("s_raw", [SL, HP]), sb("s_t", [HP, SL])
        bx, t_row, t_wide, bs_row = sb("bx", [HP, HEADS]), sb("t_row", [1, HEADS]), sb("t_wide", [1, HS]), sb("bs_row", [1, HS])
        t_all = sb("t_all", [128, HS])
        bank = m["bank"]
        row = lambda v: v.rearrange("(a d) -> a d", a=1)
        turns = [(s_t[:], s_raw[:], SL, HP)]
        for k in range(KC):
            turns.append((m["w_fx"][:, k * 128:(k + 1) * 128], fx_raw[:, k, :], 128, D))
            turns.append((m["fcd"][:, k, :], fcd_raw[:, k * 128:(k + 1) * 128], HEADS, 128))
            for r in range(9):
                turns.append((m["w_in"][:, k, r * 128:(r + 1) * 128], in_raw[:, r, k * 128:(k + 1) * 128], 128, 128))
            turns.append((m["w_in"][:, k, 1152:1168], in_last[:, k * 128:(k + 1) * 128], 16, 128))
            for r in range(KC):
                turns.append((m["w_mix"][:, k, r * 128:(r + 1) * 128], out_raw[:, r, k * 128:(k + 1) * 128], 128, 128))
        for h in range(HEADS):
            turns.append((m["w_out"][:, h, :], o_raw[:, h * HP:(h + 1) * HP], 128, HP))
        loads = 9 + 2
        block = c.enter_context(nc.Block())

        @block.sync
        def _(sp):
            sp.dma_start(s_raw[:], W_slice).then_inc(loaded, 16)
            sp.dma_start(fx_raw[:], W_fx.rearrange("(k p) d -> p k d", p=128)).then_inc(loaded, 16)
            sp.dma_start(fcd_raw[:], fcD_w).then_inc(loaded, 16)
            sp.dma_start(in_raw[:], hy_in_w[0:1152].rearrange("(r p) d -> p r d", p=128)).then_inc(loaded, 16)
            sp.dma_start(in_last[:], hy_in_w[1152:1168]).then_inc(loaded, 16)
            sp.dma_start(out_raw[:], hy_out_w.rearrange("(r p) d -> p r d", p=128)).then_inc(loaded, 16)
            sp.dma_start(o_raw[:], out_w).then_inc(loaded, 16)
            sp.dma_start(x_raw[:], W_x.rearrange("(h p) d -> p h d", p=HP)).then_inc(loaded, 16)
            sp.dma_start(bx[:], b_x.rearrange("(h p) -> p h", p=HP), allow_slow_non_contiguous=True).then_inc(loaded, 16)
            sp.dma_start(t_row[:], temperature.rearrange("a h b c -> a (h b c)")).then_inc(loaded, 16)
            sp.dma_start(m["b_fx"][:], row(b_fx)).then_inc(loaded, 16)
            for h in range(HEADS):
                sp.dma_start(bs_row[0:1, h * SL:(h + 1) * SL], row(b_slice)).then_inc(loaded, 16)

        @block.tensor
        def _(pe):
            pe.wait_ge(loaded, 16 * (loads + HEADS))
            for n, (dst, src, r, cc) in enumerate(turns):
                if n >= 4:
                    pe.wait_ge(kept, n - 3)
                nc.tensor.transpose(bank[n % 4][0:cc, 0:r], src, m["ident"][0:r, 0:r]).then_inc(turned, 1)
            pe.wait_ge(kept, len(turns))
            pe.wait_ge(temp_ready, 1)
            nc.tensor.matmul(bank[4][:, :], m["ones_row"][:], t_wide[:], start=True, stop=True).then_inc(temp_made, 1)
            for h in range(HEADS):
                nc.tensor.matmul(bank[5][:, h * SL:(h + 1) * SL], x_raw[:, h, :], s_t[:],
                                 start=(h == 0), stop=(h == HEADS - 1), skip_group_check=True)
            for h in range(HEADS):
                i = nc.tensor.matmul(bank[6][0:1, h * SL:(h + 1) * SL], bx[:, h:h + 1], s_t[:],
                                     start=(h == 0), stop=(h == HEADS - 1), skip_group_check=True)
            i.then_inc(products, 1)

        @block.vector
        def _(dve):
            for n, (dst, src, r, cc) in enumerate(turns):
                dve.wait_ge(turned, n + 1)
                nc.vector.tensor_copy(dst, bank[n % 4][0:cc, 0:r]).then_inc(kept, 1)
            link = chain(dve, step)
            link(nc.vector.tensor_scalar(t_row[:], t_row[:], 1e-6, None, ALU.max))
            link(nc.vector.reciprocal(t_row[:], t_row[:]))
            nc.vector.tensor_copy(t_wide[:].rearrange("a (h g) -> a h g", g=SL),
                                  t_row[:].rearrange("a (h b) -> a h b", b=1).to_broadcast([1, HEADS, SL])).then_inc(temp_ready, 1)
            dve.wait_ge(temp_made, 1)
            link(nc.vector.tensor_copy(t_all[:], bank[4][:, :]))
            dve.wait_ge(products, 1)
            nc.vector.tensor_tensor(m["w_logit"][:], bank[5][:, :], t_all[:], ALU.mult)
            link(nc.vector.tensor_tensor(bs_row[:], bank[6][0:1, :], bs_row[:], ALU.add))
            link(nc.vector.tensor_tensor(bs_row[:], bs_row[:], t_wide[:], ALU.mult))
            link(nc.vector.tensor_copy(m["b_logit"][0:1, 0, :], bs_row[:]))
            nc.vector.tensor_tensor(m["b_logit"][0:1, 1, :], bs_row[:], m["b_logit"][0:1, 0, :].bitcast(F32), ALU.subtract)
            nc.vector.tensor_copy(m["ones_r"][:], m["ones_row"][:])


RING = 8


def slice_tokens(nc, m, scratch):
    with ExitStack() as c:
        sem = lambda n: c.enter_context(nc.semaphore(n + "_s"))
        sb = lambda n, s: c.enter_context(nc.sbuf_tensor(n + "_s", s, F32))
        rows_ready, turned, kept, logits, maxed, lessened, exped, summed, inverted, weighed = (
            sem("rows_ready"), sem("turned"), sem("kept"), sem("logits"), sem("maxed"), sem("lessened"), sem("exped"),
            sem("summed"), sem("inverted"), sem("weighed"))
        w_turned, w_kept = sem("w_turned"), sem("w_kept")
        w_stored = [sem(f"w_stored{k}") for k in range(2)]
        rows = [sb(f"rows{k}", [T, DE]) for k in range(RING)]
        norm_t = [sb(f"norm_t{k}", [D, T]) for k in range(4)]
        less = [sb(f"less{k}", [T, HEADS, SL]) for k in range(4)]
        weight = [sb(f"weight{k}", [T, HEADS, SL]) for k in range(4)]
        peak = [sb(f"peak{k}", [T, HEADS]) for k in range(2)]
        share = [sb(f"share{k}", [T, HEADS]) for k in range(4)]
        weight_t = [sb(f"weight_t{k}", [128, KC, T]) for k in range(2)]
        bank = m["bank"]
        block = c.enter_context(nc.Block())
        wide = lambda v: v[:].rearrange("p (h a) -> p h a", a=1).to_broadcast([T, HEADS, SL])

        def all_tiles(engine, step):
            for n in range(RING):
                step(n, n)
            with engine.Fori(1, TILES // RING - 1) as i:
                for r in range(RING):
                    step(i * RING + r, r)
            for n in range(TILES - RING, TILES):
                step(n, n % RING)

        def exists(n):
            return not isinstance(n, int) or 0 <= n < TILES

        def wait_from(engine, s, value):
            if not isinstance(value, int) or value > 0:
                engine.wait_ge(s, value)

        @block.vector
        def _(dve):
            for k in range(RING):
                nc.vector.memset(rows[k][:, D:DE], 1.0)

            def normalise(n, r):
                wait_from(dve, w_turned, n - (RING - 1))
                nc.vector.tensor_scalar(rows[r][:, 0:D], m["stream"][:, bass.ds(n, 1), :].rearrange("p a d -> p (a d)"),
                                        m["mean"][:, bass.ds(n, 1)], m["rstd"][:, bass.ds(n, 1)],
                                        ALU.subtract, ALU.mult).then_inc(rows_ready, 1)

            def finish(n, r):
                q = r % 4
                dve.wait_ge(exped, n + 1)
                nc.vector.tensor_reduce(share[q][:], less[q][:], AXX, ALU.add).then_inc(summed, 1)
                dve.wait_ge(summed, n + 1)
                nc.vector.reciprocal(share[q][:], share[q][:]).then_inc(inverted, 1)

            def step(n, r):
                b, q = r % 2, r % 4
                sums = bank[2 + b][0:T, :].rearrange("p (h g) -> p h g", g=SL)
                dve.wait_ge(logits, n + 1)
                nc.vector.tensor_reduce(peak[b][:], sums, AXX, ALU.max).then_inc(maxed, 1)
                if exists(n + 4):
                    normalise(n + 4, (r + 4) % RING)
                wait_from(dve, weighed, n - 3)
                dve.wait_ge(maxed, n + 1)
                nc.vector.tensor_tensor(less[q][:], sums, wide(peak[b]), ALU.subtract).then_inc(lessened, 1)
                if exists(n - 1):
                    finish(n - 1, r - 1)

            for n in range(4):
                normalise(n, n)
            all_tiles(dve, step)
            finish(TILES - 1, TILES - 1)

        @block.gpsimd
        def _(pool):
            def step(n, r):
                q = r % 4
                pool.wait_ge(inverted, n + 1)
                wait_from(pool, w_turned, n - 3)
                nc.gpsimd.tensor_tensor(weight[q][:], less[q][:], wide(share[q]), ALU.mult).then_inc(weighed, 1)
            all_tiles(pool, step)

        @block.scalar
        def _(act):
            def keep_rows(n, r):
                act.wait_ge(turned, n + 1)
                nc.scalar.activation(norm_t[r % 4][:], bank[r % 2][:, 0:T], ACT.Copy).then_inc(kept, 1)

            def keep_weights(n, r, stores):
                b = r % 2
                act.wait_ge(w_turned, n + 1)
                wait_from(act, w_stored[b], stores * 16)
                nc.scalar.activation(weight_t[b][:].rearrange("p k t -> p (k t)"), bank[4 + b][:, 0:KC * T],
                                     ACT.Copy).then_inc(w_kept, 1)

            def step_of(turn):
                def step(n, r):
                    q = r % 4
                    act.wait_ge(lessened, n + 1)
                    nc.scalar.activation(less[q][:], less[q][:], ACT.Exp).then_inc(exped, 1)
                    if exists(n + 3):
                        keep_rows(n + 3, r + 3)
                    if exists(n - 3):
                        keep_weights(n - 3, r - 3, turn * (RING // 2) + (r - 3) // 2)
                return step

            for n in range(3):
                keep_rows(n, n)
            for n in range(RING):
                step_of(0)(n, n)
            with act.Fori(1, TILES // RING - 1) as i:
                for r in range(RING):
                    step_of(i)(i * RING + r, r)
            for r in range(RING):
                step_of(TILES // RING - 1)(TILES - RING + r, r)
            for n in range(TILES - 3, TILES):
                keep_weights(n, n, n // 2)

        @block.sync
        def _(sp):
            with sp.Fori(0, TILES // 2) as i:
                for b in range(2):
                    sp.wait_ge(w_kept, i * 2 + (b + 1))
                    sp.dma_start(scratch[bass.ds(i * 2 + b, 1)].rearrange("a p c -> p (a c)"),
                                 weight_t[b][:].rearrange("p k t -> p (k t)")).then_inc(w_stored[b], 16)
            for b in range(2):
                sp.wait_ge(w_stored[b], 16 * (TILES // 2))

        @block.tensor
        def _(pe):
            zeros = m["zero_row"][0:1].rearrange("a q d -> a (q d)")
            for h in range(2):
                nc.tensor.matmul(bank[6 + h][:, 0:2 * DE], m["ones_row"][0:1, :], zeros, start=True, stop=False,
                                 skip_group_check=True)

            def turn_rows(n, r):
                pe.wait_ge(rows_ready, n + 1)
                wait_from(pe, kept, n - 1)
                nc.tensor.transpose(bank[r % 2][:, 0:T], rows[r % RING][:, 0:D], m["ident"][0:T, 0:T]).then_inc(turned, 1)

            def make_logits(n, r):
                b = r % 2
                wait_from(pe, lessened, n - 1)
                for half in range(2):
                    nc.tensor.matmul(bank[2 + b][0:T, :], m["ones_r"][0:1, 0:T], m["b_logit"][0:1, half, :],
                                     start=(half == 0), stop=False)
                pe.wait_ge(kept, n + 1)
                nc.tensor.matmul(bank[2 + b][0:T, :], norm_t[r % 4][:], m["w_logit"][:], start=False, stop=True
                                 ).then_inc(logits, 1)

            def apply(n, r):
                b = r % 2
                pe.wait_ge(weighed, n + 1)
                flat = weight[r % 4][:].rearrange("p h g -> p (h g)")
                for k in range(KC):
                    nc.tensor.matmul(bank[6 + k // 2][:, k % 2 * DE:(k % 2 + 1) * DE], flat[:, k * 128:(k + 1) * 128],
                                     rows[r % RING][:], start=False, stop=False, skip_group_check=True)
                wait_from(pe, w_kept, n - 1)
                for k in range(KC):
                    t = nc.tensor.transpose(bank[4 + b][:, k * T:(k + 1) * T], flat[:, k * 128:(k + 1) * 128],
                                            m["ident"][0:T, 0:T])
                t.then_inc(w_turned, 1)

            def step(n, r):
                make_logits(n, r)
                if exists(n + 3):
                    turn_rows(n + 3, r + 3)
                if exists(n - 3):
                    apply(n - 3, r - 3)

            for n in range(3):
                turn_rows(n, n)
            all_tiles(pe, step)
            for n in range(TILES - 3, TILES):
                apply(n, n)
            for h in range(2):
                nc.tensor.matmul(bank[6 + h][:, 0:2 * DE], m["ones_row"][0:1, :], zeros, start=False, stop=True,
                                 skip_group_check=True)


def mixer(nc, m, hy_conv_w, hy_conv_b, hy_dt_bias, hy_A_log, hy_D, hy_norm_w):
    with ExitStack() as c:
        sem = lambda n: c.enter_context(nc.semaphore(n + "_x"))
        sb = lambda n, s: c.enter_context(nc.sbuf_tensor(n + "_x", s, F32))
        loaded, pe_done, dve_done, act_done, step, dt_step = (
            sem("loaded"), sem("pe_done"), sem("dve_done"), sem("act_done"), sem("step"), sem("dt_step"))
        S = SL
        cw_x, cw_bc, cb_x, cb_bc = sb("cw_x", [128, KC, 3]), sb("cw_bc", [S, 2, 3]), sb("cb_x", [128, KC]), sb("cb_bc", [S, 2])
        dt_row, a_row, d_row, nw = sb("dt_row", [1, 16]), sb("a_row", [1, 16]), sb("d_row", [1, HEADS]), sb("nw", [128, KC])
        sums, sums_t, n_row, n_col = sb("sums", [128, KC, DE]), sb("sums_t", [D, HS]), sb("n_row", [1, HS]), sb("n_col", [S, HEADS])
        slices, slices_t = sb("slices", [S, HEADS, HP]), sb("slices_t", [128, KC, S])
        z_t, x_pad, bc_pad = sb("z_t", [128, KC, S]), sb("x_pad", [128, KC, S + 2]), sb("bc_pad", [S, 2, S + 2])
        x_t, bc_t, gate_x, gate_bc, gate_z = (
            sb("x_t", [128, KC, S]), sb("bc_t", [S, 2, S]), sb("gate_x", [128, KC, S]), sb("gate_bc", [S, 2, S]), sb("gate_z", [128, KC, S]))
        x_nat, z_nat = sb("x_nat", [S, HEADS, HP]), sb("z_nat", [S, HEADS, HP])
        raw_dt, dt, e_dt, l_dt, mask, w1, rate, over = (
            sb(n, [S, 16]) for n in ("raw_dt", "dt", "e_dt", "l_dt", "mask", "w1", "rate", "over"))
        dA, dA_t = sb("dA", [S, 16]), sb("dA_t", [16, S])
        decay = sb("decay", [S, 2, HEADS, S])
        cb, mf, mb = sb("cb", [S, S]), sb("mf", [S, HEADS, S + 1]), sb("mb", [S, HEADS, S + 1])
        xf, xb = sb("xf", [S, HEADS, HP]), sb("xb", [S, HEADS, HP])
        fc, y, y2 = sb("fc", [S, HEADS]), sb("y", [S, HEADS, HP]), sb("y2", [S, HEADS, HP])
        ms, root, inv, spare = sb("ms", [S, 1]), sb("root", [S, 1]), sb("inv", [S, 1]), sb("spare", [S, 1])
        y_t, mixed = sb("y_t", [128, KC, S]), sb("mixed", [HP, HEADS, S])
        bank = m["bank"]
        ident, ones_row = m["ident"], m["ones_row"]
        row = lambda v: v.rearrange("(a d) -> a d", a=1)
        block = c.enter_context(nc.Block())

        @block.sync
        def _(sp):
            slow = dict(allow_slow_non_contiguous=True)
            sp.dma_start(cw_x[:], hy_conv_w[0:HID].rearrange("(k p) t -> p k t", p=128), **slow).then_inc(loaded, 16)
            sp.dma_start(cw_bc[:], hy_conv_w[HID:HID + 2 * S].rearrange("(k p) t -> p k t", p=S), **slow).then_inc(loaded, 16)
            sp.dma_start(cb_x[:], hy_conv_b[0:HID].rearrange("(k p) -> p k", p=128), **slow).then_inc(loaded, 16)
            sp.dma_start(cb_bc[:], hy_conv_b[HID:HID + 2 * S].rearrange("(k p) -> p k", p=S), **slow).then_inc(loaded, 16)
            sp.dma_start(nw[:], hy_norm_w.rearrange("(k p) -> p k", p=128), **slow).then_inc(loaded, 16)
            for h in range(2):
                sp.dma_start(dt_row[0:1, h * 8:h * 8 + 8], row(hy_dt_bias)).then_inc(loaded, 16)
                sp.dma_start(a_row[0:1, h * 8:h * 8 + 8], row(hy_A_log)).then_inc(loaded, 16)
            sp.dma_start(d_row[:], row(hy_D)).then_inc(loaded, 16)

        @block.tensor
        def _(pe):
            mm, turn = nc.tensor.matmul, nc.tensor.transpose
            loose = dict(skip_group_check=True)
            pe.wait_ge(dve_done, 1)
            for k in range(KC):
                i = turn(bank[0][:, k * 128:(k + 1) * 128], sums[:, k, 0:D], ident[:])
            for k in range(KC):
                i = mm(bank[1][0:1, k * 128:(k + 1) * 128], sums[:, k, D:DE], ident[:], start=(k == 0), stop=True, **loose)
            i.then_inc(pe_done, 1)
            pe.wait_ge(dve_done, 2)
            for h in range(HEADS):
                i = mm(bank[2][0:S, h:h + 1], n_row[0:1, h * S:(h + 1) * S], ones_row[0:1, 0:1], start=(h == 0), stop=True, **loose)
            for h in range(HEADS):
                mm(bank[3][0:S, h * HP:(h + 1) * HP], sums_t[:, h * S:(h + 1) * S], m["w_fx"][:, h * HP:(h + 1) * HP],
                   start=(h == 0), stop=False, **loose)
                i = mm(bank[3][0:S, h * HP:(h + 1) * HP], n_row[0:1, h * S:(h + 1) * S], m["b_fx"][0:1, h * HP:(h + 1) * HP],
                       start=False, stop=True, **loose)
            i.then_inc(pe_done, 1)
            pe.wait_ge(dve_done, 3)
            for k in range(KC):
                i = turn(bank[4][:, k * S:(k + 1) * S], slices[:].rearrange("p h c -> p (h c)")[:, k * 128:(k + 1) * 128], ident[0:S, 0:S])
            i.then_inc(pe_done, 1)
            pe.wait_ge(dve_done, 4)
            pe.wait_ge(loaded, 16 * 10)
            for r in range(2 * KC):
                for k in range(KC):
                    mm(bank[5][:, r * S:(r + 1) * S], m["w_in"][:, k, r * 128:(r + 1) * 128], slices_t[:, k, :],
                       start=(r == 0 and k == 0), stop=(k == KC - 1), **loose)
            for r in range(2):
                for k in range(KC):
                    mm(bank[6][0:S, r * S:(r + 1) * S], m["w_in"][:, k, 1024 + r * S:1024 + (r + 1) * S], slices_t[:, k, :],
                       start=(r == 0 and k == 0), stop=(k == KC - 1), **loose)
            for k in range(KC):
                mm(bank[6][0:S, 128:144], slices_t[:, k, :], m["w_in"][:, k, 1152:1168], start=False, stop=False, **loose)
            mm(bank[6][0:S, 128:144], ones_row[0:1, 0:S], dt_row[:], start=False, stop=True, **loose)
            i = mm(bank[6][0:S, 144:160], ones_row[0:1, 0:S], a_row[:], start=False, stop=True, **loose)
            i.then_inc(pe_done, 1)
            pe.wait_ge(dve_done, 6)
            for k in range(KC):
                turn(bank[0][0:S, k * 128:(k + 1) * 128], x_t[:, k, :], ident[:])
            for k in range(KC):
                turn(bank[1][0:S, k * 128:(k + 1) * 128], z_t[:, k, :], ident[:])
            mm(bank[2][0:S, 0:S], bc_t[:, 0, :], bc_t[:, 1, :], start=True, stop=True)
            for k in range(KC):
                mm(bank[2][0:S, 128:128 + HEADS], x_t[:, k, :], m["fcd"][:, k, :], start=False, stop=False, **loose)
            mm(bank[2][0:S, 128:128 + HEADS], ones_row[0:1, 0:S], d_row[:], start=False, stop=True, **loose)
            pe.wait_ge(act_done, 5)
            i = turn(bank[7][0:16, 0:S], dA[:], ident[0:S, 0:S])
            i.then_inc(pe_done, 1)
            pe.wait_ge(dve_done, 7)
            for d in range(2):
                for h in range(HEADS):
                    j = d * HEADS + h
                    i = mm(bank[3 + d][0:S, h * S:(h + 1) * S], ident[0:16, j:j + 1].to_broadcast([16, S]), dA_t[:],
                           start=(h == 0), stop=True, **loose)
            i.then_inc(pe_done, 1)
            pe.wait_ge(dve_done, 8)
            for h in range(HEADS):
                mm(bank[5][0:S, h * HP:(h + 1) * HP], mf[:, h, 0:S], xf[:, h, :], start=(h == 0), stop=False, **loose)
                i = mm(bank[5][0:S, h * HP:(h + 1) * HP], mb[:, h, 1:S + 1], xb[:, h, :], start=False, stop=True, **loose)
            i.then_inc(pe_done, 1)
            pe.wait_ge(dve_done, 10)
            for k in range(KC):
                i = turn(bank[0][:, k * S:(k + 1) * S], y2[:].rearrange("p h c -> p (h c)")[:, k * 128:(k + 1) * 128], ident[0:S, 0:S])
            i.then_inc(pe_done, 1)
            pe.wait_ge(dve_done, 11)
            for h in range(HEADS):
                for k in range(KC):
                    i = mm(bank[1][0:HP, h * S:(h + 1) * S], m["w_mix"][:, k, h * HP:(h + 1) * HP], y_t[:, k, :],
                           start=(h == 0 and k == 0), stop=(k == KC - 1), **loose)
            i.then_inc(pe_done, 1)
            pe.wait_ge(dve_done, 12)
            for h in range(HEADS):
                p = h % 2 * S
                i = mm(bank[3][p:p + S, h // 2 * D:(h // 2 + 1) * D], mixed[:, h, :], m["w_out"][:, h, :],
                       start=(h < 2), stop=True, **loose)
            i.then_inc(pe_done, 1)

        @block.scalar
        def _(act):
            act.wait_ge(dve_done, 5)
            nc.scalar.activation(gate_x[:], x_t[:], ACT.Exp, scale=-1.0)
            nc.scalar.activation(gate_bc[:], bc_t[:], ACT.Exp, scale=-1.0)
            nc.scalar.activation(gate_z[:], z_t[:], ACT.Exp, scale=-1.0).then_inc(act_done, 1)
            nc.scalar.activation(e_dt[:], w1[:], ACT.Exp, scale=-1.0).then_inc(act_done, 1)
            nc.scalar.activation(rate[:], rate[:], ACT.Exp, scale=0.5).then_inc(act_done, 1)
            act.wait_ge(dt_step, 1)
            nc.scalar.activation(l_dt[:], w1[:], ACT.Ln).then_inc(act_done, 1)
            act.wait_ge(dt_step, 2)
            nc.scalar.activation(dA[:], mask[:], ACT.Exp, scale=-1.0).then_inc(act_done, 1)
            act.wait_ge(dve_done, 9)
            nc.scalar.activation(root[:], ms[:], ACT.Sqrt).then_inc(act_done, 1)

        @block.vector
        def _(dve):
            v = nc.vector
            link = chain(dve, step)
            wide = lambda t: t.rearrange("p (h a) -> p h a", a=1).to_broadcast([S, HEADS, HP])
            v.tensor_copy(sums[:, 0:2, :], bank[6][:, 0:2 * DE].rearrange("p (q d) -> p q d", d=DE))
            v.tensor_copy(sums[:, 2:4, :], bank[7][:, 0:2 * DE].rearrange("p (q d) -> p q d", d=DE)).then_inc(dve_done, 1)
            dve.wait_ge(pe_done, 1)
            v.tensor_copy(sums_t[:], bank[0][:, :])
            v.tensor_copy(n_row[:], bank[1][0:1, :]).then_inc(dve_done, 1)
            dve.wait_ge(pe_done, 2)
            link(v.tensor_scalar(n_col[:], bank[2][0:S, 0:HEADS], 1e-5, None, ALU.add))
            link(v.reciprocal(n_col[:], n_col[:]))
            v.tensor_tensor(slices[:], bank[3][0:S, :].rearrange("p (h c) -> p h c", c=HP), wide(n_col[:]), ALU.mult).then_inc(dve_done, 1)
            dve.wait_ge(pe_done, 3)
            v.tensor_copy(slices_t[:], bank[4][:, 0:KC * S].rearrange("p (k s) -> p k s", s=S)).then_inc(dve_done, 1)
            v.memset(x_pad[:, :, 0:2], 0.0)
            v.memset(bc_pad[:, :, 0:2], 0.0)
            v.memset(mf[:, :, 0:1], 0.0)
            v.memset(mb[:, :, S:S + 1], 0.0)
            dve.wait_ge(pe_done, 4)
            dve.wait_ge(loaded, 16 * 10)
            v.tensor_copy(z_t[:], bank[5][:, 0:KC * S].rearrange("p (k s) -> p k s", s=S))
            v.tensor_copy(x_pad[:, :, 2:S + 2], bank[5][:, KC * S:2 * KC * S].rearrange("p (k s) -> p k s", s=S))
            v.tensor_copy(bc_pad[:, :, 2:S + 2], bank[6][0:S, 0:2 * S].rearrange("p (k s) -> p k s", s=S))
            link(v.tensor_copy(raw_dt[:], bank[6][0:S, 128:144]))
            v.tensor_scalar(over[:], bank[6][0:S, 144:160], 88.7228, 1e30, ALU.is_gt, ALU.mult)
            v.tensor_scalar(rate[:], bank[6][0:S, 144:160], 88.7228, None, ALU.min)
            link(v.scalar_tensor_tensor(w1[:], raw_dt[:], -1.0, raw_dt[:], ALU.mult, ALU.max))
            for pad, out, taps, bias, n in ((x_pad, x_t, cw_x, cb_x, KC), (bc_pad, bc_t, cw_bc, cb_bc, 2)):
                for k in range(n):
                    i = v.tensor_scalar(out[:, k, :], pad[:, k, 0:S], taps[:, k, 0:1], bias[:, k:k + 1], ALU.mult, ALU.add)
                link(i)
                for tap in (1, 2):
                    for k in range(n):
                        i = v.scalar_tensor_tensor(out[:, k, :], pad[:, k, tap:S + tap], taps[:, k, tap:tap + 1], out[:, k, :],
                                                   ALU.mult, ALU.add)
                    link(i)
            dve.sem_inc(dve_done, 1)
            dve.wait_ge(act_done, 1)
            for g in (gate_x, gate_bc, gate_z):
                i = v.tensor_scalar(g[:], g[:], 1.0, None, ALU.add)
            link(i)
            for g in (gate_x, gate_bc, gate_z):
                i = v.reciprocal(g[:], g[:])
            link(i)
            v.tensor_tensor(x_t[:], x_t[:], gate_x[:], ALU.mult)
            v.tensor_tensor(bc_t[:], bc_t[:], gate_bc[:], ALU.mult)
            v.tensor_tensor(z_t[:], z_t[:], gate_z[:], ALU.mult).then_inc(dve_done, 1)
            dve.wait_ge(act_done, 3)
            v.tensor_scalar(w1[:], e_dt[:], 1.0, None, ALU.add).then_inc(dt_step, 1)
            dve.wait_ge(dt_step, 1)
            link(v.tensor_scalar(mask[:], w1[:], 1.0, None, ALU.is_equal))
            link(v.tensor_tensor(mask[:], mask[:], e_dt[:], ALU.mult))
            link(v.tensor_scalar(dt[:], w1[:], -1.0, 1e-30, ALU.add, ALU.max))
            link(v.reciprocal(dt[:], dt[:]))
            link(v.tensor_tensor(dt[:], dt[:], e_dt[:], ALU.mult))
            dve.wait_ge(act_done, 4)
            link(v.tensor_tensor(dt[:], dt[:], l_dt[:], ALU.mult))
            link(v.tensor_tensor(dt[:], dt[:], mask[:], ALU.add))
            link(v.scalar_tensor_tensor(dt[:], raw_dt[:], 0.0, dt[:], ALU.max, ALU.add))
            link(v.tensor_tensor(mask[:], dt[:], rate[:], ALU.mult))
            link(v.scalar_tensor_tensor(mask[:], mask[:], 1e18, rate[:], ALU.min, ALU.mult))
            v.tensor_tensor(mask[:], mask[:], over[:], ALU.add).then_inc(dt_step, 1)
            dve.wait_ge(pe_done, 5)
            v.tensor_copy(x_nat[:], bank[0][0:S, :].rearrange("p (h c) -> p h c", c=HP))
            v.tensor_copy(z_nat[:], bank[1][0:S, :].rearrange("p (h c) -> p h c", c=HP))
            v.tensor_copy(cb[:], bank[2][0:S, 0:S])
            v.tensor_copy(fc[:], bank[2][0:S, 128:128 + HEADS])
            link(v.tensor_copy(dA_t[:], bank[7][0:16, 0:S]))
            dve.sem_inc(dve_done, 1)
            v.tensor_tensor(xf[:], x_nat[:], wide(dt[:, 0:HEADS]), ALU.mult)
            v.tensor_tensor(xb[:], x_nat[:], wide(dt[:, HEADS:]), ALU.mult)
            v.tensor_tensor(y[:], x_nat[:], wide(fc[:]), ALU.mult)
            dve.wait_ge(pe_done, 6)
            for h in range(HEADS):
                v.tensor_tensor_scan(decay[:, 0, h, :], bank[3][0:S, h * S:(h + 1) * S], ident[0:S, 0:S], 0.0, ALU.mult, ALU.add)
                i = v.tensor_tensor_scan(decay[:, 1, h, :][:, ::-1], bank[4][0:S, h * S:(h + 1) * S][:, ::-1],
                                         ident[0:S, 0:S][:, ::-1], 0.0, ALU.mult, ALU.add)
            link(i)
            cb_all = cb[:].rearrange("p (a t) -> p a t", a=1).to_broadcast([S, HEADS, S])
            v.tensor_tensor(mf[:, :, 1:S + 1], decay[:, 0], cb_all, ALU.mult)
            v.tensor_tensor(mb[:, :, 0:S], decay[:, 1], cb_all, ALU.mult).then_inc(dve_done, 1)
            dve.wait_ge(pe_done, 7)
            link(v.tensor_tensor(y[:], bank[5][0:S, :].rearrange("p (h c) -> p h c", c=HP), y[:], ALU.add))
            link(v.tensor_tensor(y[:], y[:], z_nat[:], ALU.mult))
            link(v.tensor_tensor(y2[:], y[:], y[:], ALU.mult))
            link(v.tensor_reduce(ms[:], y2[:].rearrange("p h c -> p (h c)"), AXX, ALU.add))
            link(v.tensor_scalar(ms[:], ms[:], 1.0 / HID, EPS, ALU.mult, ALU.add))
            dve.sem_inc(dve_done, 1)
            dve.wait_ge(act_done, 6)
            inverse_root(nc, link, inv[:], root[:], ms[:], spare[:])
            v.tensor_scalar(y2[:], y[:], inv[:], None, ALU.mult).then_inc(dve_done, 1)
            dve.wait_ge(pe_done, 8)
            v.tensor_tensor(y_t[:], bank[0][:, 0:KC * S].rearrange("p (k s) -> p k s", s=S),
                            nw[:].rearrange("p (k a) -> p k a", a=1).to_broadcast([128, KC, S]), ALU.mult).then_inc(dve_done, 1)
            dve.wait_ge(pe_done, 9)
            v.tensor_copy(mixed[:], bank[1][0:HP, :].rearrange("p (h s) -> p h s", s=S)).then_inc(dve_done, 1)
            dve.wait_ge(pe_done, 10)
            v.tensor_copy(m["proj"][:].rearrange("p k d -> p (k d)"), bank[3][:, :])


AHEAD_LOADS = 4


def gather_out(nc, m, scratch, out_b, out):
    with ExitStack() as c:
        sem = lambda n: c.enter_context(nc.semaphore(n + "_o"))
        sb = lambda n, s: c.enter_context(nc.sbuf_tensor(n + "_o", s, F32))
        w_loaded = [sem(f"w_loaded{k}") for k in range(AHEAD_LOADS)]
        row_loaded, products, added, stored = sem("row_loaded"), sem("products"), sem("added"), sem("stored")
        weight = [sb(f"weight{k}", [128, GROUP, KC * T]) for k in range(AHEAD_LOADS)]
        b_row, bias = sb("b_row", [1, GROUP, D]), sb("bias", [T, GROUP, D])
        bias_spread, bias_kept, biased = sem("bias_spread"), sem("bias_kept"), sem("biased")
        bank = m["bank"]
        out_view = out.rearrange("(t p) d -> p t d", p=T)
        block = c.enter_context(nc.Block())

        @block.sync
        def _(sp):
            for q in range(GROUP):
                sp.dma_start(b_row[0:1, q, :], out_b.rearrange("(a d) -> a d", a=1)).then_inc(row_loaded, 16)

            def load(g, k):
                sp.dma_start(weight[k][:], scratch[bass.ds(g * GROUP, GROUP)].rearrange("t p c -> p t c")).then_inc(w_loaded[k], 16)

            for k in range(AHEAD_LOADS):
                load(k, k)
            with sp.Fori(0, GROUPS // AHEAD_LOADS - 1) as i:
                for k in range(AHEAD_LOADS):
                    sp.wait_ge(products, i * AHEAD_LOADS + (k + 1))
                    load(i * AHEAD_LOADS + (AHEAD_LOADS + k), k)

        @block.tensor
        def _(pe):
            pe.wait_ge(row_loaded, 16 * GROUP)
            nc.tensor.matmul(bank[2][0:T, 0:GD], m["ones_row"][0:1, 0:T], b_row[0:1].rearrange("a q d -> a (q d)"),
                             start=True, stop=True).then_inc(bias_spread, 1)

            def work(g, i, k, free):
                pe.wait_ge(w_loaded[k], (i + 1) * 16)
                if free is not None:
                    pe.wait_ge(added, free)
                for q in range(GROUP):
                    for r in range(KC):
                        t = nc.tensor.matmul(bank[k % 2][0:T, q * D:(q + 1) * D], weight[k][:, q, r * T:(r + 1) * T],
                                             m["proj"][:, r, :], start=(q == 0 and r == 0), stop=(r == KC - 1),
                                             skip_group_check=True)
                t.then_inc(products, 1)
            for k in range(AHEAD_LOADS):
                work(k, 0, k, k - 1 if k >= 2 else None)
            with pe.Fori(1, GROUPS // AHEAD_LOADS) as i:
                for k in range(AHEAD_LOADS):
                    work(i * AHEAD_LOADS + k, i, k, i * AHEAD_LOADS + (k - 1))

        @block.gpsimd
        def _(pool):
            pool.wait_ge(bias_kept, 1)
            with pool.Fori(0, GROUPS) as g:
                here = m["stream"][:, bass.ds(g * GROUP, GROUP), :]
                nc.gpsimd.tensor_tensor(here, here, bias[:], ALU.add).then_inc(biased, 1)

        @block.vector
        def _(dve):
            dve.wait_ge(bias_spread, 1)
            nc.vector.tensor_copy(bias[:].rearrange("p q d -> p (q d)"), bank[2][0:T, 0:GD]).then_inc(bias_kept, 1)
            with dve.Fori(0, GROUPS // 2) as i:
                for k in range(2):
                    g = i * 2 + k
                    dve.wait_ge(products, g + 1)
                    dve.wait_ge(biased, g + 1)
                    here = m["stream"][:, bass.ds(g * GROUP, GROUP), :]
                    nc.vector.tensor_tensor(here, bank[k][0:T, 0:GD].rearrange("p (q d) -> p q d", d=D), here, ALU.add
                                            ).then_inc(added, 1)

        @block.scalar
        def _(act):
            with act.Fori(0, GROUPS) as g:
                act.wait_ge(added, g + 1)
                act.dma_start(out_view[:, bass.ds(g * GROUP, GROUP), :], m["stream"][:, bass.ds(g * GROUP, GROUP), :]
                              ).then_inc(stored, 16)
            act.wait_ge(stored, 16 * GROUPS)


NAMES = ['x', 'adj', 'L0_gnn_item_feat', 'L0_gnn_W_item', 'L0_gnn_b_item', 'L0_gnn_W_user', 'L0_gnn_b_user',
         'L0_ffn_W_ih', 'L0_ffn_W_hh', 'L0_ffn_b_ih', 'L0_ffn_b_hh', 'L0_ffn_W_lin', 'L0_ffn_b_lin', 'L0_ffn_fw_att',
         'L0_ffn_bw_att', 'L1_gnn_W', 'L1_ffn_W_fx', 'L1_ffn_b_fx', 'L1_ffn_W_x', 'L1_ffn_b_x', 'L1_ffn_W_slice',
         'L1_ffn_b_slice', 'L1_ffn_temperature', 'L1_ffn_hy_in_w', 'L1_ffn_hy_conv_w', 'L1_ffn_hy_conv_b',
         'L1_ffn_hy_dt_bias', 'L1_ffn_hy_A_log', 'L1_ffn_hy_D', 'L1_ffn_hy_fcD_w', 'L1_ffn_hy_norm_w',
         'L1_ffn_hy_out_w', 'L1_ffn_out_w', 'L1_ffn_out_b']


def build(nc, a, scratch, out):
    with ExitStack() as c:
        m = common(nc, c)

        def place_operands(stack, tag):
            for half in ("feats_high", "feats_low"):
                m[half] = stack.enter_context(nc.sbuf_tensor(half + tag, [T, TILES, D], F32R))
            m["panel"] = [stack.enter_context(nc.sbuf_tensor(f"panel{k}{tag}", [T, GROUP, PCOLS], F32)) for k in range(SLOTS)]
            m["panel_loaded"] = [stack.enter_context(nc.semaphore(f"panel_loaded{k}{tag}")) for k in range(SLOTS)]

        with ExitStack() as graph0:
            place_operands(graph0, "_a")
            setup(nc, m, a['L0_gnn_W_item'], a['L0_gnn_b_item'], a['L0_gnn_W_user'], a['L0_ffn_W_ih'],
                  a['L0_ffn_W_hh'], a['L0_ffn_b_ih'], a['L0_ffn_b_hh'], a['L1_gnn_W'], a['x'], a['L0_gnn_item_feat'],
                  a['adj'])
            norm_stats(nc, m, 0)
            adjacency_pass(nc, m, a['adj'], a['L0_gnn_b_user'], True)
        norm_stats(nc, m, 1)
        with ExitStack() as sequence:
            m["doubled_t"] = sequence.enter_context(nc.sbuf_tensor("doubled_t", [128, N + 1], F32))
            m["norm_t"] = sequence.enter_context(nc.sbuf_tensor("norm_t", [128, N], F32))
            norm_transposed(nc, m, "_2")
            lstm(nc, m)
            mix(nc, m, a['L0_ffn_W_lin'], a['L0_ffn_b_lin'], a['L0_ffn_fw_att'], a['L0_ffn_bw_att'])
        norm_stats(nc, m, 2)
        with ExitStack() as graph1:
            place_operands(graph1, "_b")
            graph_features(nc, m, a['adj'])
            adjacency_pass(nc, m, a['adj'], None, False)
        norm_stats(nc, m, 3)
        with ExitStack() as late:
            sb = lambda n, s: late.enter_context(nc.sbuf_tensor(n, s, F32))
            m["w_fx"], m["fcd"] = sb("w_fx", [D, HID]), sb("fcd", [128, KC, HEADS])
            m["w_mix"], m["w_out"] = sb("w_mix", [128, KC, HID]), sb("w_out", [HP, HEADS, D])
            m["w_logit"], m["b_fx"] = sb("w_logit", [D, HS]), sb("b_fx", [1, HID])
            m["b_logit"] = late.enter_context(nc.sbuf_tensor("b_logit", [1, 2, HS], F32R))
            m["ones_r"] = late.enter_context(nc.sbuf_tensor("ones_r", [1, 128], F32R))
            m["w_in"] = sb("w_in", [128, KC, 1168])
            m["proj"] = sb("proj", [128, KC, D])
            slice_weights(nc, m, a['L1_ffn_W_fx'], a['L1_ffn_b_fx'], a['L1_ffn_W_x'], a['L1_ffn_b_x'], a['L1_ffn_W_slice'],
                          a['L1_ffn_b_slice'], a['L1_ffn_temperature'], a['L1_ffn_hy_fcD_w'], a['L1_ffn_hy_in_w'],
                          a['L1_ffn_hy_out_w'], a['L1_ffn_out_w'])
            slice_tokens(nc, m, scratch)
            mixer(nc, m, a['L1_ffn_hy_conv_w'], a['L1_ffn_hy_conv_b'], a['L1_ffn_hy_dt_bias'], a['L1_ffn_hy_A_log'],
                  a['L1_ffn_hy_D'], a['L1_ffn_hy_norm_w'])
            gather_out(nc, m, scratch, a['L1_ffn_out_b'], out)


def kernel(**inputs):
    from concourse import bacc
    from concourse.bass_utils import run_bass_kernel_spmd

    nc = bacc.Bacc("TRN2", target_bir_lowering=False, num_devices=1)
    arrays, aps = {}, {}
    for name in NAMES:
        a = np.ascontiguousarray(inputs[name])
        arrays[f"in_{name}_dram"] = a
        aps[name] = nc.dram_tensor(f"in_{name}_dram", a.shape, mybir.dt.from_np(a.dtype), kind="ExternalInput").ap()
    scratch = nc.dram_tensor("slice_weights_dram", (TILES, 128, KC * T), F32, kind="Internal").ap()
    out = nc.dram_tensor("out_0_dram", (N, D), F32, kind="ExternalOutput").ap()
    build(nc, aps, scratch, out)
    r = run_bass_kernel_spmd(nc, [arrays], core_ids=[0])
    return r.results[0]["out_0_dram"]
```
